# Optimizing a Trainium2 kernel written in Bass

```python
import numpy as np
import jax
import jax.numpy as jnp

def _softmax(x, axis=-1):
    return jax.nn.softmax(x, axis=axis)

def _gelu(x):
    return jax.nn.gelu(x, approximate=True)

def _silu(x):
    return jax.nn.silu(x)

def _sigmoid(x):
    return jax.nn.sigmoid(x)

def _layernorm(x, axis=-1, eps=1e-05):
    m = jnp.mean(x, axis=axis, keepdims=True)
    v = jnp.var(x, axis=axis, keepdims=True)
    return (x - m) / jnp.sqrt(v + eps)

def _scatter_add(tgt, idx, src, axis=0):
    return tgt.at[idx].add(src)

def _segment_sum(src, seg, n):
    return jax.ops.segment_sum(src, seg, n)
kernel_name = 'mk_seq_postln_d1_jaxref_r8_cd8388'

def setup_inputs(seed: int=0):
    np.random.seed(seed)
    _w = jnp.asarray

    def _L0_attn_setup():
        import jax, jax.numpy as jnp
        import numpy as np
        B, S, H = (2, 256, 256)
        NH, NKV, HD = (16, 4, 128)
        GROUPS = NH // NKV
        ROPE_THETA = 10000.0

        def _rope_cos_sin(seq_len, head_dim, dtype):
            inv_freq = 1.0 / ROPE_THETA ** (jnp.arange(0, head_dim, 2, dtype=jnp.float32) / head_dim)
            pos = jnp.arange(seq_len, dtype=jnp.float32)
            freqs = pos[:, None] * inv_freq[None, :]
            emb = jnp.concatenate([freqs, freqs], axis=-1)
            return (jnp.cos(emb).astype(dtype), jnp.sin(emb).astype(dtype))

        def _rotate_half(x):
            d = x.shape[-1] // 2
            return jnp.concatenate([-x[..., d:], x[..., :d]], axis=-1)
        key = jax.random.key(seed)
        ks = jax.random.split(key, 5)
        s = 0.02
        return {'hidden_states': jax.random.normal(ks[0], (B, S, H), jnp.float32), 'Wq': jax.random.normal(ks[1], (NH * HD, H), jnp.float32) * s, 'Wk': jax.random.normal(ks[2], (NKV * HD, H), jnp.float32) * s, 'Wv': jax.random.normal(ks[3], (NKV * HD, H), jnp.float32) * s, 'Wo': jax.random.normal(ks[4], (H, NH * HD), jnp.float32) * s}
    _L0_attn_in = _L0_attn_setup()

    def _L0_ffn_setup():
        import jax, jax.numpy as jnp
        import numpy as np
        HIDDEN = 256
        FFN = 176
        N_EXPERTS = 64
        TOP_K = 6
        N_SHARED = 2
        SHARED_FFN = FFN * N_SHARED
        ROUTED_SCALING = 1.0
        EPS = 1e-20

        def _moe_forward(x, gate_w, w_gate_up, w_down, ws_gate_up, ws_down):
            T = x.shape[0]
            logits = jnp.einsum('th,eh->te', x.astype(jnp.float32), gate_w.astype(jnp.float32))
            scores = jax.nn.softmax(logits, axis=-1)
            topk_w, topk_ids = jax.lax.top_k(scores, TOP_K)
            topk_w = topk_w / (jnp.sum(topk_w, axis=-1, keepdims=True) + EPS)
            topk_w = topk_w * ROUTED_SCALING
            comb = jnp.zeros((T, N_EXPERTS), dtype=x.dtype)
            comb = comb.at[jnp.arange(T)[:, None], topk_ids].add(topk_w.astype(x.dtype))
            gu = jnp.einsum('th,efh->tef', x, w_gate_up)
            g, u = (gu[..., :FFN], gu[..., FFN:])
            act = jax.nn.silu(g) * u
            act = act * comb[:, :, None]
            routed = jnp.einsum('tef,ehf->th', act, w_down)
            sgu = jnp.einsum('th,fh->tf', x, ws_gate_up)
            sg, su = (sgu[..., :SHARED_FFN], sgu[..., SHARED_FFN:])
            shared = jnp.einsum('tf,hf->th', jax.nn.silu(sg) * su, ws_down)
            return routed + shared
        key = jax.random.key(seed)
        k0, k1, k2, k3, k4, k5 = jax.random.split(key, 6)
        hidden_states = jax.random.normal(k0, (1, 32, HIDDEN), dtype=jnp.float32)
        gate_w = jax.random.normal(k1, (N_EXPERTS, HIDDEN), dtype=jnp.float32) * 0.05
        w_gate_up = jax.random.normal(k2, (N_EXPERTS, 2 * FFN, HIDDEN), dtype=jnp.float32) * 0.02
        w_down = jax.random.normal(k3, (N_EXPERTS, HIDDEN, FFN), dtype=jnp.float32) * 0.02
        ws_gate_up = jax.random.normal(k4, (2 * SHARED_FFN, HIDDEN), dtype=jnp.float32) * 0.02
        ws_down = jax.random.normal(k5, (HIDDEN, SHARED_FFN), dtype=jnp.float32) * 0.02
        return {'hidden_states': hidden_states, 'gate_w': gate_w, 'w_gate_up': w_gate_up, 'w_down': w_down, 'ws_gate_up': ws_gate_up, 'ws_down': ws_down}
    _L0_ffn_in = _L0_ffn_setup()
    _d = {'L0_attn_hidden_states': _L0_attn_in['hidden_states'], 'L0_attn_Wq': _L0_attn_in['Wq'], 'L0_attn_Wk': _L0_attn_in['Wk'], 'L0_attn_Wv': _L0_attn_in['Wv'], 'L0_attn_Wo': _L0_attn_in['Wo'], 'L0_ffn_gate_w': _L0_ffn_in['gate_w'], 'L0_ffn_w_gate_up': _L0_ffn_in['w_gate_up'], 'L0_ffn_w_down': _L0_ffn_in['w_down'], 'L0_ffn_ws_gate_up': _L0_ffn_in['ws_gate_up'], 'L0_ffn_ws_down': _L0_ffn_in['ws_down']}
    _x0 = _d['L0_attn_hidden_states']
    _d['L0_attn_hidden_states'] = jax.random.normal(jax.random.fold_in(jax.random.key(seed), 1), (2, 1024, 256), dtype=_x0.dtype)
    del _x0
    return _d

def reference(L0_attn_hidden_states, L0_attn_Wq, L0_attn_Wk, L0_attn_Wv, L0_attn_Wo, L0_ffn_gate_w, L0_ffn_w_gate_up, L0_ffn_w_down, L0_ffn_ws_gate_up, L0_ffn_ws_down):

    def _L0_attn_ref(hidden_states, Wq, Wk, Wv, Wo):
        import jax, jax.numpy as jnp
        import numpy as np
        B, S, H = (2, 256, 256)
        NH, NKV, HD = (16, 4, 128)
        GROUPS = NH // NKV
        ROPE_THETA = 10000.0

        def _rope_cos_sin(seq_len, head_dim, dtype):
            inv_freq = 1.0 / ROPE_THETA ** (jnp.arange(0, head_dim, 2, dtype=jnp.float32) / head_dim)
            pos = jnp.arange(seq_len, dtype=jnp.float32)
            freqs = pos[:, None] * inv_freq[None, :]
            emb = jnp.concatenate([freqs, freqs], axis=-1)
            return (jnp.cos(emb).astype(dtype), jnp.sin(emb).astype(dtype))

        def _rotate_half(x):
            d = x.shape[-1] // 2
            return jnp.concatenate([-x[..., d:], x[..., :d]], axis=-1)
        b, s, _ = hidden_states.shape
        q = (hidden_states @ Wq.T).reshape(b, s, NH, HD)
        k = (hidden_states @ Wk.T).reshape(b, s, NKV, HD)
        v = (hidden_states @ Wv.T).reshape(b, s, NKV, HD)
        cos, sin = _rope_cos_sin(s, HD, q.dtype)
        cos, sin = (cos[None, :, None, :], sin[None, :, None, :])
        q = q * cos + _rotate_half(q) * sin
        k = k * cos + _rotate_half(k) * sin
        k = jnp.repeat(k, GROUPS, axis=2)
        v = jnp.repeat(v, GROUPS, axis=2)
        scale = 1.0 / jnp.sqrt(jnp.asarray(HD, q.dtype))
        scores = jnp.einsum('bqhd,bkhd->bhqk', q, k) * scale
        causal = jnp.tril(jnp.ones((s, s), dtype=bool))
        scores = jnp.where(causal[None, None], scores, jnp.finfo(scores.dtype).min)
        attn = jax.nn.softmax(scores, axis=-1)
        out = jnp.einsum('bhqk,bkhd->bqhd', attn, v).reshape(b, s, NH * HD)
        return out @ Wo.T

    def _L0_ffn_ref(hidden_states, gate_w, w_gate_up, w_down, ws_gate_up, ws_down):
        import jax, jax.numpy as jnp
        import numpy as np
        HIDDEN = 256
        FFN = 176
        N_EXPERTS = 64
        TOP_K = 6
        N_SHARED = 2
        SHARED_FFN = FFN * N_SHARED
        ROUTED_SCALING = 1.0
        EPS = 1e-20

        def _moe_forward(x, gate_w, w_gate_up, w_down, ws_gate_up, ws_down):
            T = x.shape[0]
            logits = jnp.einsum('th,eh->te', x.astype(jnp.float32), gate_w.astype(jnp.float32))
            scores = jax.nn.softmax(logits, axis=-1)
            topk_w, topk_ids = jax.lax.top_k(scores, TOP_K)
            topk_w = topk_w / (jnp.sum(topk_w, axis=-1, keepdims=True) + EPS)
            topk_w = topk_w * ROUTED_SCALING
            comb = jnp.zeros((T, N_EXPERTS), dtype=x.dtype)
            comb = comb.at[jnp.arange(T)[:, None], topk_ids].add(topk_w.astype(x.dtype))
            gu = jnp.einsum('th,efh->tef', x, w_gate_up)
            g, u = (gu[..., :FFN], gu[..., FFN:])
            act = jax.nn.silu(g) * u
            act = act * comb[:, :, None]
            routed = jnp.einsum('tef,ehf->th', act, w_down)
            sgu = jnp.einsum('th,fh->tf', x, ws_gate_up)
            sg, su = (sgu[..., :SHARED_FFN], sgu[..., SHARED_FFN:])
            shared = jnp.einsum('tf,hf->th', jax.nn.silu(sg) * su, ws_down)
            return routed + shared
        B, S, H = hidden_states.shape
        x = hidden_states.reshape(-1, H)
        out = _moe_forward(x, gate_w, w_gate_up, w_down, ws_gate_up, ws_down)
        return out.reshape(B, S, H)
    x = L0_attn_hidden_states
    x = _layernorm(x + _L0_attn_ref(x, L0_attn_Wq, L0_attn_Wk, L0_attn_Wv, L0_attn_Wo), axis=-1)
    x = _layernorm(x + _L0_ffn_ref(x, L0_ffn_gate_w, L0_ffn_w_gate_up, L0_ffn_w_down, L0_ffn_ws_gate_up, L0_ffn_ws_down), axis=-1)
    return x

_drawn_inputs = setup_inputs


def setup_inputs(seed=0):
    import zlib

    import numpy as np

    out = dict(_drawn_inputs(seed))
    spreads = {}
    factors = {'L0_attn_Wq': 8.0,
     'L0_attn_Wk': 8.0,
     'L0_ffn_gate_w': 8.0,
     'L0_ffn_w_gate_up': 8.0,
     'L0_ffn_w_down': 8.0,
     'L0_ffn_ws_gate_up': 2.842,
     'L0_ffn_ws_down': 2.845}
    for name, (base, spread) in spreads.items():
        noise = np.random.default_rng([zlib.crc32(name.encode()), seed]).standard_normal(out[name].shape)
        drawn = base * np.exp(spread * noise) if base else spread * noise
        out[name] = jnp.asarray(drawn.astype(out[name].dtype))
    for name, factor in factors.items():
        out[name] = (out[name] * factor).astype(out[name].dtype)
    return out
```

```python
from contextlib import ExitStack

import numpy as np
import concourse.bass as bass
from concourse import mybir

F32 = mybir.dt.float32
F32R = mybir.dt.float32r
BF16 = mybir.dt.bfloat16
I32 = mybir.dt.int32
U32 = mybir.dt.uint32
ALU = mybir.AluOpType
ACT = mybir.ActivationFunctionType
AX = mybir.AxisListType

P = 128
B, S, H = 2, 1024, 256
T = B * S
HK = H // P
NH, NKV, HD = 16, 4, 128
GROUP = NH // NKV
HALF = S // 2
TILES = T // P
BT = S // P
WCOLS = (GROUP + 2) * HD
EPS_LN = 1e-5

E, TOPK, FFN = 64, 6, 176
SHARED = 2
WAYS = TOPK + SHARED
TAIL = FFN - P
UP_AT = 64
GCOLS = 2 * P + UP_AT + TAIL
BLK = 256
SUB = BLK // P
SHARED_BLOCKS = SHARED * T // BLK
MAX_BLOCKS = SHARED_BLOCKS + T * TOPK // BLK + E - 1
ROWS = (MAX_BLOCKS + 1) * BLK
ROW = H + 2
SKIP = 1.0e6
EPS_TOPK = 1e-20
MASKED = -1.0e30

STEPS = 2 * GROUP * 4
PAIRS = STEPS // 2
POSITIONS = STEPS + 5
K_OF = {"K0": 0, "V0": 1, "Q0": 2, "Q1": 3, "Q2": 4, "Q3": 5, "K1": 6, "V1": 7, "Q4": 8, "Q5": 9,
        "Q6": 10, "O0": 11, "O1": 12, "Q7": 13, "O2": 14, "O3": 15}
USES = len(K_OF)
ROPES = {"K0": 0, "Q0": 1, "Q1": 2, "Q2": 3, "Q3": 4, "K1": 5, "Q4": 6, "Q5": 7, "Q6": 8, "Q7": 9}
FIRST_USES = ["K0", "V0", "Q0"]
USE_AT = {1: "Q1", 5: "Q2", 9: "Q3", 11: "K1", 12: "V1", 13: "Q4", 17: "Q5", 21: "Q6", 22: "O0",
          23: "O1", 25: "Q7"}
LAST_USES = ["O2", "O3"]


def half_of(n):
    return n // (STEPS // 2)


def head_of(n):
    return n // 4 % GROUP


def key_tiles(n):
    return 4 * half_of(n) + n % 4 + 1


def chunks(n):
    return [(a, min(a + 4, key_tiles(n))) for a in range(0, key_tiles(n), 4)]


CHUNKS = sum(len(chunks(n)) for n in range(STEPS))


def chunks_before(n):
    if n < 0:
        return chunks_before(STEPS + n) - CHUNKS
    return sum(len(chunks(m)) for m in range(n))


def now(it, per, n):
    return (it + 1) * per + n


def attention(nc, dram, resid, consts):
    with ExitStack() as ctx:
        def sb(name, shape, dt=F32):
            return ctx.enter_context(nc.sbuf_tensor(name, shape, dt))

        def sem(name):
            return ctx.enter_context(nc.semaphore(name))

        x_raw = sb("x_raw", [P, HK, HALF])
        x_hi, x_lo = sb("x_hi", [P, HK, S], F32R), sb("x_lo", [P, HK, S], F32R)
        w_raw = sb("w_raw", [P, HK, WCOLS])
        w_hi, w_lo = sb("w_hi", [P, HK, WCOLS], F32R), sb("w_lo", [P, HK, WCOLS], F32R)
        wo_raw = sb("wo_raw", [P, GROUP, H])
        wo_hi, wo_lo = sb("wo_hi", [P, GROUP, H], F32R), sb("wo_lo", [P, GROUP, H], F32R)
        cos, sin = sb("cos", [P, S]), sb("sin", [P, S])
        q_hi, q_lo = sb("q_hi", [P, 2, HALF], F32R), sb("q_lo", [P, 2, HALF], F32R)
        k_hi, k_lo = sb("k_hi", [P, S], F32R), sb("k_lo", [P, S], F32R)
        v_hi, v_lo = sb("v_hi", [P, BT, HD], F32R), sb("v_lo", [P, BT, HD], F32R)
        turn_cos, turn_sin = sb("turn_cos", [P, 2, HALF]), sb("turn_sin", [P, 2, HALF])
        turned = sb("turned", [P, 2, HALF])
        probs = sb("probs", [P, 4, S])
        pt_hi, pt_lo = sb("pt_hi", [P, 2, BT, 2 * P], F32R), sb("pt_lo", [P, 2, BT, 2 * P], F32R)
        o_hi, o_lo = sb("o_hi", [P, 2, GROUP, HALF], F32R), sb("o_lo", [P, 2, GROUP, HALF], F32R)
        neg_max, row_sum, row_inv = sb("neg_max", [P, 4]), sb("row_sum", [P, 4]), sb("row_inv", [P, 4])
        empty = sb("empty", [P, 7, ROW])
        ident_bf = sb("ident_bf", [P, P], BF16)
        causal = sb("causal", [P, P], BF16)
        ident = consts["ident"]

        scores_ps = [ctx.enter_context(nc.psum_tensor(f"scores{i}", [P, S], F32)) for i in range(2)]
        pt_ps = [ctx.enter_context(nc.psum_tensor(f"pt{i}", [P, 512], F32)) for i in range(2)]
        o_ps = ctx.enter_context(nc.psum_tensor("o_ps", [P, 512], F32))
        proj_ps = ctx.enter_context(nc.psum_tensor("proj_ps", [P, 512], F32))

        tables_in, resid_in = sem("tables_in"), sem("resid_in")
        x_in, w_in, wo_in, empty_out = sem("x_in"), sem("w_in"), sem("wo_in"), sem("empty_out")
        consts_made, const_step = sem("consts_made"), sem("const_step")
        x_hi_made, x_split = sem("x_hi_made"), sem("x_split")
        w_hi_made, w_split = sem("w_hi_made"), sem("w_split")
        wo_hi_made, wo_split = sem("wo_hi_made"), sem("wo_split")
        projected, proj_free = sem("projected"), sem("proj_free")
        turned_sum = sem("turned_sum")
        turned_hi, turned_split = sem("turned_hi"), sem("turned_split")
        v_hi_made = sem("v_hi_made")
        scored, max_made, exped = sem("scored"), sem("max_made"), sem("exped")
        inv_made, scaled = sem("inv_made"), sem("scaled")
        transposed, pt_hi_made, pt_split = sem("transposed"), sem("pt_hi_made"), sem("pt_split")
        o_summed, o_hi_made, o_split = sem("o_summed"), sem("o_hi_made"), sem("o_split")

        block = ctx.enter_context(nc.Block())

        def w_cols(name):
            head = {"K": GROUP, "V": GROUP + 1}.get(name[0], int(name[1]) % GROUP)
            return slice(head * HD, (head + 1) * HD)

        def half(name):
            return int(name[1]) // GROUP if name[0] == "Q" else int(name[1])

        def turned_into(name):
            if name[0] == "K":
                cols = slice(half(name) * HALF, (half(name) + 1) * HALF)
                return k_hi[:, cols], k_lo[:, cols]
            return q_hi[:, int(name[1]) % 2, :], q_lo[:, int(name[1]) % 2, :]

        @block.sync
        def _(sp):
            sp.dma_start(cos[:], dram["cos"]).then_inc(tables_in, 16)
            sp.dma_start(sin[:], dram["sin"]).then_inc(tables_in, 16)
            sp.dma_start(resid[:], dram["x"].rearrange("(i p) c -> p i c", p=P)).then_inc(resid_in, 16)
            sp.wait_ge(consts_made, 2)
            with sp.Fori(0, B) as b:
                for c in range(2):
                    sp.wait_ge(x_split, now(b, 2, c))
                    sp.dma_start(x_raw[:], dram["xT"][b, c]).then_inc(x_in, 16)
                with sp.Fori(0, NKV) as kv:
                    it = b * NKV + kv
                    sp.wait_ge(w_split, now(it, 1, 0))
                    sp.dma_start(w_raw[:], dram["w"][kv]).then_inc(w_in, 16)
                    sp.wait_ge(wo_split, now(it, 1, 0))
                    sp.dma_start(wo_raw[:], dram["wo"][kv]).then_inc(wo_in, 16)
                    for q in range(4):
                        sp.dma_start(dram["empty"][it * 4 + q], empty[:]).then_inc(empty_out, 16)
            sp.wait_ge(empty_out, 16 * 4 * B * NKV)
            sp.wait_ge(tables_in, 32)
            sp.wait_ge(resid_in, 16)

        @block.gpsimd
        def _(pool):
            pool.sem_inc(turned_sum, len(ROPES))
            pool.sem_inc(turned_split, len(ROPES))
            pool.sem_inc(wo_split, 1)
            pool.memset(ident[:], 0.0).then_inc(const_step, 1)
            pool.memset(causal[:], 0.0).then_inc(const_step, 1)
            pool.memset(empty[:], 0.0).then_inc(const_step, 1)
            pool.wait_ge(const_step, 3)
            pool.affine_select(ident[:], ident[:], [[-1, P]], ALU.not_equal, 1.0, base=0,
                               channel_multiplier=1).then_inc(const_step, 1)
            pool.affine_select(causal[:], causal[:], [[-1, P]], ALU.is_ge, MASKED, base=0,
                               channel_multiplier=1).then_inc(const_step, 1)
            pool.memset(empty[:, :, H:H + 1], SKIP).then_inc(const_step, 1)
            pool.wait_ge(const_step, 6)
            pool.tensor_copy(ident_bf[:], ident[:]).then_inc(consts_made, 2)
            with pool.Fori(0, B) as b:
                with pool.Fori(0, NKV) as kv:
                    it = b * NKV + kv

                    def rotate(name):
                        r = ROPES[name]
                        pool.wait_ge(proj_free, now(it, USES, K_OF[name] + 1))
                        pool.wait_ge(turned_split, now(it, len(ROPES), r - 1))
                        nc.gpsimd.tensor_tensor(turned[:, r % 2], turn_cos[:, r % 2], turn_sin[:, r % 2],
                                                ALU.add).then_inc(turned_sum, 1)
                        hi, lo = turned_into(name)
                        pool.wait_ge(turned_hi, now(it, len(ROPES), r + 1))
                        nc.gpsimd.tensor_tensor(lo, turned[:, r % 2], hi.bitcast(F32),
                                                ALU.subtract).then_inc(turned_split, 1)

                    rotate("K0")
                    rotate("Q0")
                    pool.wait_ge(wo_in, 16 * (it + 1))
                    pool.wait_ge(wo_hi_made, now(it, 1, 1))
                    nc.gpsimd.tensor_tensor(wo_lo[:], wo_raw[:], wo_hi[:].bitcast(F32),
                                            ALU.subtract).then_inc(wo_split, 1)
                    for n in sorted(USE_AT):
                        if USE_AT[n] in ROPES:
                            rotate(USE_AT[n])

        @block.scalar
        def _(act):
            act.sem_inc(exped, STEPS)
            act.sem_inc(w_hi_made, 1)
            act.sem_inc(wo_hi_made, 1)
            act.sem_inc(turned_hi, len(ROPES))
            act.sem_inc(v_hi_made, 2)
            act.sem_inc(pt_hi_made, CHUNKS)
            act.sem_inc(o_hi_made, PAIRS)
            act.sem_inc(x_hi_made, 2)
            with act.Fori(0, B) as b:
                for c in range(2):
                    act.wait_ge(x_in, 32 * b + 16 * (c + 1))
                    act.wait_ge(projected, now(b * NKV, USES, -2))
                    nc.scalar.activation(x_hi[:, :, c * HALF:(c + 1) * HALF], x_raw[:],
                                         ACT.Copy).then_inc(x_hi_made, 1)
                with act.Fori(0, NKV) as kv:
                    it = b * NKV + kv

                    def rotated_hi(name):
                        r = ROPES[name]
                        act.wait_ge(turned_sum, now(it, len(ROPES), r + 1))
                        nc.scalar.activation(turned_into(name)[0], turned[:, r % 2],
                                             ACT.Copy).then_inc(turned_hi, 1)

                    def value_hi(name):
                        c = half(name)
                        act.wait_ge(projected, now(it, USES, K_OF[name] + 1))
                        nc.scalar.activation(v_hi[:, 4 * c:4 * c + 4, :], proj_ps[:],
                                             ACT.Copy).then_inc(v_hi_made, 1)

                    act.wait_ge(w_in, 16 * (it + 1))
                    act.wait_ge(projected, now(it, USES, -2))
                    nc.scalar.activation(w_hi[:], w_raw[:], ACT.Copy).then_inc(w_hi_made, 1)
                    rotated_hi("K0")
                    value_hi("V0")
                    rotated_hi("Q0")
                    act.wait_ge(wo_in, 16 * (it + 1))
                    act.wait_ge(projected, now(it, USES, 0))
                    nc.scalar.activation(wo_hi[:], wo_raw[:], ACT.Copy).then_inc(wo_hi_made, 1)
                    for n in range(POSITIONS):
                        if n >= 6 and n % 2 == 0:
                            j = (n - 6) // 2
                            act.wait_ge(o_summed, now(it, PAIRS, j + 1))
                            nc.scalar.activation(o_hi[:, half_of(2 * j), head_of(2 * j), 256 * (j % 2):256 * (j % 2) + 256],
                                                 o_ps[:, 0:256], ACT.Copy).then_inc(o_hi_made, 1)
                        if 2 <= n < STEPS + 2:
                            m = n - 2
                            for i, (a, z) in enumerate(chunks(m)):
                                c = chunks_before(m) + i
                                act.wait_ge(transposed, now(it, CHUNKS, c + 1))
                                act.wait_ge(o_summed, now(it, PAIRS, m // 2 - 1))
                                nc.scalar.activation(pt_hi[:, m // 2 % 2, a:z, P * (m % 2):P * (m % 2) + P],
                                                     pt_ps[c % 2][:, 0:P * (z - a)].rearrange("p (k q) -> p k q", q=P),
                                                     ACT.Copy).then_inc(pt_hi_made, 1)
                        if n < STEPS:
                            act.wait_ge(max_made, now(it, STEPS, n + 1))
                            act.wait_ge(transposed, now(it, CHUNKS, chunks_before(n - 3)))
                            w = key_tiles(n) * P
                            nc.scalar.activation(probs[:, n % 4, 0:w], scores_ps[n % 2][:, 0:w], ACT.Exp,
                                                 bias=neg_max[:, n % 4:n % 4 + 1],
                                                 accum_out=row_sum[:, n % 4:n % 4 + 1]).then_inc(exped, 1)
                        if USE_AT.get(n - 1) in ROPES:
                            rotated_hi(USE_AT[n - 1])
                        if USE_AT.get(n, " ")[0] == "V":
                            value_hi(USE_AT[n])

        @block.vector
        def _(dve):
            dve.sem_inc(x_split, 2)
            dve.sem_inc(w_split, 1)
            dve.sem_inc(proj_free, USES)
            dve.sem_inc(max_made, STEPS)
            dve.sem_inc(inv_made, STEPS)
            dve.sem_inc(scaled, STEPS)
            dve.sem_inc(pt_split, CHUNKS)
            dve.sem_inc(o_split, PAIRS)
            dve.wait_ge(tables_in, 32)
            dve.wait_ge(resid_in, 16)
            with dve.Fori(0, B) as b:
                for c in range(2):
                    dve.wait_ge(x_hi_made, now(b, 2, c + 1))
                    cols = slice(c * HALF, (c + 1) * HALF)
                    nc.vector.tensor_tensor(x_lo[:, :, cols], x_raw[:], x_hi[:, :, cols].bitcast(F32),
                                            ALU.subtract).then_inc(x_split, 1)
                with dve.Fori(0, NKV) as kv:
                    it = b * NKV + kv

                    def evacuate(name):
                        use = K_OF[name]
                        dve.wait_ge(projected, now(it, USES, use + 1))
                        if name[0] == "O":
                            a = int(name[1])
                            tok = resid[:].rearrange("p i c -> p (i c)")[:, bass.ds(b * (BT * H) + a * 2 * H, 2 * H)]
                            nc.vector.tensor_tensor(tok, proj_ps[:], tok, ALU.add).then_inc(proj_free, 1)
                        elif name[0] == "V":
                            c = half(name)
                            dve.wait_ge(v_hi_made, now(it, 2, c + 1))
                            nc.vector.tensor_tensor(v_lo[:, 4 * c:4 * c + 4, :].rearrange("p t d -> p (t d)"), proj_ps[:],
                                                    v_hi[:, 4 * c:4 * c + 4, :].rearrange("p t d -> p (t d)").bitcast(F32),
                                                    ALU.subtract).then_inc(proj_free, 1)
                        else:
                            r = ROPES[name]
                            pos = slice(half(name) * HALF, (half(name) + 1) * HALF)
                            dve.wait_ge(turned_sum, now(it, len(ROPES), r - 1))
                            nc.vector.tensor_tensor(turn_cos[:, r % 2], proj_ps[:], cos[:, pos], ALU.mult)
                            nc.vector.tensor_tensor(turn_sin[0:64, r % 2], proj_ps[64:128, :], sin[64:128, pos], ALU.mult)
                            nc.vector.tensor_tensor(turn_sin[64:128, r % 2], proj_ps[0:64, :], sin[0:64, pos],
                                                    ALU.mult).then_inc(proj_free, 1)

                    dve.wait_ge(w_hi_made, now(it, 1, 1))
                    nc.vector.tensor_tensor(w_lo[:], w_raw[:], w_hi[:].bitcast(F32), ALU.subtract).then_inc(w_split, 1)
                    for name in FIRST_USES:
                        evacuate(name)
                    for n in range(POSITIONS):
                        if n < STEPS:
                            dve.wait_ge(scored, now(it, STEPS, n + 1))
                            nc.vector.tensor_reduce(neg_max[:, n % 4:n % 4 + 1], scores_ps[n % 2][:, 0:key_tiles(n) * P],
                                                    AX.X, ALU.max, negate=True).then_inc(max_made, 1)
                        if n >= 6 and n % 2 == 0:
                            j = (n - 6) // 2
                            out = slice(256 * (j % 2), 256 * (j % 2) + 256)
                            dve.wait_ge(o_hi_made, now(it, PAIRS, j + 1))
                            nc.vector.tensor_tensor(o_lo[:, half_of(2 * j), head_of(2 * j), out], o_ps[:, 0:256],
                                                    o_hi[:, half_of(2 * j), head_of(2 * j), out].bitcast(F32),
                                                    ALU.subtract).then_inc(o_split, 1)
                        if 2 <= n < STEPS + 2:
                            m = n - 2
                            for i, (a, z) in enumerate(chunks(m)):
                                c = chunks_before(m) + i
                                part = (slice(None), m // 2 % 2, slice(a, z), slice(P * (m % 2), P * (m % 2) + P))
                                dve.wait_ge(pt_hi_made, now(it, CHUNKS, c + 1))
                                nc.vector.tensor_tensor(pt_lo[part],
                                                        pt_ps[c % 2][:, 0:P * (z - a)].rearrange("p (k q) -> p k q", q=P),
                                                        pt_hi[part].bitcast(F32), ALU.subtract).then_inc(pt_split, 1)
                        if n < STEPS:
                            w = key_tiles(n) * P
                            dve.wait_ge(exped, now(it, STEPS, n + 1))
                            nc.vector.reciprocal(row_inv[:, n % 4:n % 4 + 1], row_sum[:, n % 4:n % 4 + 1]).then_inc(inv_made, 1)
                            dve.wait_ge(inv_made, now(it, STEPS, n + 1))
                            nc.vector.tensor_scalar(probs[:, n % 4, 0:w], probs[:, n % 4, 0:w], row_inv[:, n % 4:n % 4 + 1],
                                                    None, ALU.mult).then_inc(scaled, 1)
                        if n in USE_AT:
                            evacuate(USE_AT[n])
                    for name in LAST_USES:
                        evacuate(name)

        @block.tensor
        def _(pe):
            pe.sem_inc(projected, USES)
            pe.sem_inc(scored, STEPS)
            pe.sem_inc(transposed, CHUNKS)
            pe.sem_inc(o_summed, PAIRS)
            pe.wait_ge(consts_made, 2)

            def products(out, left, right, first, last):
                (lh, ll), (rh, rl) = left, right
                nc.tensor.matmul(out, lh, rh, start=first, stop=False)
                nc.tensor.matmul(out, lh, rl, start=False, stop=False)
                return nc.tensor.matmul(out, ll, rh, start=False, stop=last)

            with pe.Fori(0, B) as b:
                with pe.Fori(0, NKV) as kv:
                    it = b * NKV + kv

                    def project(name):
                        use = K_OF[name]
                        pe.wait_ge(proj_free, now(it, USES, use))
                        if name[0] == "O":
                            a = int(name[1])
                            if a % 2 == 0:
                                pe.wait_ge(o_split, now(it, PAIRS, PAIRS // 2 * (a // 2 + 1)))
                                pe.wait_ge(wo_split, now(it, 1, 1))
                            for t in range(2):
                                tok = slice((a % 2 * 2 + t) * P, (a % 2 * 2 + t + 1) * P)
                                for h in range(GROUP):
                                    mm = products(proj_ps[:, t * H:(t + 1) * H], (o_hi[:, a // 2, h, tok], o_lo[:, a // 2, h, tok]),
                                                  (wo_hi[:, h, :], wo_lo[:, h, :]), h == 0, h == GROUP - 1)
                        elif name[0] == "V":
                            for t in range(4):
                                tok = slice((4 * half(name) + t) * P, (4 * half(name) + t + 1) * P)
                                for k in range(HK):
                                    mm = products(proj_ps[:, t * HD:(t + 1) * HD], (x_hi[:, k, tok], x_lo[:, k, tok]),
                                                  (w_hi[:, k, w_cols(name)], w_lo[:, k, w_cols(name)]), k == 0, k == HK - 1)
                        else:
                            tok = slice(half(name) * HALF, (half(name) + 1) * HALF)
                            for k in range(HK):
                                mm = products(proj_ps[:], (w_hi[:, k, w_cols(name)], w_lo[:, k, w_cols(name)]),
                                              (x_hi[:, k, tok], x_lo[:, k, tok]), k == 0, k == HK - 1)
                        mm.then_inc(projected, 1)

                    pe.wait_ge(x_split, now(b, 2, 2))
                    pe.wait_ge(w_split, now(it, 1, 1))
                    for name in FIRST_USES:
                        project(name)
                    for n in range(POSITIONS):
                        if n < STEPS:
                            if n % 4 == 0:
                                qi = n // 4
                                pe.wait_ge(turned_split, now(it, len(ROPES), ROPES[f"Q{qi}"] + 1))
                            pe.wait_ge(exped, now(it, STEPS, n - 1))
                            qt = (slice(None), n // 4 % 2, slice(P * (n % 4), P * (n % 4) + P))
                            for a, z in chunks(n):
                                keys = slice(a * P, z * P)
                                out = scores_ps[n % 2][:, keys]
                                nc.tensor.matmul(out, q_hi[qt], k_hi[:, keys], start=True, stop=False)
                                nc.tensor.matmul(out, q_hi[qt], k_lo[:, keys], start=False, stop=False)
                                if z == key_tiles(n):
                                    nc.tensor.matmul(scores_ps[n % 2][:, (z - 1) * P:z * P], ident_bf[:], causal[:],
                                                     start=False, stop=False)
                                mm = nc.tensor.matmul(out, q_lo[qt], k_hi[:, keys], start=False, stop=True)
                            mm.then_inc(scored, 1)
                        if 2 <= n < STEPS + 2:
                            m = n - 2
                            pe.wait_ge(scaled, now(it, STEPS, m + 1))
                            for i, (a, z) in enumerate(chunks(m)):
                                c = chunks_before(m) + i
                                pe.wait_ge(pt_split, now(it, CHUNKS, c - 1))
                                for k in range(a, z):
                                    mm = nc.tensor.transpose(pt_ps[c % 2][:, (k - a) * P:(k - a + 1) * P],
                                                             probs[:, m % 4, k * P:(k + 1) * P], ident[:])
                                mm.then_inc(transposed, 1)
                        if 4 <= n < STEPS + 4:
                            j = (n - 4) // 2
                            count = key_tiles(2 * j + 1)
                            if n % 2 == 0:
                                pe.wait_ge(pt_split, now(it, CHUNKS, chunks_before(2 * j + 2)))
                                pe.wait_ge(o_split, now(it, PAIRS, j))
                            for k in (range(count // 2) if n % 2 == 0 else range(count // 2, count)):
                                q0 = P if k == count - 1 else 0
                                qs = slice(q0, 2 * P)
                                mm = products(o_ps[:, qs], (v_hi[:, k, :], v_lo[:, k, :]),
                                              (pt_hi[:, j % 2, k, qs], pt_lo[:, j % 2, k, qs]), k == 0, k == count - 1)
                            if n % 2 == 1:
                                mm.then_inc(o_summed, 1)
                        if n in USE_AT:
                            project(USE_AT[n])
                    for name in LAST_USES:
                        project(name)


def routing(nc, dram, resid, consts):
    with ExitStack() as ctx:
        def sb(name, shape, dt=F32):
            return ctx.enter_context(nc.sbuf_tensor(name, shape, dt))

        def sem(name):
            return ctx.enter_context(nc.semaphore(name))

        ident = consts["ident"]
        stats, moments = sb("stats", [P, TILES, 6]), sb("moments", [P, TILES, 2])
        deviation, inv_dev = sb("deviation", [P, TILES]), sb("inv_dev", [P, TILES])
        xt = sb("xt", [P, 2, HK, P])
        gate = sb("gate", [P, HK, E])
        logits = sb("logits", [P, TILES, E])
        top, top_at = sb("top", [P, TILES, 8]), sb("top_at", [P, TILES, 8], U32)
        top_id = sb("top_id", [P, TILES, 8])
        shifted, exp_all = sb("shifted", [P, TILES, E]), sb("exp_all", [P, TILES, E])
        exp_top = sb("exp_top", [P, TILES, TOPK])
        sum_all, sum_top = sb("sum_all", [P, TILES]), sb("sum_top", [P, TILES])
        expert_ids = sb("expert_ids", [P, E])
        chosen = sb("chosen", [P, TOPK, TILES, E], BF16)
        mask = sb("mask", [P, 2, TILES, E], BF16)
        before, ones = sb("before", [P, P], BF16), sb("ones", [P, P], BF16)
        counts, counts_int = sb("counts", [P, E]), sb("counts_int", [P, E], I32)
        blocks, blocks_to, first_row = sb("blocks", [P, E]), sb("blocks_to", [P, E]), sb("first_row", [P, E])
        one_row = sb("one_row", [P, E])
        slot_of = sb("slot_of", [P, TILES, E])
        product = sb("product", [P, TILES, E])
        slots, slots_int = sb("slots", [P, TILES, TOPK]), sb("slots_int", [P, TILES, TOPK], I32)
        goes_with = sb("goes_with", [P, TILES, WAYS, 2])
        rows = sb("rows", [P, 2, WAYS, ROW])
        block_id = sb("block_id", [P, 1])
        started, owner, owner_int = sb("started", [P, E]), sb("owner", [P, 2]), sb("owner_int", [P, 1], I32)
        pairs, pairs_int = sb("pairs", [P, 1]), sb("pairs_int", [P, 1], I32)

        logits_ps = ctx.enter_context(nc.psum_tensor("logits_ps", [P, TILES * E], F32))
        places_ps = ctx.enter_context(nc.psum_tensor("places_ps", [P, TILES * E], F32))
        xt_ps = [ctx.enter_context(nc.psum_tensor(f"xt_ps{i}", [P, 512], F32)) for i in range(2)]
        counts_ps = ctx.enter_context(nc.psum_tensor("counts_ps", [P, 512], F32))

        gate_in, table_out, table_in = sem("gate_in"), sem("table_out"), sem("table_in")
        consts_set, const_step, iotas = sem("consts_set"), sem("const_step"), sem("iotas")
        dve_step = sem("dve_step")
        moments_made, deviation_made, normed = sem("moments_made"), sem("deviation_made"), sem("normed")
        xt_turned, xt_made, logits_made = sem("xt_turned"), sem("xt_made"), sem("logits_made")
        shifted_made, exps_made = sem("shifted_made"), sem("exps_made")
        mask_made, places_made = sem("mask_made"), sem("places_made")
        slots_made, weights_made, table_made = sem("slots_made"), sem("weights_made"), sem("table_made")
        rows_filled, rows_ready = sem("rows_filled"), sem("rows_ready")
        sent = [sem(f"sent{i}") for i in range(2)]
        shared_sent = [sem(f"shared_sent{i}") for i in range(2)]

        block = ctx.enter_context(nc.Block())
        shared_rows = dram["rows"][0:SHARED * T, :].rearrange("(s i p) c -> i s p c", s=SHARED, p=P)

        @block.sync
        def _(sp):
            sp.dma_start(gate[:], dram["gate"]).then_inc(gate_in, 16)
            sp.wait_ge(table_made, 1)
            sp.dma_start(dram["table"][0:P, :], owner_int[:]).then_inc(table_out, 16)
            sp.dma_start(dram["table"][P:P + 1, :], pairs_int[0:1, :]).then_inc(table_out, 16)
            sp.wait_ge(table_out, 32)
            sp.dma_start(consts["table"][:], dram["table"].rearrange("r c -> c r")).then_inc(table_in, 16)
            for i in range(TILES):
                sp.wait_ge(rows_ready, i + 1)
                for s in range(SHARED):
                    sp.dma_start(shared_rows[i, s], rows[:, i % 2, TOPK + s, :]).then_inc(shared_sent[i % 2], 16)
            sp.wait_ge(table_in, 16)
            for i in range(2):
                sp.wait_ge(shared_sent[i], 16 * SHARED * TILES // 2)

        @block.gpsimd
        def _(pool):
            pool.memset(before[:], 1.0).then_inc(const_step, 1)
            pool.memset(ones[:], 1.0).then_inc(const_step, 1)
            pool.memset(one_row[:], 1.0).then_inc(const_step, 1)
            pool.memset(goes_with[:], 1.0).then_inc(const_step, 1)
            pool.iota(expert_ids[:], [[1, E]], base=0, channel_multiplier=0,
                      allow_small_or_imprecise_dtypes=True).then_inc(const_step, 1)
            pool.iota(block_id[:], [[0, 1]], base=0, channel_multiplier=1,
                      allow_small_or_imprecise_dtypes=True).then_inc(const_step, 1)
            pool.wait_ge(const_step, 6)
            pool.affine_select(before[:], before[:], [[1, P]], ALU.is_gt, 0.0, base=0,
                               channel_multiplier=-1).then_inc(const_step, 1)
            pool.iota(goes_with[:, :, :, 0], [[P, TILES], [T, WAYS]], base=0, channel_multiplier=1,
                      allow_small_or_imprecise_dtypes=True).then_inc(const_step, 1)
            pool.wait_ge(const_step, 8)
            pool.sem_inc(consts_set, 1)
            pool.wait_ge(slots_made, 1)
            for i in range(TILES):
                pool.wait_ge(rows_ready, i + 1)
                for j in range(TOPK):
                    pool.indirect_dma_start(
                        out=dram["rows"], out_offset=bass.IndirectOffsetOnAxis(ap=slots_int[:, i, j:j + 1], axis=0),
                        in_=rows[:, i % 2, j, :], in_offset=None, bounds_check=ROWS - 1,
                        oob_is_err=False).then_inc(sent[i % 2], 16)
            for i in range(2):
                pool.wait_ge(sent[i], 16 * TOPK * TILES // 2)

        @block.scalar
        def _(act):
            act.wait_ge(moments_made, 1)
            act.activation(deviation[:], deviation[:], ACT.Sqrt).then_inc(deviation_made, 1)
            for i in range(TILES):
                act.wait_ge(xt_turned, i + 1)
                if i >= 2:
                    act.wait_ge(logits_made, i - 1)
                act.activation(xt[:, i % 2].rearrange("p k t -> p (k t)"), xt_ps[i % 2][:, 0:H], ACT.Copy).then_inc(xt_made, 1)
            act.wait_ge(shifted_made, 1)
            act.activation(exp_all[:], shifted[:], ACT.Exp).then_inc(exps_made, 1)
            act.activation(exp_top[:], exp_top[:], ACT.Exp).then_inc(exps_made, 1)
            for i in range(TILES):
                if i >= 2:
                    act.wait_ge(sent[i % 2], 16 * TOPK * (i // 2))
                    act.wait_ge(shared_sent[i % 2], 16 * SHARED * (i // 2))
                act.activation(rows[:, i % 2, :, 0:H], resid[:, i, :].unsqueeze(1).broadcast_to([P, WAYS, H]),
                               ACT.Copy).then_inc(rows_filled, 1)

        @block.vector
        def _(dve):
            steps = [0]

            def then(ins):
                steps[0] += 1
                ins.then_inc(dve_step, 1)
                dve.wait_ge(dve_step, steps[0])

            for i in range(TILES):
                ins = dve.bn_stats(stats[:, i, :], resid[:, i, :])
            then(ins)
            for i in range(TILES):
                ins = dve.bn_aggr(moments[:, i, :], stats[:, i, :])
            then(ins)
            dve.tensor_scalar(deviation[:], moments[:, :, 1], EPS_LN, None, ALU.add).then_inc(moments_made, 1)
            dve.wait_ge(deviation_made, 1)
            then(dve.reciprocal(inv_dev[:], deviation[:]))
            for i in range(TILES):
                dve.tensor_scalar(resid[:, i, :], resid[:, i, :], moments[:, i, 0:1], inv_dev[:, i:i + 1],
                                  ALU.subtract, ALU.mult).then_inc(normed, 1)
            dve.wait_ge(consts_set, 1)
            dve.wait_ge(logits_made, TILES)
            then(dve.tensor_copy(logits[:].rearrange("p i e -> p (i e)"), logits_ps[:]))
            for i in range(TILES):
                ins = dve.max(top[:, i, :], logits[:, i, :])
            then(ins)
            for i in range(TILES):
                ins = dve.max_index(top_at[:, i, :], top[:, i, :], logits[:, i, :])
            dve.tensor_tensor(shifted[:], logits[:], top[:, :, 0:1].broadcast_to([P, TILES, E]), ALU.subtract)
            dve.tensor_tensor(exp_top[:], top[:, :, 0:TOPK], top[:, :, 0:1].broadcast_to([P, TILES, TOPK]),
                              ALU.subtract).then_inc(shifted_made, 1)
            dve.wait_ge(shifted_made, 1)
            then(dve.tensor_copy(top_id[:], top_at[:]))
            for j in range(TOPK):
                ins = dve.tensor_tensor(chosen[:, j], expert_ids[:].unsqueeze(1).broadcast_to([P, TILES, E]),
                                        top_id[:, :, j:j + 1].broadcast_to([P, TILES, E]), ALU.is_equal)
            then(ins)
            then(dve.tensor_tensor(mask[:, 1], chosen[:, 0], chosen[:, 1], ALU.add))
            for j in range(2, TOPK):
                ins = dve.tensor_tensor(mask[:, j % 2], mask[:, (j - 1) % 2], chosen[:, j], ALU.add)
                then(ins)
            dve.sem_inc(mask_made, 1)
            dve.wait_ge(places_made, 1)
            then(dve.tensor_scalar(counts[:], counts_ps[:, 0:E], float(BLK - 1), None, ALU.add))
            then(dve.tensor_copy(counts_int[:], counts[:]))
            then(dve.tensor_scalar(counts_int[:], counts_int[:], BLK.bit_length() - 1, None, ALU.logical_shift_right))
            then(dve.tensor_copy(blocks[:], counts_int[:]))
            then(dve.tensor_tensor_scan(blocks_to[:], one_row[:], blocks[:], float(SHARED_BLOCKS), ALU.mult, ALU.add))
            then(dve.tensor_tensor(started[:], blocks_to[:], blocks[:], ALU.subtract))
            then(dve.tensor_scalar(first_row[:], started[:], float(BLK), None, ALU.mult))
            dve.wait_ge(places_made, 2)
            then(dve.tensor_tensor(slot_of[:], places_ps[:].rearrange("p (i e) -> p i e", e=E),
                                   first_row[:].unsqueeze(1).broadcast_to([P, TILES, E]), ALU.add))
            for j in range(TOPK):
                then(dve.tensor_tensor(product[:], chosen[:, j], slot_of[:], ALU.mult))
                then(dve.tensor_reduce(slots[:, :, j], product[:], AX.X, ALU.add))
            dve.tensor_copy(slots_int[:], slots[:]).then_inc(slots_made, 1)
            dve.wait_ge(exps_made, 2)
            dve.tensor_reduce(sum_all[:], exp_all[:], AX.X, ALU.add)
            then(dve.tensor_reduce(sum_top[:], exp_top[:], AX.X, ALU.add))
            then(dve.scalar_tensor_tensor(out=sum_top[:], in0=sum_all[:], scalar=EPS_TOPK, in1=sum_top[:],
                                          op0=ALU.mult, op1=ALU.add))
            then(dve.reciprocal(sum_top[:], sum_top[:]))
            then(dve.tensor_tensor(goes_with[:, :, 0:TOPK, 1], exp_top[:],
                                   sum_top[:].unsqueeze(2).broadcast_to([P, TILES, TOPK]), ALU.mult))
            for i in range(TILES):
                dve.wait_ge(rows_filled, i + 1)
                dve.tensor_copy(rows[:, i % 2, :, H:ROW], goes_with[:, i]).then_inc(rows_ready, 1)
                if i == 0:
                    then(dve.tensor_scalar(started[:], started[:], block_id[:], None, ALU.is_le))
                    then(dve.tensor_reduce(owner[:, 0:1], started[:], AX.X, ALU.add))
                    then(dve.tensor_scalar(owner[:, 1:2], block_id[:], float(SHARED_BLOCKS // SHARED), None, ALU.is_ge))
                    then(dve.tensor_tensor(owner[:, 0:1], owner[:, 0:1], owner[:, 1:2], ALU.add))
                    then(dve.tensor_copy(owner_int[:], owner[:, 0:1]))
                    then(dve.tensor_copy(pairs_int[:], blocks_to[:, E - 1:E]))
                    dve.tensor_scalar(pairs_int[:], pairs_int[:], 1, None,
                                      ALU.logical_shift_right).then_inc(table_made, 1)

        @block.tensor
        def _(pe):
            pe.wait_ge(gate_in, 16)

            def turn(i):
                pe.wait_ge(normed, i + 1)
                if i >= 2:
                    pe.wait_ge(xt_made, i - 1)
                for k in range(HK):
                    mm = nc.tensor.transpose(xt_ps[i % 2][:, k * P:(k + 1) * P], resid[:, i, k * P:(k + 1) * P], ident[:])
                mm.then_inc(xt_turned, 1)

            turn(0)
            for i in range(TILES):
                if i + 1 < TILES:
                    turn(i + 1)
                pe.wait_ge(xt_made, i + 1)
                for k in range(HK):
                    mm = nc.tensor.matmul(logits_ps[:, i * E:(i + 1) * E], xt[:, i % 2, k, :], gate[:, k, :],
                                          start=(k == 0), stop=(k == HK - 1))
                mm.then_inc(logits_made, 1)
            pe.wait_ge(mask_made, 1)
            pe.wait_ge(consts_set, 1)
            picks = mask[:, (TOPK - 1) % 2]
            for i in range(TILES):
                mm = nc.tensor.matmul(counts_ps[:, 0:E], ones[:], picks[:, i, :], start=(i == 0), stop=(i == TILES - 1))
            mm.then_inc(places_made, 1)
            for i in range(TILES):
                out = places_ps[:, i * E:(i + 1) * E]
                mm = nc.tensor.matmul(out, before[:], picks[:, i, :], start=True, stop=(i == 0))
                for k in range(i):
                    mm = nc.tensor.matmul(out, ones[:], picks[:, k, :], start=False, stop=(k == i - 1))
            mm.then_inc(places_made, 1)


def done(n, back=0):
    return n + 3 - back


def experts(nc, dram, resid, consts, out):
    with ExitStack() as ctx:
        def sb(name, shape, dt=F32):
            return ctx.enter_context(nc.sbuf_tensor(name, shape, dt))

        def sem(name):
            return ctx.enter_context(nc.semaphore(name))

        def both(name):
            return [sem(f"{name}{i}") for i in range(2)]

        ident, table = consts["ident"], consts["table"]
        up_w = [sb(f"up_w{i}", [P, HK, GCOLS]) for i in range(2)]
        down_w = [sb(f"down_w{i}", [P, 2, H]) for i in range(2)]
        x_in = [sb(f"x_in{i}", [P, SUB, ROW]) for i in range(2)]
        xt = [sb(f"xt{i}", [P, HK, BLK]) for i in range(2)]
        silu = [sb(f"silu{i}", [P, 2, BLK]) for i in range(2)]
        hidden = [sb(f"hidden{i}", [P, 2, BLK]) for i in range(2)]
        y_sb = [sb(f"y_sb{i}", [P, SUB, H]) for i in range(2)]
        dest = [sb(f"dest{i}", [P, SUB], I32) for i in range(2)]
        goes_with = sb("goes_with_all", [P, MAX_BLOCKS + 1, SUB, 2])
        RING = 4
        parts = [sb(f"parts{i}", [P, WAYS, H]) for i in range(RING)]
        total = sb("total", [P, 2, H])
        stats, moments = sb("stats2", [P, TILES, 6]), sb("moments2", [P, TILES, 2])
        deviation, inv_dev = sb("deviation2", [P, TILES]), sb("inv_dev2", [P, TILES])

        xt_ps = ctx.enter_context(nc.psum_tensor("x_ps", [P, 512], F32))
        gate_up_ps = [ctx.enter_context(nc.psum_tensor(f"gate_up{i}", [P, 512], F32)) for i in range(2)]
        tail_ps = [ctx.enter_context(nc.psum_tensor(f"tail{i}", [P, 512], F32)) for i in range(2)]
        y_ps = [ctx.enter_context(nc.psum_tensor(f"y{i}", [P, 512], F32)) for i in range(2)]

        up_in, down_in, rows_in, y_out = both("up_in"), both("down_in"), both("rows_in"), both("y_out")
        x_turned, xt_made, goes_made = sem("x_turned"), sem("xt_made"), sem("goes_made")
        gated, silu_made, hidden_made = sem("gated"), sem("silu_made"), sem("hidden_made")
        downed, y_made, y_sent = sem("downed"), sem("y_made"), sem("y_sent")
        send_begun, all_sent = sem("send_begun"), sem("all_sent")
        parts_in = [sem(f"parts_in{i}") for i in range(RING)]
        parts_used, dve_step = sem("parts_used"), sem("dve_step2")
        variance_made, deviation_made, normed, out_done = sem("variance_made"), sem("deviation_made"), sem("normed2"), sem("out_done")

        block = ctx.enter_context(nc.Block())
        row_blocks = dram["rows"].rearrange("(n p s) c -> n p s c", p=P, s=SUB)
        results = dram["results"].rearrange("(j i p) c -> i p j c", j=WAYS, p=P)
        out_tiles = out.rearrange("b (i p) c -> (b i) p c", p=P)

        def pairs_of(eng):
            return eng.value_load(table[0:1, P:P + 1], min_val=SHARED_BLOCKS // 2, max_val=MAX_BLOCKS // 2)

        @block.sync
        def _(sp):
            def load_rows(n, buf, count):
                sp.wait_ge(x_turned, done(n, 2))
                sp.wait_ge(goes_made, done(n, 2))
                sp.dma_start(x_in[buf][:], row_blocks[bass.ds(n, 1)].rearrange("o p s c -> (o p) s c")).then_inc(rows_in[buf], 16)

            def load_weights(n, buf):
                e = sp.value_load(table[0:1, bass.ds(n, 1)], min_val=0, max_val=E + SHARED - 1)
                sp.wait_ge(gated, done(n, 2))
                sp.dma_start(up_w[buf][:], dram["up"][bass.ds(e, 1)].rearrange("o p k c -> (o p) k c")).then_inc(up_in[buf], 16)
                sp.wait_ge(downed, done(n, 2))
                sp.dma_start(down_w[buf][:, 0, :], dram["down"][bass.ds(e, 1)].rearrange("o p c -> (o p) c")).then_inc(down_in[buf], 16)
                sp.dma_start(down_w[buf][0:TAIL, 1, :], dram["down_tail"][bass.ds(e, 1)].rearrange("o p c -> (o p) c")).then_inc(down_in[buf], 16)

            pairs = pairs_of(sp)
            load_rows(0, 0, 0)
            load_weights(0, 0)
            load_rows(1, 1, 0)
            with sp.Fori(0, pairs) as i:
                for u in range(2):
                    n = 2 * i + (1 + u)
                    load_weights(n, (1 + u) % 2)
                    load_rows(n + 1, u, 0)
            sp.wait_ge(all_sent, 1)
            for t in range(TILES):
                if t >= RING:
                    sp.wait_ge(parts_used, t - RING + 1)
                sp.dma_start(parts[t % RING][:], results[t]).then_inc(parts_in[t % RING], 16)
            for t in range(TILES):
                sp.wait_ge(normed, t + 1)
                sp.dma_start(out_tiles[t], resid[:, t, :]).then_inc(out_done, 16)
            sp.wait_ge(out_done, 16 * TILES)

        @block.gpsimd
        def _(pool):
            pool.sem_inc(y_sent, 2)
            last_row = pool.to_reg(WAYS * T - 1)

            def send(n, buf):
                pool.wait_ge(y_made, done(n))
                pool.sem_inc(send_begun, 1)
                for s in range(SUB):
                    pool.indirect_dma_start(
                        out=dram["results"], out_offset=bass.IndirectOffsetOnAxis(ap=dest[buf][:, s:s + 1], axis=0),
                        in_=y_sb[buf][:, s, :], in_offset=None, bounds_check=last_row,
                        oob_is_err=False).then_inc(y_out[buf], 16)

            def sent(buf, count):
                pool.wait_ge(y_out[buf], 16 * SUB * count)
                pool.sem_inc(y_sent, 1)

            pairs = pairs_of(pool)
            send(0, 0)
            with pool.Fori(0, pairs) as i:
                sent(0, i + 1)
                send(2 * i + 1, 1)
                sent(1, i + 1)
                send(2 * i + 2, 0)
            sent(0, pairs + 1)
            pool.sem_inc(all_sent, 1)

        @block.scalar
        def _(act):
            act.sem_inc(xt_made, 2)
            act.sem_inc(silu_made, 2)

            def turned(n, buf):
                act.wait_ge(x_turned, done(n))
                act.wait_ge(gated, done(n, 2))
                nc.scalar.activation(xt[buf][:].rearrange("p k t -> p (k t)"), xt_ps[:], ACT.Copy).then_inc(xt_made, 1)

            def gate(n, buf):
                act.wait_ge(gated, done(n))
                act.wait_ge(hidden_made, done(n, 2))
                nc.scalar.activation(silu[buf][:, 0, :], gate_up_ps[buf][:, 0:BLK], ACT.Silu)
                nc.scalar.activation(silu[buf][0:TAIL, 1, :], tail_ps[buf][0:TAIL, 0:BLK], ACT.Silu).then_inc(silu_made, 1)

            pairs = pairs_of(act)
            turned(0, 0)
            gate(0, 0)
            turned(1, 1)
            with act.Fori(0, pairs) as i:
                for u in range(2):
                    n = 2 * i + (1 + u)
                    gate(n, (1 + u) % 2)
                    turned(n + 1, u)
            act.wait_ge(variance_made, 1)
            nc.scalar.activation(deviation[:], deviation[:], ACT.Sqrt).then_inc(deviation_made, 1)

        @block.vector
        def _(dve):
            dve.sem_inc(goes_made, 2)
            dve.sem_inc(hidden_made, 2)
            dve.sem_inc(y_made, 2)

            def note(n, buf, count):
                dve.wait_ge(rows_in[buf], 16 * count)
                dve.tensor_copy(goes_with[:, bass.ds(n, 1)].rearrange("p o s c -> p (o s) c"), x_in[buf][:, :, H:ROW]).then_inc(goes_made, 1)

            def hide(n, buf):
                dve.wait_ge(silu_made, done(n))
                dve.wait_ge(downed, done(n, 2))
                dve.tensor_tensor(hidden[buf][:, 0, :], silu[buf][:, 0, :], gate_up_ps[buf][:, BLK:2 * BLK], ALU.mult)
                dve.tensor_tensor(hidden[buf][0:TAIL, 1, :], silu[buf][0:TAIL, 1, :], tail_ps[buf][UP_AT:UP_AT + TAIL, 0:BLK],
                                  ALU.mult).then_inc(hidden_made, 1)

            def weigh(n, buf):
                dve.wait_ge(downed, done(n))
                dve.wait_ge(y_sent, done(n, 2))
                dve.wait_ge(goes_made, done(n))
                dve.tensor_copy(dest[buf][:], goes_with[:, bass.ds(n, 1), :, 0].rearrange("p o s -> p (o s)"))
                for s in range(SUB):
                    ins = dve.tensor_tensor(y_sb[buf][:, s, :], y_ps[buf][:, s * H:(s + 1) * H],
                                            goes_with[:, bass.ds(n, 1), s, 1].broadcast_to([P, H]), ALU.mult)
                ins.then_inc(y_made, 1)

            pairs = pairs_of(dve)
            note(0, 0, 1)
            hide(0, 0)
            note(1, 1, 1)
            with dve.Fori(0, pairs) as i:
                hide(2 * i + 1, 1)
                note(2 * i + 2, 0, i + 2)
                weigh(2 * i, 0)
                hide(2 * i + 2, 0)
                note(2 * i + 3, 1, i + 2)
                weigh(2 * i + 1, 1)
            weigh(2 * pairs, 0)

            steps = [0]

            def then(ins):
                steps[0] += 1
                ins.then_inc(dve_step, 1)
                dve.wait_ge(dve_step, steps[0])

            for t in range(TILES):
                dve.wait_ge(parts_in[t % RING], 16 * (t // RING + 1))
                ins = dve.tensor_reduce(total[:, t % 2, :], parts[t % RING][:].rearrange("p j c -> p c j"), AX.X, ALU.add)
                ins.then_inc(parts_used, 1)
                dve.wait_ge(parts_used, t + 1)
                then(dve.tensor_tensor(resid[:, t, :], resid[:, t, :], total[:, t % 2, :], ALU.add))
                then(dve.bn_stats(stats[:, t, :], resid[:, t, :]))
                then(dve.bn_aggr(moments[:, t, :], stats[:, t, :]))
            dve.tensor_scalar(deviation[:], moments[:, :, 1], EPS_LN, None, ALU.add).then_inc(variance_made, 1)
            dve.wait_ge(deviation_made, 1)
            then(dve.reciprocal(inv_dev[:], deviation[:]))
            for t in range(TILES):
                dve.tensor_scalar(resid[:, t, :], resid[:, t, :], moments[:, t, 0:1], inv_dev[:, t:t + 1],
                                  ALU.subtract, ALU.mult).then_inc(normed, 1)

        @block.tensor
        def _(pe):
            pe.sem_inc(x_turned, 2)
            pe.sem_inc(gated, 2)
            pe.sem_inc(downed, 2)

            def turn(n, buf, count):
                pe.wait_ge(rows_in[buf], 16 * count)
                pe.wait_ge(xt_made, done(n, 1))
                for k in range(HK):
                    for s in range(SUB):
                        mm = nc.tensor.transpose(xt_ps[:, k * BLK + s * P:k * BLK + (s + 1) * P],
                                                 x_in[buf][:, s, k * P:(k + 1) * P], ident[:])
                mm.then_inc(x_turned, 1)

            def gate_up(n, buf, count):
                pe.wait_ge(up_in[buf], 16 * count)
                pe.wait_ge(xt_made, done(n))
                pe.wait_ge(hidden_made, done(n, 2))
                for out, c, z in ((gate_up_ps[buf][:, 0:BLK], 0, P), (gate_up_ps[buf][:, BLK:2 * BLK], P, 2 * P),
                                  (tail_ps[buf][0:GCOLS - 2 * P, 0:BLK], 2 * P, GCOLS)):
                    for k in range(HK):
                        mm = nc.tensor.matmul(out, up_w[buf][:, k, c:z], xt[buf][:, k, :], start=(k == 0), stop=(k == HK - 1))
                mm.then_inc(gated, 1)

            def down(n, buf, count):
                pe.wait_ge(down_in[buf], 32 * count)
                pe.wait_ge(hidden_made, done(n))
                pe.wait_ge(y_made, done(n, 2))
                for s in range(SUB):
                    tok = slice(s * P, (s + 1) * P)
                    nc.tensor.matmul(y_ps[buf][:, s * H:(s + 1) * H], hidden[buf][:, 0, tok], down_w[buf][:, 0, :],
                                     start=True, stop=False)
                    mm = nc.tensor.matmul(y_ps[buf][:, s * H:(s + 1) * H], hidden[buf][0:TAIL, 1, tok], down_w[buf][0:TAIL, 1, :],
                                          start=False, stop=True)
                mm.then_inc(downed, 1)

            pairs = pairs_of(pe)
            turn(0, 0, 1)
            gate_up(0, 0, 1)
            turn(1, 1, 1)
            with pe.Fori(0, pairs) as i:
                gate_up(2 * i + 1, 1, i + 1)
                turn(2 * i + 2, 0, i + 2)
                down(2 * i, 0, i + 1)
                gate_up(2 * i + 2, 0, i + 2)
                turn(2 * i + 3, 1, i + 2)
                down(2 * i + 1, 1, i + 1)
            down(2 * pairs, 0, pairs + 1)


def rope_tables():
    inv = (1.0 / 10000.0 ** (np.arange(0, HD, 2, dtype=np.float64) / HD)).astype(np.float32)
    angle = (np.arange(S, dtype=np.float32)[:, None] * inv[None, :]).astype(np.float64)
    angle = np.concatenate([angle, angle], axis=-1).T
    sin = np.sin(angle) * HD ** -0.25
    sin[HD // 2:] *= -1
    return (np.cos(angle) * HD ** -0.25).astype(np.float32), sin.astype(np.float32)


def build(nc, dram, out):
    with ExitStack() as ctx:
        resid = ctx.enter_context(nc.sbuf_tensor("resid", [P, TILES, H], F32))
        consts = {"ident": ctx.enter_context(nc.sbuf_tensor("ident", [P, P], F32)),
                  "table": ctx.enter_context(nc.sbuf_tensor("table", [1, P + 1], I32))}
        attention(nc, dram, resid, consts)
        routing(nc, dram, resid, consts)
        experts(nc, dram, resid, consts, out)


def kernel(**inputs):
    import concourse.bacc as bacc
    from concourse.bass_utils import run_bass_kernel_spmd

    def given(name):
        return np.asarray(inputs[f"L0_{name}"])

    x = given("attn_hidden_states").reshape(T, H)
    cos, sin = rope_tables()
    qkv = np.concatenate([given("attn_Wq").reshape(NKV, GROUP * HD, H), given("attn_Wk").reshape(NKV, HD, H),
                          given("attn_Wv").reshape(NKV, HD, H)], axis=1)
    shared_up = given("ffn_ws_gate_up").reshape(2, SHARED, FFN, H).transpose(1, 0, 2, 3).reshape(SHARED, 2 * FFN, H)
    up = np.concatenate([shared_up, given("ffn_w_gate_up")], axis=0)
    gap = np.zeros((E + SHARED, UP_AT - TAIL, H), up.dtype)
    up = np.concatenate([up[:, 0:P], up[:, FFN:FFN + P], up[:, P:FFN], gap, up[:, FFN + P:]], axis=1)
    shared_down = given("ffn_ws_down").reshape(H, SHARED, FFN).transpose(1, 0, 2)
    down = np.concatenate([shared_down, given("ffn_w_down")], axis=0).transpose(0, 2, 1)
    arrays = {
        "x": x,
        "xT": x.reshape(B, 2, HALF, HK, P).transpose(0, 1, 4, 3, 2),
        "cos": cos, "sin": sin,
        "w": qkv.reshape(NKV, WCOLS, HK, P).transpose(0, 3, 2, 1),
        "wo": given("attn_Wo").reshape(H, NKV, GROUP, HD).transpose(1, 3, 2, 0),
        "gate": given("ffn_gate_w").reshape(E, HK, P).transpose(2, 1, 0),
        "up": up.reshape(E + SHARED, GCOLS, HK, P).transpose(0, 3, 2, 1),
        "down": down[:, 0:P], "down_tail": down[:, P:],
    }
    arrays = {f"in_{k}": np.ascontiguousarray(v) for k, v in arrays.items()}
    nc = bacc.Bacc("TRN2", target_bir_lowering=False, num_devices=1)
    dram = {k[3:]: nc.dram_tensor(k, v.shape, F32, kind="ExternalInput").ap() for k, v in arrays.items()}
    dram["rows"] = nc.dram_tensor("rows_dram", (ROWS, ROW), F32, kind="Internal").ap()
    dram["results"] = nc.dram_tensor("results_dram", (WAYS * T, H), F32, kind="Internal").ap()
    dram["table"] = nc.dram_tensor("table_dram", (P + 1, 1), I32, kind="Internal").ap()
    dram["empty"] = dram["rows"][SHARED * T:, :].rearrange("(n p r) c -> n p r c", p=P, r=7)
    out = nc.dram_tensor("out", (B, S, H), F32, kind="ExternalOutput").ap()
    build(nc, dram, out)
    got = run_bass_kernel_spmd(nc, [arrays], core_ids=[0])
    return got.results[0]["out"]
```

```python
from contextlib import ExitStack

import numpy as np
import concourse.bass as bass
from concourse import mybir

F32 = mybir.dt.float32
F32R = mybir.dt.float32r
BF16 = mybir.dt.bfloat16
I32 = mybir.dt.int32
U32 = mybir.dt.uint32
ALU = mybir.AluOpType
ACT = mybir.ActivationFunctionType
AX = mybir.AxisListType

P = 128
B, S, H = 2, 1024, 256
T = B * S
HK = H // P
NH, NKV, HD = 16, 4, 128
GROUP = NH // NKV
HALF = S // 2
TILES = T // P
BT = S // P
WCOLS = (GROUP + 2) * HD
EPS_LN = 1e-5

E, TOPK, FFN = 64, 6, 176
SHARED = 2
WAYS = TOPK + SHARED
TAIL = FFN - P
UP_AT = 64
GCOLS = 2 * P + UP_AT + TAIL
BLK = 256
SUB = BLK // P
SHARED_BLOCKS = SHARED * T // BLK
MAX_BLOCKS = SHARED_BLOCKS + T * TOPK // BLK + E - 1
ROWS = (MAX_BLOCKS + 1) * BLK
ROW = H + 2
SKIP = 1.0e6
EPS_TOPK = 1e-20
MASKED = -1.0e30

KV_ROUND = 2
ROUNDS = B * NKV // KV_ROUND
STEPS = KV_ROUND * 2 * GROUP * 4
PAIRS = STEPS // 2
QUADS = STEPS // 4
FIRST = 7
SPLITS = 2
FILLS = {"K": [16 * i - 9 for i in range(2 * KV_ROUND)],
         "V": [16 * i - 5 for i in range(2 * KV_ROUND)],
         "Q": [4 * q - 6 for q in range(QUADS)],
         "O": [4 * (i // 2) + 8 + i % 2 for i in range(2 * QUADS)]}
ROPES = sorted([("K", i) for i in range(2 * KV_ROUND)] + [("Q", i) for i in range(QUADS)],
               key=lambda use: FILLS[use[0]][use[1]])
SPLIT_X = [-20, -4]
SPLIT_W = [-16, 16]
SPLIT_WO = [2, 34]


def key_tiles(n):
    return 4 * (n // 16 % 2) + n % 4 + 1


def chunks(n):
    return [(a, min(a + 4, key_tiles(n))) for a in range(0, key_tiles(n), 4)]


CHUNKS = sum(len(chunks(n)) for n in range(STEPS))


def chunks_before(n):
    return n // STEPS * CHUNKS + sum(len(chunks(m)) for m in range(n % STEPS))


def rope_of(kind, i):
    per = len(FILLS[kind])
    return i // per * len(ROPES) + ROPES.index((kind, i % per))


def at(positions, n):
    for shift in (-1, 0, 1):
        if n - shift * STEPS in positions:
            return positions.index(n - shift * STEPS) + shift * len(positions)
    return None


def fill_at(n):
    for kind, positions in FILLS.items():
        if at(positions, n) is not None:
            return kind, at(positions, n)
    return None


def runs(i, per, first, last):
    return i is not None and not (first and i < per) and not (last and i >= per)


def now(k, per, n):
    return (k + 1) * per + n


def run_rounds(eng, body):
    body(-1, True, False)
    with eng.Fori(0, ROUNDS - 1) as k:
        body(k, False, False)
    body(ROUNDS - 1, False, True)


def attention(nc, dram, resid, consts):
    with ExitStack() as ctx:
        def sb(name, shape, dt=F32):
            return ctx.enter_context(nc.sbuf_tensor(name, shape, dt))

        def sem(name):
            return ctx.enter_context(nc.semaphore(name))

        def pair_of(name, shape, dt):
            return [sb(f"{name}{i}", shape, dt) for i in range(2)]

        x_raw = sb("x_raw", [P, HK, HALF])
        x_hi, x_lo = sb("x_hi", [P, HK, S], F32R), sb("x_lo", [P, HK, S], F32R)
        w_raw, wo_raw = sb("w_raw", [P, HK, WCOLS]), sb("wo_raw", [P, GROUP, H])
        w_hi, w_lo = pair_of("w_hi", [P, HK, WCOLS], F32R), pair_of("w_lo", [P, HK, WCOLS], F32R)
        wo_hi, wo_lo = pair_of("wo_hi", [P, GROUP, H], F32R), pair_of("wo_lo", [P, GROUP, H], F32R)
        k_hi, k_lo = pair_of("k_hi", [P, S], F32R), pair_of("k_lo", [P, S], F32R)
        v_hi, v_lo = pair_of("v_hi", [P, BT, HD], F32R), pair_of("v_lo", [P, BT, HD], F32R)
        q_hi, q_lo = pair_of("q_hi", [P, HALF], F32R), pair_of("q_lo", [P, HALF], F32R)
        o_hi, o_lo = pair_of("o_hi", [P, HALF], F32R), pair_of("o_lo", [P, HALF], F32R)
        swapped, turn_cos = pair_of("swapped", [P, HALF], F32), pair_of("turn_cos", [P, HALF], F32)
        turned = pair_of("turned", [P, HALF], F32)
        pt_hi, pt_lo = pair_of("pt_hi", [P, BT, 2 * P], F32R), pair_of("pt_lo", [P, BT, 2 * P], F32R)
        cos, sin = sb("cos", [P, S]), sb("sin", [P, S])
        probs = sb("probs", [P, 4, S])
        neg_max, row_sum, row_inv = sb("neg_max", [P, 4]), sb("row_sum", [P, 16]), sb("row_inv", [P, 16])
        empty = sb("empty", [P, ROW])
        ident_bf, causal = sb("ident_bf", [P, P], BF16), sb("causal", [P, P], BF16)
        ident = consts["ident"]

        scores_ps = [ctx.enter_context(nc.psum_tensor(f"scores{i}", [P, S], F32)) for i in range(2)]
        pt_ps = [ctx.enter_context(nc.psum_tensor(f"pt{i}", [P, 512], F32)) for i in range(2)]
        o_ps = ctx.enter_context(nc.psum_tensor("o_ps", [P, 512], F32))
        proj_ps = ctx.enter_context(nc.psum_tensor("proj_ps", [P, 512], F32))

        tables_in, resid_in = sem("tables_in"), sem("resid_in")
        x_in, w_in, wo_in, empty_out = sem("x_in"), sem("w_in"), sem("wo_in"), sem("empty_out")
        consts_made, const_step = sem("consts_made"), sem("const_step")
        x_hi_made, x_split = sem("x_hi_made"), sem("x_split")
        w_hi_made, w_split = sem("w_hi_made"), sem("w_split")
        wo_hi_made, wo_split = sem("wo_hi_made"), sem("wo_split")
        filled = {kind: sem(f"filled_{kind}") for kind in ("rope", "V", "O")}
        swap_made, cos_made, sin_made = sem("swap_made"), sem("cos_made"), sem("sin_made")
        turn_made, turn_hi_made, turn_split = sem("turn_made"), sem("turn_hi_made"), sem("turn_split")
        v_hi_made, v_split, resid_added = sem("v_hi_made"), sem("v_split"), sem("resid_added")
        scored, max_made, exped, inv_made = sem("scored"), sem("max_made"), sem("exped"), sem("inv_made")
        transposed, pt_hi_made, pt_split = sem("transposed"), sem("pt_hi_made"), sem("pt_split")
        o_summed, o_hi_made, o_split = sem("o_summed"), sem("o_hi_made"), sem("o_split")

        block = ctx.enter_context(nc.Block())

        def per(kind):
            return len(FILLS[kind])

        def w_cols(kind, i):
            head = {"K": GROUP, "V": GROUP + 1}.get(kind, i % GROUP)
            return slice(head * HD, (head + 1) * HD)

        def half(kind, i):
            return i // GROUP % 2 if kind == "Q" else i % 2

        def kv_of(kind, i):
            return i // (2 * GROUP) % 2 if kind == "Q" else i // 2 % 2

        def turned_into(kind, i):
            if kind == "K":
                cols = slice(half(kind, i) * HALF, (half(kind, i) + 1) * HALF)
                return k_hi[kv_of(kind, i)][:, cols], k_lo[kv_of(kind, i)][:, cols]
            return q_hi[i % 2][:], q_lo[i % 2][:]

        @block.sync
        def _(sp):
            sp.dma_start(cos[:], dram["cos"]).then_inc(tables_in, 16)
            sp.dma_start(sin[:], dram["sin"]).then_inc(tables_in, 16)

            def body(k, first, last):
                def batch_of(r):
                    return r % ROUNDS // (NKV // KV_ROUND)

                def kv_at(i):
                    return (k + i // SPLITS) % (NKV // KV_ROUND) * KV_ROUND + i % SPLITS

                for n in range(FIRST, FIRST + STEPS):
                    i = at(SPLIT_X, n)
                    if runs(i, SPLITS, first, last):
                        sp.wait_ge(x_split, now(k, SPLITS, i))
                        sp.dma_start(x_raw[:], dram["xT"][bass.ds(batch_of(k + i // SPLITS), 1), i % 2]
                                     .rearrange("o p k t -> (o p) k t")).then_inc(x_in, 16)
                    i = at(SPLIT_W, n)
                    if runs(i, SPLITS, first, last):
                        sp.wait_ge(w_split, now(k, SPLITS, i))
                        sp.dma_start(w_raw[:], dram["w"][bass.ds(kv_at(i), 1)]
                                     .rearrange("o p k c -> (o p) k c")).then_inc(w_in, 16)
                    i = at(SPLIT_WO, n)
                    if runs(i, SPLITS, first, last):
                        sp.wait_ge(wo_split, now(k, SPLITS, i))
                        sp.dma_start(wo_raw[:], dram["wo"][bass.ds(kv_at(i), 1)]
                                     .rearrange("o p h c -> (o p) h c")).then_inc(wo_in, 16)
                    if first and n == FIRST + STEPS - 1:
                        sp.dma_start(resid[:], dram["x"].rearrange("(i p) c -> p i c", p=P)).then_inc(resid_in, 16)
                        sp.wait_ge(consts_made, 2)
                    if not first and n % 8 == 0:
                        sp.dma_start(dram["empty"][bass.ds(k * 8 + (n // 8 - 1), 1)].rearrange("o p r c -> (o p) r c"),
                                     empty[:].unsqueeze(1).broadcast_to([P, 7, ROW])).then_inc(empty_out, 16)

            run_rounds(sp, body)
            sp.wait_ge(empty_out, 16 * 8 * ROUNDS)
            sp.wait_ge(tables_in, 32)
            sp.wait_ge(resid_in, 16)

        @block.gpsimd
        def _(pool):
            pool.sem_inc(x_split, SPLITS)
            pool.sem_inc(w_split, SPLITS)
            pool.sem_inc(wo_split, SPLITS)
            for s in (sin_made, turn_made, turn_split):
                pool.sem_inc(s, len(ROPES))
            pool.memset(ident[:], 0.0).then_inc(const_step, 1)
            pool.memset(causal[:], 0.0).then_inc(const_step, 1)
            pool.memset(empty[:], 0.0).then_inc(const_step, 1)
            pool.wait_ge(const_step, 3)
            pool.affine_select(ident[:], ident[:], [[-1, P]], ALU.not_equal, 1.0, base=0,
                               channel_multiplier=1).then_inc(const_step, 1)
            pool.affine_select(causal[:], causal[:], [[-1, P]], ALU.is_ge, MASKED, base=0,
                               channel_multiplier=1).then_inc(const_step, 1)
            pool.memset(empty[:, H:H + 1], SKIP).then_inc(const_step, 1)
            pool.wait_ge(const_step, 6)
            pool.tensor_copy(ident_bf[:], ident[:]).then_inc(consts_made, 2)
            pool.wait_ge(tables_in, 32)

            def body(k, first, last):
                def low_part(raw, hi, lo, hi_made, split, i):
                    pool.wait_ge(hi_made, now(k, SPLITS, i + 1))
                    nc.gpsimd.tensor_tensor(lo, raw[:], hi.bitcast(F32), ALU.subtract).then_inc(split, 1)

                for n in range(FIRST, FIRST + STEPS):
                    use = fill_at(n - 3)
                    if use and use[0] in "KQ" and runs(use[1], per(use[0]), first, last):
                        r = rope_of(*use)
                        hi, lo = turned_into(*use)
                        pool.wait_ge(turn_hi_made, now(k, len(ROPES), r + 1))
                        nc.gpsimd.tensor_tensor(lo, turned[r % 2][:], hi.bitcast(F32), ALU.subtract).then_inc(turn_split, 1)
                    use = fill_at(n - 1)
                    if use and use[0] in "KQ" and runs(use[1], per(use[0]), first, last):
                        r = rope_of(*use)
                        pos = slice(half(*use) * HALF, (half(*use) + 1) * HALF)
                        pool.wait_ge(swap_made, now(k, len(ROPES), r + 1))
                        pool.wait_ge(turn_split, now(k, len(ROPES), r - 1))
                        nc.gpsimd.tensor_tensor(turned[r % 2][:], swapped[r % 2][:], sin[:, pos], ALU.mult).then_inc(sin_made, 1)
                        pool.wait_ge(cos_made, now(k, len(ROPES), r + 1))
                        pool.wait_ge(sin_made, now(k, len(ROPES), r + 1))
                        nc.gpsimd.tensor_tensor(turned[r % 2][:], turned[r % 2][:], turn_cos[r % 2][:],
                                                ALU.add).then_inc(turn_made, 1)
                    i = at(SPLIT_X, n)
                    if runs(i, SPLITS, first, last):
                        cols = slice(i % 2 * HALF, (i % 2 + 1) * HALF)
                        low_part(x_raw, x_hi[:, :, cols], x_lo[:, :, cols], x_hi_made, x_split, i)
                    i = at(SPLIT_W, n)
                    if runs(i, SPLITS, first, last):
                        low_part(w_raw, w_hi[i % 2][:], w_lo[i % 2][:], w_hi_made, w_split, i)
                    i = at(SPLIT_WO, n)
                    if runs(i, SPLITS, first, last):
                        low_part(wo_raw, wo_hi[i % 2][:], wo_lo[i % 2][:], wo_hi_made, wo_split, i)

            run_rounds(pool, body)

        @block.scalar
        def _(act):
            act.sem_inc(x_hi_made, SPLITS)
            act.sem_inc(w_hi_made, SPLITS)
            act.sem_inc(wo_hi_made, SPLITS)
            act.sem_inc(swap_made, len(ROPES))
            act.sem_inc(turn_hi_made, len(ROPES))
            act.sem_inc(v_hi_made, per("V"))
            act.sem_inc(exped, STEPS)
            act.sem_inc(pt_hi_made, CHUNKS)
            act.sem_inc(o_hi_made, PAIRS)

            def body(k, first, last):
                for n in range(FIRST, FIRST + STEPS):
                    j = (n - 6) // 2
                    if n % 2 == 0 and runs(j, PAIRS, first, last):
                        act.wait_ge(o_summed, now(k, PAIRS, j + 1))
                        act.wait_ge(filled["O"], now(k, per("O"), j - 3))
                        nc.scalar.activation(o_hi[j // 2 % 2][:, 256 * (j % 2):256 * (j % 2) + 256], o_ps[:, 0:256],
                                             ACT.Copy).then_inc(o_hi_made, 1)
                    m = n - 1
                    if runs(m, STEPS, first, last):
                        act.wait_ge(max_made, now(k, STEPS, m + 1))
                        act.wait_ge(transposed, now(k, CHUNKS, chunks_before(m - 3)))
                        act.wait_ge(inv_made, now(k, QUADS, m // 4 - 3))
                        w = key_tiles(m) * P
                        nc.scalar.activation(probs[:, m % 4, 0:w], scores_ps[m % 2][:, 0:w], ACT.Exp,
                                             bias=neg_max[:, m % 4:m % 4 + 1],
                                             accum_out=row_sum[:, m % 16:m % 16 + 1]).then_inc(exped, 1)
                    use = fill_at(n - 1)
                    if use and runs(use[1], per(use[0]), first, last):
                        kind, i = use
                        if kind in "KQ":
                            r = rope_of(*use)
                            act.wait_ge(filled["rope"], now(k, len(ROPES), r + 1))
                            act.wait_ge(sin_made, now(k, len(ROPES), r - 1))
                            nc.scalar.activation(swapped[r % 2][0:64, :], proj_ps[64:128, :], ACT.Copy)
                            nc.scalar.activation(swapped[r % 2][64:128, :], proj_ps[0:64, :],
                                                 ACT.Copy).then_inc(swap_made, 1)
                        if kind == "V":
                            act.wait_ge(filled["V"], now(k, per("V"), i + 1))
                            act.wait_ge(o_summed, now(k, PAIRS, 16 * (i // 2) + 16 - PAIRS))
                            nc.scalar.activation(v_hi[kv_of(*use)][:, 4 * (i % 2):4 * (i % 2) + 4, :], proj_ps[:],
                                                 ACT.Copy).then_inc(v_hi_made, 1)
                    m = n - 2
                    if runs(m, STEPS, first, last):
                        for i, (a, z) in enumerate(chunks(m)):
                            c = chunks_before(m) + i
                            act.wait_ge(transposed, now(k, CHUNKS, c + 1))
                            act.wait_ge(o_summed, now(k, PAIRS, m // 2 - 1))
                            nc.scalar.activation(pt_hi[m // 2 % 2][:, a:z, P * (m % 2):P * (m % 2) + P],
                                                 pt_ps[c % 2][:, 0:P * (z - a)].rearrange("p (k q) -> p k q", q=P),
                                                 ACT.Copy).then_inc(pt_hi_made, 1)
                    use = fill_at(n - 3)
                    if use and use[0] in "KQ" and runs(use[1], per(use[0]), first, last):
                        r = rope_of(*use)
                        last_reader = 32 * (use[1] // 2) + 32 - STEPS if use[0] == "K" else 4 * (use[1] - 1)
                        act.wait_ge(scored, now(k, STEPS, last_reader))
                        act.wait_ge(turn_made, now(k, len(ROPES), r + 1))
                        nc.scalar.activation(turned_into(*use)[0], turned[r % 2][:], ACT.Copy).then_inc(turn_hi_made, 1)
                    i = at(SPLIT_X, n)
                    if runs(i, SPLITS, first, last):
                        act.wait_ge(x_in, 16 * (SPLITS * k + i + 1))
                        act.wait_ge(filled["rope"], now(k, len(ROPES), rope_of("Q", 12 + 4 * (i % 2) - 1 + QUADS * (i // 2 - 1)) + 1))
                        nc.scalar.activation(x_hi[:, :, i % 2 * HALF:(i % 2 + 1) * HALF], x_raw[:], ACT.Copy).then_inc(x_hi_made, 1)
                    i = at(SPLIT_W, n)
                    if runs(i, SPLITS, first, last):
                        act.wait_ge(w_in, 16 * (SPLITS * k + i + 1))
                        act.wait_ge(filled["rope"], now(k, len(ROPES), rope_of("Q", 8 * (i % 2) + 7 + QUADS * (i // 2 - 1)) + 1))
                        nc.scalar.activation(w_hi[i % 2][:], w_raw[:], ACT.Copy).then_inc(w_hi_made, 1)
                    i = at(SPLIT_WO, n)
                    if runs(i, SPLITS, first, last):
                        act.wait_ge(wo_in, 16 * (SPLITS * k + i + 1))
                        act.wait_ge(filled["O"], now(k, per("O"), 16 * (i - SPLITS + 1)))
                        nc.scalar.activation(wo_hi[i % 2][:], wo_raw[:], ACT.Copy).then_inc(wo_hi_made, 1)

            run_rounds(act, body)

        @block.vector
        def _(dve):
            dve.sem_inc(cos_made, len(ROPES))
            dve.sem_inc(v_split, per("V"))
            dve.sem_inc(resid_added, per("O"))
            dve.sem_inc(max_made, STEPS)
            dve.sem_inc(inv_made, QUADS)
            dve.sem_inc(pt_split, CHUNKS)
            dve.sem_inc(o_split, PAIRS)
            dve.wait_ge(tables_in, 32)

            def body(k, first, last):
                for n in range(FIRST, FIRST + STEPS):
                    m = n - 3
                    if runs(m, STEPS, first, last):
                        for i, (a, z) in enumerate(chunks(m)):
                            c = chunks_before(m) + i
                            part = (slice(None), slice(a, z), slice(P * (m % 2), P * (m % 2) + P))
                            dve.wait_ge(pt_hi_made, now(k, CHUNKS, c + 1))
                            nc.vector.tensor_tensor(pt_lo[m // 2 % 2][part],
                                                    pt_ps[c % 2][:, 0:P * (z - a)].rearrange("p (k q) -> p k q", q=P),
                                                    pt_hi[m // 2 % 2][part].bitcast(F32), ALU.subtract).then_inc(pt_split, 1)
                    j = (n - 6) // 2
                    if n % 2 == 0 and runs(j, PAIRS, first, last):
                        part = (slice(None), slice(256 * (j % 2), 256 * (j % 2) + 256))
                        dve.wait_ge(o_hi_made, now(k, PAIRS, j + 1))
                        nc.vector.tensor_tensor(o_lo[j // 2 % 2][part], o_ps[:, 0:256], o_hi[j // 2 % 2][part].bitcast(F32),
                                                ALU.subtract).then_inc(o_split, 1)
                    q = (n - 5) // 4
                    if n % 4 == 1 and runs(q, QUADS, first, last):
                        dve.wait_ge(exped, now(k, STEPS, 4 * q + 4))
                        cols = slice(q % 4 * 4, q % 4 * 4 + 4)
                        nc.vector.reciprocal(row_inv[:, cols], row_sum[:, cols]).then_inc(inv_made, 1)
                    use = fill_at(n - 1)
                    if use and use[0] == "O" and runs(use[1], per("O"), first, last):
                        i = use[1] % per("O")
                        dve.wait_ge(filled["O"], now(k, per("O"), use[1] + 1))
                        dve.wait_ge(inv_made, now(k, QUADS, use[1] // 2 + 1))
                        for t in range(2):
                            tile = 4 * (i // 8 % 2) + 2 * (i % 2) + t
                            col = 4 * (i // 2 % 4) + 2 * (i % 2) + t
                            row = resid[:].rearrange("p i c -> p (i c)")[:, bass.ds(k // (NKV // KV_ROUND) * (BT * H) + tile * H, H)]
                            ins = nc.vector.scalar_tensor_tensor(out=row, in0=proj_ps[:, t * H:(t + 1) * H],
                                                                 scalar=row_inv[:, col:col + 1], in1=row,
                                                                 op0=ALU.mult, op1=ALU.add)
                        ins.then_inc(resid_added, 1)
                    if runs(n, STEPS, first, last):
                        dve.wait_ge(scored, now(k, STEPS, n + 1))
                        nc.vector.tensor_reduce(neg_max[:, n % 4:n % 4 + 1], scores_ps[n % 2][:, 0:key_tiles(n) * P],
                                                AX.X, ALU.max, negate=True).then_inc(max_made, 1)
                    if use and use[0] in "KQ" and runs(use[1], per(use[0]), first, last):
                        r = rope_of(*use)
                        pos = slice(half(*use) * HALF, (half(*use) + 1) * HALF)
                        dve.wait_ge(swap_made, now(k, len(ROPES), r + 1))
                        dve.wait_ge(turn_made, now(k, len(ROPES), r - 1))
                        nc.vector.tensor_tensor(turn_cos[r % 2][:], proj_ps[:], cos[:, pos], ALU.mult).then_inc(cos_made, 1)
                    if use and use[0] == "V" and runs(use[1], per("V"), first, last):
                        u, c = kv_of(*use), use[1] % 2
                        dve.wait_ge(v_hi_made, now(k, per("V"), use[1] + 1))
                        nc.vector.tensor_tensor(v_lo[u][:, 4 * c:4 * c + 4, :].rearrange("p t d -> p (t d)"), proj_ps[:],
                                                v_hi[u][:, 4 * c:4 * c + 4, :].rearrange("p t d -> p (t d)").bitcast(F32),
                                                ALU.subtract).then_inc(v_split, 1)
                if first:
                    dve.wait_ge(resid_in, 16)

            run_rounds(dve, body)

        @block.tensor
        def _(pe):
            pe.sem_inc(filled["rope"], len(ROPES))
            pe.sem_inc(filled["V"], per("V"))
            pe.sem_inc(filled["O"], per("O"))
            pe.sem_inc(scored, STEPS)
            pe.sem_inc(transposed, CHUNKS)
            pe.sem_inc(o_summed, PAIRS)
            pe.wait_ge(consts_made, 2)

            def products(out, left, right, first, last):
                (lh, ll), (rh, rl) = left, right
                nc.tensor.matmul(out, lh, rh, start=first, stop=False)
                nc.tensor.matmul(out, lh, rl, start=False, stop=False)
                return nc.tensor.matmul(out, ll, rh, start=False, stop=last)

            def body(k, first, last):
                def bank_free(n):
                    for before in range(n - 1, 0, -1):
                        use = fill_at(before)
                        if use and (before < FIRST or runs(use[1], per(use[0]), first, last)):
                            break
                    else:
                        return
                    if use[0] == "O":
                        pe.wait_ge(resid_added, now(k, per("O"), use[1] + 1))
                    elif use[0] == "V":
                        pe.wait_ge(v_split, now(k, per("V"), use[1] + 1))
                    else:
                        pe.wait_ge(cos_made, now(k, len(ROPES), rope_of(*use) + 1))

                def fill(n, kind, i):
                    bank_free(n)
                    u = kv_of(kind, i)
                    if kind == "O":
                        q, a = i // 2, i % 2
                        u, head = q // 8 % 2, q % GROUP
                        pe.wait_ge(o_split, now(k, PAIRS, i + 1))
                        if q % 8 == 0 and a == 0:
                            pe.wait_ge(wo_split, now(k, SPLITS, q // 8 + 1))
                        for t in range(2):
                            tok = slice((a * 2 + t) * P, (a * 2 + t + 1) * P)
                            mm = products(proj_ps[:, t * H:(t + 1) * H], (o_hi[q % 2][:, tok], o_lo[q % 2][:, tok]),
                                          (wo_hi[u][:, head, :], wo_lo[u][:, head, :]), True, True)
                        mm.then_inc(filled["O"], 1)
                        return
                    if kind == "K":
                        if i % 2 == 0:
                            pe.wait_ge(w_split, now(k, SPLITS, i // 2 + 1))
                        if i % per("K") < 2:
                            pe.wait_ge(x_split, now(k, SPLITS, i // per("K") * SPLITS + i % 2 + 1))
                    if kind == "V":
                        for t in range(4):
                            tok = slice((4 * half(kind, i) + t) * P, (4 * half(kind, i) + t + 1) * P)
                            for c in range(HK):
                                mm = products(proj_ps[:, t * HD:(t + 1) * HD], (x_hi[:, c, tok], x_lo[:, c, tok]),
                                              (w_hi[u][:, c, w_cols(kind, i)], w_lo[u][:, c, w_cols(kind, i)]), c == 0, c == HK - 1)
                        mm.then_inc(filled["V"], 1)
                        return
                    tok = slice(half(kind, i) * HALF, (half(kind, i) + 1) * HALF)
                    for c in range(HK):
                        mm = products(proj_ps[:], (w_hi[u][:, c, w_cols(kind, i)], w_lo[u][:, c, w_cols(kind, i)]),
                                      (x_hi[:, c, tok], x_lo[:, c, tok]), c == 0, c == HK - 1)
                    mm.then_inc(filled["rope"], 1)

                for n in range(FIRST, FIRST + STEPS):
                    if runs(n, STEPS, first, last):
                        if n % 4 == 0:
                            pe.wait_ge(turn_split, now(k, len(ROPES), rope_of("Q", n // 4) + 1))
                        pe.wait_ge(exped, now(k, STEPS, n - 1))
                        u, b = n // 32 % 2, n // 4 % 2
                        qt = (slice(None), slice(P * (n % 4), P * (n % 4) + P))
                        for a, z in chunks(n):
                            keys = slice(a * P, z * P)
                            out = scores_ps[n % 2][:, keys]
                            nc.tensor.matmul(out, q_hi[b][qt], k_hi[u][:, keys], start=True, stop=False)
                            nc.tensor.matmul(out, q_hi[b][qt], k_lo[u][:, keys], start=False, stop=False)
                            if z == key_tiles(n):
                                nc.tensor.matmul(scores_ps[n % 2][:, (z - 1) * P:z * P], ident_bf[:], causal[:],
                                                 start=False, stop=False)
                            mm = nc.tensor.matmul(out, q_lo[b][qt], k_hi[u][:, keys], start=False, stop=True)
                        mm.then_inc(scored, 1)
                    m = n - 2
                    if runs(m, STEPS, first, last):
                        pe.wait_ge(exped, now(k, STEPS, m + 1))
                        for i, (a, z) in enumerate(chunks(m)):
                            c = chunks_before(m) + i
                            pe.wait_ge(pt_split, now(k, CHUNKS, c - 1))
                            for t in range(a, z):
                                mm = nc.tensor.transpose(pt_ps[c % 2][:, (t - a) * P:(t - a + 1) * P],
                                                         probs[:, m % 4, t * P:(t + 1) * P], ident[:])
                            mm.then_inc(transposed, 1)
                    j = (n - 4) // 2
                    if runs(j, PAIRS, first, last):
                        u, count = j // 16 % 2, key_tiles(2 * j + 1)
                        if n % 2 == 0:
                            if j % 8 == 0:
                                pe.wait_ge(v_split, now(k, per("V"), j // 8 + 1))
                            pe.wait_ge(pt_split, now(k, CHUNKS, chunks_before(2 * j + 2)))
                            pe.wait_ge(o_split, now(k, PAIRS, j))
                        for t in (range(count // 2) if n % 2 == 0 else range(count // 2, count)):
                            q0 = P if t == count - 1 else 0
                            qs = slice(q0, 2 * P)
                            mm = products(o_ps[:, qs], (v_hi[u][:, t, :], v_lo[u][:, t, :]),
                                          (pt_hi[j % 2][:, t, qs], pt_lo[j % 2][:, t, qs]), t == 0, t == count - 1)
                        if n % 2 == 1:
                            mm.then_inc(o_summed, 1)
                    use = fill_at(n)
                    if use and runs(use[1], per(use[0]), first, last):
                        fill(n, *use)

            run_rounds(pe, body)


def routing(nc, dram, resid, consts):
    with ExitStack() as ctx:
        def sb(name, shape, dt=F32):
            return ctx.enter_context(nc.sbuf_tensor(name, shape, dt))

        def sem(name):
            return ctx.enter_context(nc.semaphore(name))

        ident = consts["ident"]
        stats, moments = sb("stats", [P, TILES, 6]), sb("moments", [P, TILES, 2])
        deviation, inv_dev = sb("deviation", [P, TILES]), sb("inv_dev", [P, TILES])
        xt = sb("xt", [P, 2, HK, P])
        gate = sb("gate", [P, HK, E])
        logits = sb("logits", [P, TILES, E])
        top, top_at = sb("top", [P, TILES, 8]), sb("top_at", [P, TILES, 8], U32)
        top_id = sb("top_id", [P, TILES, 8])
        shifted, exp_all = sb("shifted", [P, TILES, E]), sb("exp_all", [P, TILES, E])
        exp_top = sb("exp_top", [P, TILES, TOPK])
        sum_all, sum_top = sb("sum_all", [P, TILES]), sb("sum_top", [P, TILES])
        expert_ids = sb("expert_ids", [P, E])
        chosen = sb("chosen", [P, TOPK, TILES, E], BF16)
        mask = sb("mask", [P, 2, TILES, E], BF16)
        before, ones = sb("before", [P, P], BF16), sb("ones", [P, P], BF16)
        counts, counts_int = sb("counts", [P, E]), sb("counts_int", [P, E], I32)
        blocks, blocks_to, first_row = sb("blocks", [P, E]), sb("blocks_to", [P, E]), sb("first_row", [P, E])
        one_row = sb("one_row", [P, E])
        slot_of = sb("slot_of", [P, TILES, E])
        product = sb("product", [P, TILES, E])
        slots, slots_int = sb("slots", [P, TILES, TOPK]), sb("slots_int", [P, TILES, TOPK], I32)
        goes_with = sb("goes_with", [P, TILES, WAYS, 2])
        rows = sb("rows", [P, 2, WAYS, ROW])
        block_id = sb("block_id", [P, 1])
        started, owner, owner_int = sb("started", [P, E]), sb("owner", [P, 2]), sb("owner_int", [P, 1], I32)
        pairs, pairs_int = sb("pairs", [P, 1]), sb("pairs_int", [P, 1], I32)

        logits_ps = ctx.enter_context(nc.psum_tensor("logits_ps", [P, TILES * E], F32))
        places_ps = ctx.enter_context(nc.psum_tensor("places_ps", [P, TILES * E], F32))
        xt_ps = [ctx.enter_context(nc.psum_tensor(f"xt_ps{i}", [P, 512], F32)) for i in range(2)]
        counts_ps = ctx.enter_context(nc.psum_tensor("counts_ps", [P, 512], F32))

        gate_in, table_out, table_in = sem("gate_in"), sem("table_out"), sem("table_in")
        consts_set, const_step, iotas = sem("consts_set"), sem("const_step"), sem("iotas")
        dve_step = sem("dve_step")
        moments_made, deviation_made, normed = sem("moments_made"), sem("deviation_made"), sem("normed")
        xt_turned, xt_made, logits_made = sem("xt_turned"), sem("xt_made"), sem("logits_made")
        shifted_made, exps_made = sem("shifted_made"), sem("exps_made")
        mask_made, places_made = sem("mask_made"), sem("places_made")
        slots_made, weights_made, table_made = sem("slots_made"), sem("weights_made"), sem("table_made")
        rows_filled, rows_ready = sem("rows_filled"), sem("rows_ready")
        sent = [sem(f"sent{i}") for i in range(2)]
        shared_sent = [sem(f"shared_sent{i}") for i in range(2)]

        block = ctx.enter_context(nc.Block())
        shared_rows = dram["rows"][0:SHARED * T, :].rearrange("(s i p) c -> i s p c", s=SHARED, p=P)

        @block.sync
        def _(sp):
            sp.dma_start(gate[:], dram["gate"]).then_inc(gate_in, 16)
            sp.wait_ge(table_made, 1)
            sp.dma_start(dram["table"][0:P, :], owner_int[:]).then_inc(table_out, 16)
            sp.dma_start(dram["table"][P:P + 1, :], pairs_int[0:1, :]).then_inc(table_out, 16)
            sp.wait_ge(table_out, 32)
            sp.dma_start(consts["table"][:], dram["table"].rearrange("r c -> c r")).then_inc(table_in, 16)
            for i in range(TILES):
                sp.wait_ge(rows_ready, i + 1)
                for s in range(SHARED):
                    sp.dma_start(shared_rows[i, s], rows[:, i % 2, TOPK + s, :]).then_inc(shared_sent[i % 2], 16)
            sp.wait_ge(table_in, 16)
            for i in range(2):
                sp.wait_ge(shared_sent[i], 16 * SHARED * TILES // 2)

        @block.gpsimd
        def _(pool):
            pool.memset(before[:], 1.0).then_inc(const_step, 1)
            pool.memset(ones[:], 1.0).then_inc(const_step, 1)
            pool.memset(one_row[:], 1.0).then_inc(const_step, 1)
            pool.memset(goes_with[:], 1.0).then_inc(const_step, 1)
            pool.iota(expert_ids[:], [[1, E]], base=0, channel_multiplier=0,
                      allow_small_or_imprecise_dtypes=True).then_inc(const_step, 1)
            pool.iota(block_id[:], [[0, 1]], base=0, channel_multiplier=1,
                      allow_small_or_imprecise_dtypes=True).then_inc(const_step, 1)
            pool.wait_ge(const_step, 6)
            pool.affine_select(before[:], before[:], [[1, P]], ALU.is_gt, 0.0, base=0,
                               channel_multiplier=-1).then_inc(const_step, 1)
            pool.iota(goes_with[:, :, :, 0], [[P, TILES], [T, WAYS]], base=0, channel_multiplier=1,
                      allow_small_or_imprecise_dtypes=True).then_inc(const_step, 1)
            pool.wait_ge(const_step, 8)
            pool.sem_inc(consts_set, 1)
            pool.wait_ge(slots_made, 1)
            for i in range(TILES):
                pool.wait_ge(rows_ready, i + 1)
                for j in range(TOPK):
                    pool.indirect_dma_start(
                        out=dram["rows"], out_offset=bass.IndirectOffsetOnAxis(ap=slots_int[:, i, j:j + 1], axis=0),
                        in_=rows[:, i % 2, j, :], in_offset=None, bounds_check=ROWS - 1,
                        oob_is_err=False).then_inc(sent[i % 2], 16)
            for i in range(2):
                pool.wait_ge(sent[i], 16 * TOPK * TILES // 2)

        @block.scalar
        def _(act):
            act.wait_ge(moments_made, 1)
            act.activation(deviation[:], deviation[:], ACT.Sqrt).then_inc(deviation_made, 1)
            for i in range(TILES):
                act.wait_ge(xt_turned, i + 1)
                if i >= 2:
                    act.wait_ge(logits_made, i - 1)
                act.activation(xt[:, i % 2].rearrange("p k t -> p (k t)"), xt_ps[i % 2][:, 0:H], ACT.Copy).then_inc(xt_made, 1)
            act.wait_ge(shifted_made, 1)
            act.activation(exp_all[:], shifted[:], ACT.Exp).then_inc(exps_made, 1)
            act.activation(exp_top[:], exp_top[:], ACT.Exp).then_inc(exps_made, 1)
            for i in range(TILES):
                if i >= 2:
                    act.wait_ge(sent[i % 2], 16 * TOPK * (i // 2))
                    act.wait_ge(shared_sent[i % 2], 16 * SHARED * (i // 2))
                act.activation(rows[:, i % 2, :, 0:H], resid[:, i, :].unsqueeze(1).broadcast_to([P, WAYS, H]),
                               ACT.Copy).then_inc(rows_filled, 1)

        @block.vector
        def _(dve):
            steps = [0]

            def then(ins):
                steps[0] += 1
                ins.then_inc(dve_step, 1)
                dve.wait_ge(dve_step, steps[0])

            for i in range(TILES):
                ins = dve.bn_stats(stats[:, i, :], resid[:, i, :])
            then(ins)
            for i in range(TILES):
                ins = dve.bn_aggr(moments[:, i, :], stats[:, i, :])
            then(ins)
            dve.tensor_scalar(deviation[:], moments[:, :, 1], EPS_LN, None, ALU.add).then_inc(moments_made, 1)
            dve.wait_ge(deviation_made, 1)
            then(dve.reciprocal(inv_dev[:], deviation[:]))
            for i in range(TILES):
                dve.tensor_scalar(resid[:, i, :], resid[:, i, :], moments[:, i, 0:1], inv_dev[:, i:i + 1],
                                  ALU.subtract, ALU.mult).then_inc(normed, 1)
            dve.wait_ge(consts_set, 1)
            dve.wait_ge(logits_made, TILES)
            then(dve.tensor_copy(logits[:].rearrange("p i e -> p (i e)"), logits_ps[:]))
            for i in range(TILES):
                ins = dve.max(top[:, i, :], logits[:, i, :])
            then(ins)
            for i in range(TILES):
                ins = dve.max_index(top_at[:, i, :], top[:, i, :], logits[:, i, :])
            dve.tensor_tensor(shifted[:], logits[:], top[:, :, 0:1].broadcast_to([P, TILES, E]), ALU.subtract)
            dve.tensor_tensor(exp_top[:], top[:, :, 0:TOPK], top[:, :, 0:1].broadcast_to([P, TILES, TOPK]),
                              ALU.subtract).then_inc(shifted_made, 1)
            dve.wait_ge(shifted_made, 1)
            then(dve.tensor_copy(top_id[:], top_at[:]))
            for j in range(TOPK):
                ins = dve.tensor_tensor(chosen[:, j], expert_ids[:].unsqueeze(1).broadcast_to([P, TILES, E]),
                                        top_id[:, :, j:j + 1].broadcast_to([P, TILES, E]), ALU.is_equal)
            then(ins)
            then(dve.tensor_tensor(mask[:, 1], chosen[:, 0], chosen[:, 1], ALU.add))
            for j in range(2, TOPK):
                ins = dve.tensor_tensor(mask[:, j % 2], mask[:, (j - 1) % 2], chosen[:, j], ALU.add)
                then(ins)
            dve.sem_inc(mask_made, 1)
            dve.wait_ge(places_made, 1)
            then(dve.tensor_scalar(counts[:], counts_ps[:, 0:E], float(BLK - 1), None, ALU.add))
            then(dve.tensor_copy(counts_int[:], counts[:]))
            then(dve.tensor_scalar(counts_int[:], counts_int[:], BLK.bit_length() - 1, None, ALU.logical_shift_right))
            then(dve.tensor_copy(blocks[:], counts_int[:]))
            then(dve.tensor_tensor_scan(blocks_to[:], one_row[:], blocks[:], float(SHARED_BLOCKS), ALU.mult, ALU.add))
            then(dve.tensor_tensor(started[:], blocks_to[:], blocks[:], ALU.subtract))
            then(dve.tensor_scalar(first_row[:], started[:], float(BLK), None, ALU.mult))
            dve.wait_ge(places_made, 2)
            then(dve.tensor_tensor(slot_of[:], places_ps[:].rearrange("p (i e) -> p i e", e=E),
                                   first_row[:].unsqueeze(1).broadcast_to([P, TILES, E]), ALU.add))
            for j in range(TOPK):
                then(dve.tensor_tensor(product[:], chosen[:, j], slot_of[:], ALU.mult))
                then(dve.tensor_reduce(slots[:, :, j], product[:], AX.X, ALU.add))
            dve.tensor_copy(slots_int[:], slots[:]).then_inc(slots_made, 1)
            dve.wait_ge(exps_made, 2)
            dve.tensor_reduce(sum_all[:], exp_all[:], AX.X, ALU.add)
            then(dve.tensor_reduce(sum_top[:], exp_top[:], AX.X, ALU.add))
            then(dve.scalar_tensor_tensor(out=sum_top[:], in0=sum_all[:], scalar=EPS_TOPK, in1=sum_top[:],
                                          op0=ALU.mult, op1=ALU.add))
            then(dve.reciprocal(sum_top[:], sum_top[:]))
            then(dve.tensor_tensor(goes_with[:, :, 0:TOPK, 1], exp_top[:],
                                   sum_top[:].unsqueeze(2).broadcast_to([P, TILES, TOPK]), ALU.mult))
            for i in range(TILES):
                dve.wait_ge(rows_filled, i + 1)
                dve.tensor_copy(rows[:, i % 2, :, H:ROW], goes_with[:, i]).then_inc(rows_ready, 1)
                if i == 0:
                    then(dve.tensor_scalar(started[:], started[:], block_id[:], None, ALU.is_le))
                    then(dve.tensor_reduce(owner[:, 0:1], started[:], AX.X, ALU.add))
                    then(dve.tensor_scalar(owner[:, 1:2], block_id[:], float(SHARED_BLOCKS // SHARED), None, ALU.is_ge))
                    then(dve.tensor_tensor(owner[:, 0:1], owner[:, 0:1], owner[:, 1:2], ALU.add))
                    then(dve.tensor_copy(owner_int[:], owner[:, 0:1]))
                    then(dve.tensor_copy(pairs_int[:], blocks_to[:, E - 1:E]))
                    dve.tensor_scalar(pairs_int[:], pairs_int[:], 1, None,
                                      ALU.logical_shift_right).then_inc(table_made, 1)

        @block.tensor
        def _(pe):
            pe.wait_ge(gate_in, 16)

            def turn(i):
                pe.wait_ge(normed, i + 1)
                if i >= 2:
                    pe.wait_ge(xt_made, i - 1)
                for k in range(HK):
                    mm = nc.tensor.transpose(xt_ps[i % 2][:, k * P:(k + 1) * P], resid[:, i, k * P:(k + 1) * P], ident[:])
                mm.then_inc(xt_turned, 1)

            turn(0)
            for i in range(TILES):
                if i + 1 < TILES:
                    turn(i + 1)
                pe.wait_ge(xt_made, i + 1)
                for k in range(HK):
                    mm = nc.tensor.matmul(logits_ps[:, i * E:(i + 1) * E], xt[:, i % 2, k, :], gate[:, k, :],
                                          start=(k == 0), stop=(k == HK - 1))
                mm.then_inc(logits_made, 1)
            pe.wait_ge(mask_made, 1)
            pe.wait_ge(consts_set, 1)
            picks = mask[:, (TOPK - 1) % 2]
            for i in range(TILES):
                mm = nc.tensor.matmul(counts_ps[:, 0:E], ones[:], picks[:, i, :], start=(i == 0), stop=(i == TILES - 1))
            mm.then_inc(places_made, 1)
            for i in range(TILES):
                out = places_ps[:, i * E:(i + 1) * E]
                mm = nc.tensor.matmul(out, before[:], picks[:, i, :], start=True, stop=(i == 0))
                for k in range(i):
                    mm = nc.tensor.matmul(out, ones[:], picks[:, k, :], start=False, stop=(k == i - 1))
            mm.then_inc(places_made, 1)


def done(n, back=0):
    return n + 3 - back


def experts(nc, dram, resid, consts, out):
    with ExitStack() as ctx:
        def sb(name, shape, dt=F32):
            return ctx.enter_context(nc.sbuf_tensor(name, shape, dt))

        def sem(name):
            return ctx.enter_context(nc.semaphore(name))

        def both(name):
            return [sem(f"{name}{i}") for i in range(2)]

        ident, table = consts["ident"], consts["table"]
        up_w = [sb(f"up_w{i}", [P, HK, GCOLS]) for i in range(2)]
        down_w = [sb(f"down_w{i}", [P, 2, H]) for i in range(2)]
        x_in = [sb(f"x_in{i}", [P, SUB, ROW]) for i in range(2)]
        xt = [sb(f"xt{i}", [P, HK, BLK]) for i in range(2)]
        silu = [sb(f"silu{i}", [P, 2, BLK]) for i in range(2)]
        hidden = [sb(f"hidden{i}", [P, 2, BLK]) for i in range(2)]
        y_sb = [sb(f"y_sb{i}", [P, SUB, H]) for i in range(2)]
        dest = [sb(f"dest{i}", [P, SUB], I32) for i in range(2)]
        goes_with = sb("goes_with_all", [P, MAX_BLOCKS + 1, SUB, 2])
        RING = 4
        parts = [sb(f"parts{i}", [P, WAYS, H]) for i in range(RING)]
        total = sb("total", [P, 2, H])
        stats, moments = sb("stats2", [P, TILES, 6]), sb("moments2", [P, TILES, 2])
        deviation, inv_dev = sb("deviation2", [P, TILES]), sb("inv_dev2", [P, TILES])

        xt_ps = ctx.enter_context(nc.psum_tensor("x_ps", [P, 512], F32))
        gate_up_ps = [ctx.enter_context(nc.psum_tensor(f"gate_up{i}", [P, 512], F32)) for i in range(2)]
        tail_ps = [ctx.enter_context(nc.psum_tensor(f"tail{i}", [P, 512], F32)) for i in range(2)]
        y_ps = [ctx.enter_context(nc.psum_tensor(f"y{i}", [P, 512], F32)) for i in range(2)]

        up_in, down_in, rows_in, y_out = both("up_in"), both("down_in"), both("rows_in"), both("y_out")
        x_turned, xt_made, goes_made = sem("x_turned"), sem("xt_made"), sem("goes_made")
        gated, silu_made, hidden_made = sem("gated"), sem("silu_made"), sem("hidden_made")
        downed, y_made, y_sent = sem("downed"), sem("y_made"), sem("y_sent")
        send_begun, all_sent = sem("send_begun"), sem("all_sent")
        parts_in = [sem(f"parts_in{i}") for i in range(RING)]
        parts_used, dve_step = sem("parts_used"), sem("dve_step2")
        variance_made, deviation_made, normed, out_done = sem("variance_made"), sem("deviation_made"), sem("normed2"), sem("out_done")

        block = ctx.enter_context(nc.Block())
        row_blocks = dram["rows"].rearrange("(n p s) c -> n p s c", p=P, s=SUB)
        results = dram["results"].rearrange("(j i p) c -> i p j c", j=WAYS, p=P)
        out_tiles = out.rearrange("b (i p) c -> (b i) p c", p=P)

        def pairs_of(eng):
            return eng.value_load(table[0:1, P:P + 1], min_val=SHARED_BLOCKS // 2, max_val=MAX_BLOCKS // 2)

        @block.sync
        def _(sp):
            def load_rows(n, buf, count):
                sp.wait_ge(x_turned, done(n, 2))
                sp.wait_ge(goes_made, done(n, 2))
                sp.dma_start(x_in[buf][:], row_blocks[bass.ds(n, 1)].rearrange("o p s c -> (o p) s c")).then_inc(rows_in[buf], 16)

            def load_weights(n, buf):
                e = sp.value_load(table[0:1, bass.ds(n, 1)], min_val=0, max_val=E + SHARED - 1)
                sp.wait_ge(gated, done(n, 2))
                sp.dma_start(up_w[buf][:], dram["up"][bass.ds(e, 1)].rearrange("o p k c -> (o p) k c")).then_inc(up_in[buf], 16)
                sp.wait_ge(downed, done(n, 2))
                sp.dma_start(down_w[buf][:, 0, :], dram["down"][bass.ds(e, 1)].rearrange("o p c -> (o p) c")).then_inc(down_in[buf], 16)
                sp.dma_start(down_w[buf][0:TAIL, 1, :], dram["down_tail"][bass.ds(e, 1)].rearrange("o p c -> (o p) c")).then_inc(down_in[buf], 16)

            pairs = pairs_of(sp)
            load_rows(0, 0, 0)
            load_weights(0, 0)
            load_rows(1, 1, 0)
            with sp.Fori(0, pairs) as i:
                for u in range(2):
                    n = 2 * i + (1 + u)
                    load_weights(n, (1 + u) % 2)
                    load_rows(n + 1, u, 0)
            sp.wait_ge(all_sent, 1)
            for t in range(TILES):
                if t >= RING:
                    sp.wait_ge(parts_used, t - RING + 1)
                sp.dma_start(parts[t % RING][:], results[t]).then_inc(parts_in[t % RING], 16)
            for t in range(TILES):
                sp.wait_ge(normed, t + 1)
                sp.dma_start(out_tiles[t], resid[:, t, :]).then_inc(out_done, 16)
            sp.wait_ge(out_done, 16 * TILES)

        @block.gpsimd
        def _(pool):
            pool.sem_inc(y_sent, 2)
            last_row = pool.to_reg(WAYS * T - 1)

            def send(n, buf):
                pool.wait_ge(y_made, done(n))
                pool.sem_inc(send_begun, 1)
                for s in range(SUB):
                    pool.indirect_dma_start(
                        out=dram["results"], out_offset=bass.IndirectOffsetOnAxis(ap=dest[buf][:, s:s + 1], axis=0),
                        in_=y_sb[buf][:, s, :], in_offset=None, bounds_check=last_row,
                        oob_is_err=False).then_inc(y_out[buf], 16)

            def sent(buf, count):
                pool.wait_ge(y_out[buf], 16 * SUB * count)
                pool.sem_inc(y_sent, 1)

            pairs = pairs_of(pool)
            send(0, 0)
            with pool.Fori(0, pairs) as i:
                sent(0, i + 1)
                send(2 * i + 1, 1)
                sent(1, i + 1)
                send(2 * i + 2, 0)
            sent(0, pairs + 1)
            pool.sem_inc(all_sent, 1)

        @block.scalar
        def _(act):
            act.sem_inc(xt_made, 2)
            act.sem_inc(silu_made, 2)

            def turned(n, buf):
                act.wait_ge(x_turned, done(n))
                act.wait_ge(gated, done(n, 2))
                nc.scalar.activation(xt[buf][:].rearrange("p k t -> p (k t)"), xt_ps[:], ACT.Copy).then_inc(xt_made, 1)

            def gate(n, buf):
                act.wait_ge(gated, done(n))
                act.wait_ge(hidden_made, done(n, 2))
                nc.scalar.activation(silu[buf][:, 0, :], gate_up_ps[buf][:, 0:BLK], ACT.Silu)
                nc.scalar.activation(silu[buf][0:TAIL, 1, :], tail_ps[buf][0:TAIL, 0:BLK], ACT.Silu).then_inc(silu_made, 1)

            pairs = pairs_of(act)
            turned(0, 0)
            gate(0, 0)
            turned(1, 1)
            with act.Fori(0, pairs) as i:
                for u in range(2):
                    n = 2 * i + (1 + u)
                    gate(n, (1 + u) % 2)
                    turned(n + 1, u)
            act.wait_ge(variance_made, 1)
            nc.scalar.activation(deviation[:], deviation[:], ACT.Sqrt).then_inc(deviation_made, 1)

        @block.vector
        def _(dve):
            dve.sem_inc(goes_made, 2)
            dve.sem_inc(hidden_made, 2)
            dve.sem_inc(y_made, 2)

            def note(n, buf, count):
                dve.wait_ge(rows_in[buf], 16 * count)
                dve.tensor_copy(goes_with[:, bass.ds(n, 1)].rearrange("p o s c -> p (o s) c"), x_in[buf][:, :, H:ROW]).then_inc(goes_made, 1)

            def hide(n, buf):
                dve.wait_ge(silu_made, done(n))
                dve.wait_ge(downed, done(n, 2))
                dve.tensor_tensor(hidden[buf][:, 0, :], silu[buf][:, 0, :], gate_up_ps[buf][:, BLK:2 * BLK], ALU.mult)
                dve.tensor_tensor(hidden[buf][0:TAIL, 1, :], silu[buf][0:TAIL, 1, :], tail_ps[buf][UP_AT:UP_AT + TAIL, 0:BLK],
                                  ALU.mult).then_inc(hidden_made, 1)

            def weigh(n, buf):
                dve.wait_ge(downed, done(n))
                dve.wait_ge(y_sent, done(n, 2))
                dve.wait_ge(goes_made, done(n))
                dve.tensor_copy(dest[buf][:], goes_with[:, bass.ds(n, 1), :, 0].rearrange("p o s -> p (o s)"))
                for s in range(SUB):
                    ins = dve.tensor_tensor(y_sb[buf][:, s, :], y_ps[buf][:, s * H:(s + 1) * H],
                                            goes_with[:, bass.ds(n, 1), s, 1].broadcast_to([P, H]), ALU.mult)
                ins.then_inc(y_made, 1)

            pairs = pairs_of(dve)
            note(0, 0, 1)
            hide(0, 0)
            note(1, 1, 1)
            with dve.Fori(0, pairs) as i:
                hide(2 * i + 1, 1)
                note(2 * i + 2, 0, i + 2)
                weigh(2 * i, 0)
                hide(2 * i + 2, 0)
                note(2 * i + 3, 1, i + 2)
                weigh(2 * i + 1, 1)
            weigh(2 * pairs, 0)

            steps = [0]

            def then(ins):
                steps[0] += 1
                ins.then_inc(dve_step, 1)
                dve.wait_ge(dve_step, steps[0])

            for t in range(TILES):
                dve.wait_ge(parts_in[t % RING], 16 * (t // RING + 1))
                ins = dve.tensor_reduce(total[:, t % 2, :], parts[t % RING][:].rearrange("p j c -> p c j"), AX.X, ALU.add)
                ins.then_inc(parts_used, 1)
                dve.wait_ge(parts_used, t + 1)
                then(dve.tensor_tensor(resid[:, t, :], resid[:, t, :], total[:, t % 2, :], ALU.add))
                then(dve.bn_stats(stats[:, t, :], resid[:, t, :]))
                then(dve.bn_aggr(moments[:, t, :], stats[:, t, :]))
            dve.tensor_scalar(deviation[:], moments[:, :, 1], EPS_LN, None, ALU.add).then_inc(variance_made, 1)
            dve.wait_ge(deviation_made, 1)
            then(dve.reciprocal(inv_dev[:], deviation[:]))
            for t in range(TILES):
                dve.tensor_scalar(resid[:, t, :], resid[:, t, :], moments[:, t, 0:1], inv_dev[:, t:t + 1],
                                  ALU.subtract, ALU.mult).then_inc(normed, 1)

        @block.tensor
        def _(pe):
            pe.sem_inc(x_turned, 2)
            pe.sem_inc(gated, 2)
            pe.sem_inc(downed, 2)

            def turn(n, buf, count):
                pe.wait_ge(rows_in[buf], 16 * count)
                pe.wait_ge(xt_made, done(n, 1))
                for k in range(HK):
                    for s in range(SUB):
                        mm = nc.tensor.transpose(xt_ps[:, k * BLK + s * P:k * BLK + (s + 1) * P],
                                                 x_in[buf][:, s, k * P:(k + 1) * P], ident[:])
                mm.then_inc(x_turned, 1)

            def gate_up(n, buf, count):
                pe.wait_ge(up_in[buf], 16 * count)
                pe.wait_ge(xt_made, done(n))
                pe.wait_ge(hidden_made, done(n, 2))
                for out, c, z in ((gate_up_ps[buf][:, 0:BLK], 0, P), (gate_up_ps[buf][:, BLK:2 * BLK], P, 2 * P),
                                  (tail_ps[buf][0:GCOLS - 2 * P, 0:BLK], 2 * P, GCOLS)):
                    for k in range(HK):
                        mm = nc.tensor.matmul(out, up_w[buf][:, k, c:z], xt[buf][:, k, :], start=(k == 0), stop=(k == HK - 1))
                mm.then_inc(gated, 1)

            def down(n, buf, count):
                pe.wait_ge(down_in[buf], 32 * count)
                pe.wait_ge(hidden_made, done(n))
                pe.wait_ge(y_made, done(n, 2))
                for s in range(SUB):
                    tok = slice(s * P, (s + 1) * P)
                    nc.tensor.matmul(y_ps[buf][:, s * H:(s + 1) * H], hidden[buf][:, 0, tok], down_w[buf][:, 0, :],
                                     start=True, stop=False)
                    mm = nc.tensor.matmul(y_ps[buf][:, s * H:(s + 1) * H], hidden[buf][0:TAIL, 1, tok], down_w[buf][0:TAIL, 1, :],
                                          start=False, stop=True)
                mm.then_inc(downed, 1)

            pairs = pairs_of(pe)
            turn(0, 0, 1)
            gate_up(0, 0, 1)
            turn(1, 1, 1)
            with pe.Fori(0, pairs) as i:
                gate_up(2 * i + 1, 1, i + 1)
                turn(2 * i + 2, 0, i + 2)
                down(2 * i, 0, i + 1)
                gate_up(2 * i + 2, 0, i + 2)
                turn(2 * i + 3, 1, i + 2)
                down(2 * i + 1, 1, i + 1)
            down(2 * pairs, 0, pairs + 1)


def rope_tables():
    inv = (1.0 / 10000.0 ** (np.arange(0, HD, 2, dtype=np.float64) / HD)).astype(np.float32)
    angle = (np.arange(S, dtype=np.float32)[:, None] * inv[None, :]).astype(np.float64)
    angle = np.concatenate([angle, angle], axis=-1).T
    sin = np.sin(angle) * HD ** -0.25
    sin[:HD // 2] *= -1
    return (np.cos(angle) * HD ** -0.25).astype(np.float32), sin.astype(np.float32)


def build(nc, dram, out):
    with ExitStack() as ctx:
        resid = ctx.enter_context(nc.sbuf_tensor("resid", [P, TILES, H], F32))
        consts = {"ident": ctx.enter_context(nc.sbuf_tensor("ident", [P, P], F32)),
                  "table": ctx.enter_context(nc.sbuf_tensor("table", [1, P + 1], I32))}
        attention(nc, dram, resid, consts)
        routing(nc, dram, resid, consts)
        experts(nc, dram, resid, consts, out)


def kernel(**inputs):
    import concourse.bacc as bacc
    from concourse.bass_utils import run_bass_kernel_spmd

    def given(name):
        return np.asarray(inputs[f"L0_{name}"])

    x = given("attn_hidden_states").reshape(T, H)
    cos, sin = rope_tables()
    qkv = np.concatenate([given("attn_Wq").reshape(NKV, GROUP * HD, H), given("attn_Wk").reshape(NKV, HD, H),
                          given("attn_Wv").reshape(NKV, HD, H)], axis=1)
    shared_up = given("ffn_ws_gate_up").reshape(2, SHARED, FFN, H).transpose(1, 0, 2, 3).reshape(SHARED, 2 * FFN, H)
    up = np.concatenate([shared_up, given("ffn_w_gate_up")], axis=0)
    gap = np.zeros((E + SHARED, UP_AT - TAIL, H), up.dtype)
    up = np.concatenate([up[:, 0:P], up[:, FFN:FFN + P], up[:, P:FFN], gap, up[:, FFN + P:]], axis=1)
    shared_down = given("ffn_ws_down").reshape(H, SHARED, FFN).transpose(1, 0, 2)
    down = np.concatenate([shared_down, given("ffn_w_down")], axis=0).transpose(0, 2, 1)
    arrays = {
        "x": x,
        "xT": x.reshape(B, 2, HALF, HK, P).transpose(0, 1, 4, 3, 2),
        "cos": cos, "sin": sin,
        "w": qkv.reshape(NKV, WCOLS, HK, P).transpose(0, 3, 2, 1),
        "wo": given("attn_Wo").reshape(H, NKV, GROUP, HD).transpose(1, 3, 2, 0),
        "gate": given("ffn_gate_w").reshape(E, HK, P).transpose(2, 1, 0),
        "up": up.reshape(E + SHARED, GCOLS, HK, P).transpose(0, 3, 2, 1),
        "down": down[:, 0:P], "down_tail": down[:, P:],
    }
    arrays = {f"in_{k}": np.ascontiguousarray(v) for k, v in arrays.items()}
    nc = bacc.Bacc("TRN2", target_bir_lowering=False, num_devices=1)
    dram = {k[3:]: nc.dram_tensor(k, v.shape, F32, kind="ExternalInput").ap() for k, v in arrays.items()}
    dram["rows"] = nc.dram_tensor("rows_dram", (ROWS, ROW), F32, kind="Internal").ap()
    dram["results"] = nc.dram_tensor("results_dram", (WAYS * T, H), F32, kind="Internal").ap()
    dram["table"] = nc.dram_tensor("table_dram", (P + 1, 1), I32, kind="Internal").ap()
    dram["empty"] = dram["rows"][SHARED * T:, :].rearrange("(n p r) c -> n p r c", p=P, r=7)
    out = nc.dram_tensor("out", (B, S, H), F32, kind="ExternalOutput").ap()
    build(nc, dram, out)
    got = run_bass_kernel_spmd(nc, [arrays], core_ids=[0])
    return got.results[0]["out"]
```

```python
from contextlib import ExitStack

import numpy as np
import concourse.bass as bass
from concourse import mybir

F32 = mybir.dt.float32
F32R = mybir.dt.float32r
BF16 = mybir.dt.bfloat16
I32 = mybir.dt.int32
U32 = mybir.dt.uint32
ALU = mybir.AluOpType
ACT = mybir.ActivationFunctionType
AX = mybir.AxisListType

P = 128
B, S, H = 2, 1024, 256
T = B * S
HK = H // P
NH, NKV, HD = 16, 4, 128
GROUP = NH // NKV
HALF = S // 2
TILES = T // P
BT = S // P
WCOLS = (GROUP + 2) * HD
EPS_LN = 1e-5

E, TOPK, FFN = 64, 6, 176
SHARED = 2
WAYS = TOPK
TAIL = FFN - P
UP_AT = 64
LOW_AT = 64
GCOLS = 2 * P + UP_AT + TAIL
BLK = 256
SUB = BLK // P
UNITS = SHARED * T // BLK
MAX_BLOCKS = T * TOPK // BLK + E - 1
LIST_BLOCKS = MAX_BLOCKS + 3
ROWS = LIST_BLOCKS * BLK
EMPTY_ROWS = 8
ROW = H + 2
SKIP = 1.0e6
EPS_TOPK = 1e-20
MASKED = -1.0e30

KV_ROUND = 2
ROUNDS = B * NKV // KV_ROUND
STEPS = KV_ROUND * 2 * GROUP * 4
PAIRS = STEPS // 2
QUADS = STEPS // 4
FIRST = 7
SPLITS = 2
FILLS = {"K": [16 * i - 9 for i in range(2 * KV_ROUND)],
         "V": [16 * i - 5 for i in range(2 * KV_ROUND)],
         "Q": [4 * q - 6 for q in range(QUADS)],
         "O": [4 * (i // 2) + 8 + i % 2 for i in range(2 * QUADS)]}
ROPES = sorted([("K", i) for i in range(2 * KV_ROUND)] + [("Q", i) for i in range(QUADS)],
               key=lambda use: FILLS[use[0]][use[1]])
SPLIT_X = [-20, -4]
SPLIT_W = [-16, 16]
SPLIT_WO = [2, 34]


def key_tiles(n):
    return 4 * (n // 16 % 2) + n % 4 + 1


def chunks(n):
    return [(a, min(a + 4, key_tiles(n))) for a in range(0, key_tiles(n), 4)]


CHUNKS = sum(len(chunks(n)) for n in range(STEPS))


def chunks_before(n):
    return n // STEPS * CHUNKS + sum(len(chunks(m)) for m in range(n % STEPS))


def rope_of(kind, i):
    per = len(FILLS[kind])
    return i // per * len(ROPES) + ROPES.index((kind, i % per))


def at(positions, n):
    for shift in (-1, 0, 1):
        if n - shift * STEPS in positions:
            return positions.index(n - shift * STEPS) + shift * len(positions)
    return None


def fill_at(n):
    for kind, positions in FILLS.items():
        if at(positions, n) is not None:
            return kind, at(positions, n)
    return None


def runs(i, per, first, last):
    return i is not None and not (first and i < per) and not (last and i >= per)


def now(k, per, n):
    return (k + 1) * per + n


def run_rounds(eng, body):
    body(-1, True, False)
    with eng.Fori(0, ROUNDS - 1) as k:
        body(k, False, False)
    body(ROUNDS - 1, False, True)


def attention(nc, dram, resid, consts):
    with ExitStack() as ctx:
        def sb(name, shape, dt=F32):
            return ctx.enter_context(nc.sbuf_tensor(name, shape, dt))

        def sem(name):
            return ctx.enter_context(nc.semaphore(name))

        def pair_of(name, shape, dt):
            return [sb(f"{name}{i}", shape, dt) for i in range(2)]

        x_raw = sb("x_raw", [P, HK, HALF])
        x_hi, x_lo = sb("x_hi", [P, HK, S], F32R), sb("x_lo", [P, HK, S], F32R)
        w_raw, wo_raw = sb("w_raw", [P, HK, WCOLS]), sb("wo_raw", [P, GROUP, H])
        w_hi, w_lo = pair_of("w_hi", [P, HK, WCOLS], F32R), pair_of("w_lo", [P, HK, WCOLS], F32R)
        wo_hi, wo_lo = pair_of("wo_hi", [P, GROUP, H], F32R), pair_of("wo_lo", [P, GROUP, H], F32R)
        k_hi, k_lo = pair_of("k_hi", [P, S], F32R), pair_of("k_lo", [P, S], F32R)
        v_hi, v_lo = pair_of("v_hi", [P, BT, HD], F32R), pair_of("v_lo", [P, BT, HD], F32R)
        q_hi, q_lo = pair_of("q_hi", [P, HALF], F32R), pair_of("q_lo", [P, HALF], F32R)
        o_hi, o_lo = pair_of("o_hi", [P, HALF], F32R), pair_of("o_lo", [P, HALF], F32R)
        taken, turn_sin = pair_of("taken", [P, HALF], F32), pair_of("turn_sin", [P, HALF], F32)
        turned = pair_of("turned", [P, HALF], F32)
        pt_hi, pt_lo = pair_of("pt_hi", [P, BT, 2 * P], F32R), pair_of("pt_lo", [P, BT, 2 * P], F32R)
        cos, sin = sb("cos", [P, S]), sb("sin", [P, S])
        probs = sb("probs", [P, 4, S])
        neg_max, row_sum, row_inv = sb("neg_max", [P, 4]), sb("row_sum", [P, 16]), sb("row_inv", [P, 16])
        empty = sb("empty", [P, ROW])
        ident_bf, causal = sb("ident_bf", [P, P], BF16), sb("causal", [P, P], BF16)
        ident = consts["ident"]

        scores_ps = [ctx.enter_context(nc.psum_tensor(f"scores{i}", [P, S], F32)) for i in range(2)]
        pt_ps = [ctx.enter_context(nc.psum_tensor(f"pt{i}", [P, 512], F32)) for i in range(2)]
        o_ps = ctx.enter_context(nc.psum_tensor("o_ps", [P, 512], F32))
        proj_ps = ctx.enter_context(nc.psum_tensor("proj_ps", [P, 512], F32))

        tables_in, resid_in = sem("tables_in"), sem("resid_in")
        x_in, w_in, wo_in, empty_out = sem("x_in"), sem("w_in"), sem("wo_in"), sem("empty_out")
        consts_made, const_step = sem("consts_made"), sem("const_step")
        x_hi_made, x_split = sem("x_hi_made"), sem("x_split")
        w_hi_made, w_split = sem("w_hi_made"), sem("w_split")
        wo_hi_made, wo_split = sem("wo_hi_made"), sem("wo_split")
        filled = {kind: sem(f"filled_{kind}") for kind in ("rope", "V", "O")}
        proj_taken, cos_made, sin_made = sem("proj_taken"), sem("cos_made"), sem("sin_made")
        turn_made, turn_hi_made, turn_split = sem("turn_made"), sem("turn_hi_made"), sem("turn_split")
        v_hi_made, v_split, resid_added = sem("v_hi_made"), sem("v_split"), sem("resid_added")
        scored, max_made, exped, inv_made = sem("scored"), sem("max_made"), sem("exped"), sem("inv_made")
        transposed, pt_hi_made, pt_split = sem("transposed"), sem("pt_hi_made"), sem("pt_split")
        o_summed, o_hi_made, o_split = sem("o_summed"), sem("o_hi_made"), sem("o_split")

        block = ctx.enter_context(nc.Block())

        def per(kind):
            return len(FILLS[kind])

        def w_cols(kind, i):
            head = {"K": GROUP, "V": GROUP + 1}.get(kind, i % GROUP)
            return slice(head * HD, (head + 1) * HD)

        def half(kind, i):
            return i // GROUP % 2 if kind == "Q" else i % 2

        def kv_of(kind, i):
            return i // (2 * GROUP) % 2 if kind == "Q" else i // 2 % 2

        def turned_into(kind, i):
            if kind == "K":
                cols = slice(half(kind, i) * HALF, (half(kind, i) + 1) * HALF)
                return k_hi[kv_of(kind, i)][:, cols], k_lo[kv_of(kind, i)][:, cols]
            return q_hi[i % 2][:], q_lo[i % 2][:]

        def lower_parts(eng, ops, k, n, first, last):
            i = at(SPLIT_X, n)
            if runs(i, SPLITS, first, last):
                cols = slice(i % 2 * HALF, (i % 2 + 1) * HALF)
                eng.wait_ge(x_hi_made, now(k, SPLITS, i + 1))
                ops.tensor_tensor(x_lo[:, :, cols], x_raw[:], x_hi[:, :, cols].bitcast(F32), ALU.subtract).then_inc(x_split, 1)
            i = at(SPLIT_W, n)
            if runs(i, SPLITS, first, last):
                eng.wait_ge(w_hi_made, now(k, SPLITS, i + 1))
                ops.tensor_tensor(w_lo[i % 2][:], w_raw[:], w_hi[i % 2][:].bitcast(F32), ALU.subtract).then_inc(w_split, 1)
            i = at(SPLIT_WO, n)
            if runs(i, SPLITS, first, last):
                eng.wait_ge(wo_hi_made, now(k, SPLITS, i + 1))
                ops.tensor_tensor(wo_lo[i % 2][:], wo_raw[:], wo_hi[i % 2][:].bitcast(F32), ALU.subtract).then_inc(wo_split, 1)

        @block.sync
        def _(sp):
            sp.dma_start(cos[:], dram["cos"]).then_inc(tables_in, 16)
            sp.dma_start(sin[:], dram["sin"]).then_inc(tables_in, 16)

            def body(k, first, last):
                def batch_of(r):
                    return r % ROUNDS // (NKV // KV_ROUND)

                def kv_at(i):
                    return (k + i // SPLITS) % (NKV // KV_ROUND) * KV_ROUND + i % SPLITS

                for n in range(FIRST, FIRST + STEPS):
                    i = at(SPLIT_X, n)
                    if runs(i, SPLITS, first, last):
                        sp.wait_ge(x_split, now(k, SPLITS, i))
                        sp.dma_start(x_raw[:], dram["xT"][bass.ds(batch_of(k + i // SPLITS), 1), i % 2]
                                     .rearrange("o p k t -> (o p) k t")).then_inc(x_in, 16)
                    i = at(SPLIT_W, n)
                    if runs(i, SPLITS, first, last):
                        sp.wait_ge(w_split, now(k, SPLITS, i))
                        sp.dma_start(w_raw[:], dram["w"][bass.ds(kv_at(i), 1)]
                                     .rearrange("o p k c -> (o p) k c")).then_inc(w_in, 16)
                    i = at(SPLIT_WO, n)
                    if runs(i, SPLITS, first, last):
                        sp.wait_ge(wo_split, now(k, SPLITS, i))
                        sp.dma_start(wo_raw[:], dram["wo"][bass.ds(kv_at(i), 1)]
                                     .rearrange("o p h c -> (o p) h c")).then_inc(wo_in, 16)
                    if first and n == FIRST + STEPS - 1:
                        sp.dma_start(resid[:], dram["x"].rearrange("(i p) c -> p i c", p=P)).then_inc(resid_in, 16)
                        sp.wait_ge(consts_made, 2)
                    if not first and n % 8 == 0:
                        sp.dma_start(dram["empty"][bass.ds(k * 8 + (n // 8 - 1), 1)].rearrange("o p r c -> (o p) r c"),
                                     empty[0:LIST_BLOCKS, :].unsqueeze(1).broadcast_to([LIST_BLOCKS, EMPTY_ROWS, ROW])).then_inc(empty_out, 16)

            run_rounds(sp, body)
            sp.wait_ge(empty_out, 16 * 8 * ROUNDS)
            sp.wait_ge(tables_in, 32)
            sp.wait_ge(resid_in, 16)

        @block.gpsimd
        def _(pool):
            pool.sem_inc(x_split, SPLITS)
            pool.sem_inc(w_split, SPLITS)
            pool.sem_inc(wo_split, SPLITS)
            for s in (cos_made, turn_made, turn_split):
                pool.sem_inc(s, len(ROPES))
            pool.memset(ident[:], 0.0).then_inc(const_step, 1)
            pool.memset(causal[:], 0.0).then_inc(const_step, 1)
            pool.memset(empty[:], 0.0).then_inc(const_step, 1)
            pool.wait_ge(const_step, 3)
            pool.affine_select(ident[:], ident[:], [[-1, P]], ALU.not_equal, 1.0, base=0,
                               channel_multiplier=1).then_inc(const_step, 1)
            pool.affine_select(causal[:], causal[:], [[-1, P]], ALU.is_ge, MASKED, base=0,
                               channel_multiplier=1).then_inc(const_step, 1)
            pool.memset(empty[:, H:H + 1], SKIP).then_inc(const_step, 1)
            pool.wait_ge(const_step, 6)
            pool.tensor_copy(ident_bf[:], ident[:]).then_inc(consts_made, 2)
            pool.wait_ge(tables_in, 32)

            def body(k, first, last):
                for n in range(FIRST, FIRST + STEPS):
                    use = fill_at(n - 3)
                    if use and use[0] in "KQ" and runs(use[1], per(use[0]), first, last):
                        r = rope_of(*use)
                        hi, lo = turned_into(*use)
                        pool.wait_ge(turn_hi_made, now(k, len(ROPES), r + 1))
                        nc.gpsimd.tensor_tensor(lo, turned[r % 2][:], hi.bitcast(F32), ALU.subtract).then_inc(turn_split, 1)
                    use = fill_at(n - 1)
                    if use and use[0] in "KQ" and runs(use[1], per(use[0]), first, last):
                        r = rope_of(*use)
                        pos = slice(half(*use) * HALF, (half(*use) + 1) * HALF)
                        pool.wait_ge(proj_taken, now(k, len(ROPES), r + 1))
                        pool.wait_ge(turn_split, now(k, len(ROPES), r - 1))
                        nc.gpsimd.tensor_tensor(turned[r % 2][:], taken[r % 2][:], cos[:, pos], ALU.mult).then_inc(cos_made, 1)
                        pool.wait_ge(cos_made, now(k, len(ROPES), r + 1))
                        pool.wait_ge(sin_made, now(k, len(ROPES), r + 1))
                        nc.gpsimd.tensor_tensor(turned[r % 2][:], turned[r % 2][:], turn_sin[r % 2][:],
                                                ALU.add).then_inc(turn_made, 1)
                    if not first:
                        lower_parts(pool, nc.gpsimd, k, n, first, last)

            run_rounds(pool, body)

        @block.scalar
        def _(act):
            act.sem_inc(x_hi_made, SPLITS)
            act.sem_inc(w_hi_made, SPLITS)
            act.sem_inc(wo_hi_made, SPLITS)
            act.sem_inc(proj_taken, len(ROPES))
            act.sem_inc(turn_hi_made, len(ROPES))
            act.sem_inc(v_hi_made, per("V"))
            act.sem_inc(exped, STEPS)
            act.sem_inc(pt_hi_made, CHUNKS)
            act.sem_inc(o_hi_made, PAIRS)

            def body(k, first, last):
                for n in range(FIRST, FIRST + STEPS):
                    j = (n - 6) // 2
                    if n % 2 == 0 and runs(j, PAIRS, first, last):
                        act.wait_ge(o_summed, now(k, PAIRS, j + 1))
                        act.wait_ge(filled["O"], now(k, per("O"), j - 3))
                        nc.scalar.activation(o_hi[j // 2 % 2][:, 256 * (j % 2):256 * (j % 2) + 256], o_ps[:, 0:256],
                                             ACT.Copy).then_inc(o_hi_made, 1)
                    m = n - 1
                    if runs(m, STEPS, first, last):
                        act.wait_ge(max_made, now(k, STEPS, m + 1))
                        act.wait_ge(transposed, now(k, CHUNKS, chunks_before(m - 3)))
                        act.wait_ge(inv_made, now(k, QUADS, m // 4 - 3))
                        w = key_tiles(m) * P
                        nc.scalar.activation(probs[:, m % 4, 0:w], scores_ps[m % 2][:, 0:w], ACT.Exp,
                                             bias=neg_max[:, m % 4:m % 4 + 1],
                                             accum_out=row_sum[:, m % 16:m % 16 + 1]).then_inc(exped, 1)
                    use = fill_at(n - 1)
                    if use and runs(use[1], per(use[0]), first, last):
                        kind, i = use
                        if kind in "KQ":
                            r = rope_of(*use)
                            act.wait_ge(filled["rope"], now(k, len(ROPES), r + 1))
                            act.wait_ge(turn_made, now(k, len(ROPES), r - 1))
                            nc.scalar.activation(taken[r % 2][:], proj_ps[:], ACT.Copy).then_inc(proj_taken, 1)
                        if kind == "V":
                            act.wait_ge(filled["V"], now(k, per("V"), i + 1))
                            act.wait_ge(o_summed, now(k, PAIRS, 16 * (i // 2) + 16 - PAIRS))
                            nc.scalar.activation(v_hi[kv_of(*use)][:, 4 * (i % 2):4 * (i % 2) + 4, :], proj_ps[:],
                                                 ACT.Copy).then_inc(v_hi_made, 1)
                    m = n - 2
                    if runs(m, STEPS, first, last):
                        for i, (a, z) in enumerate(chunks(m)):
                            c = chunks_before(m) + i
                            act.wait_ge(transposed, now(k, CHUNKS, c + 1))
                            act.wait_ge(o_summed, now(k, PAIRS, m // 2 - 1))
                            nc.scalar.activation(pt_hi[m // 2 % 2][:, a:z, P * (m % 2):P * (m % 2) + P],
                                                 pt_ps[c % 2][:, 0:P * (z - a)].rearrange("p (k q) -> p k q", q=P),
                                                 ACT.Copy).then_inc(pt_hi_made, 1)
                    use = fill_at(n - 3)
                    if use and use[0] in "KQ" and runs(use[1], per(use[0]), first, last):
                        r = rope_of(*use)
                        last_reader = 32 * (use[1] // 2) + 32 - STEPS if use[0] == "K" else 4 * (use[1] - 1)
                        act.wait_ge(scored, now(k, STEPS, last_reader))
                        act.wait_ge(turn_made, now(k, len(ROPES), r + 1))
                        nc.scalar.activation(turned_into(*use)[0], turned[r % 2][:], ACT.Copy).then_inc(turn_hi_made, 1)
                    i = at(SPLIT_X, n)
                    if runs(i, SPLITS, first, last):
                        act.wait_ge(x_in, 16 * (SPLITS * k + i + 1))
                        act.wait_ge(filled["rope"], now(k, len(ROPES), rope_of("Q", 12 + 4 * (i % 2) - 1 + QUADS * (i // 2 - 1)) + 1))
                        nc.scalar.activation(x_hi[:, :, i % 2 * HALF:(i % 2 + 1) * HALF], x_raw[:], ACT.Copy).then_inc(x_hi_made, 1)
                    i = at(SPLIT_W, n)
                    if runs(i, SPLITS, first, last):
                        act.wait_ge(w_in, 16 * (SPLITS * k + i + 1))
                        act.wait_ge(filled["rope"], now(k, len(ROPES), rope_of("Q", 8 * (i % 2) + 7 + QUADS * (i // 2 - 1)) + 1))
                        nc.scalar.activation(w_hi[i % 2][:], w_raw[:], ACT.Copy).then_inc(w_hi_made, 1)
                    i = at(SPLIT_WO, n)
                    if runs(i, SPLITS, first, last):
                        act.wait_ge(wo_in, 16 * (SPLITS * k + i + 1))
                        act.wait_ge(filled["O"], now(k, per("O"), 16 * (i - SPLITS + 1)))
                        nc.scalar.activation(wo_hi[i % 2][:], wo_raw[:], ACT.Copy).then_inc(wo_hi_made, 1)

            run_rounds(act, body)

        @block.vector
        def _(dve):
            dve.sem_inc(sin_made, len(ROPES))
            dve.sem_inc(v_split, per("V"))
            dve.sem_inc(resid_added, per("O"))
            dve.sem_inc(max_made, STEPS)
            dve.sem_inc(inv_made, QUADS)
            dve.sem_inc(pt_split, CHUNKS)
            dve.sem_inc(o_split, PAIRS)
            dve.wait_ge(tables_in, 32)

            def body(k, first, last):
                for n in range(FIRST, FIRST + STEPS):
                    m = n - 3
                    if runs(m, STEPS, first, last):
                        for i, (a, z) in enumerate(chunks(m)):
                            c = chunks_before(m) + i
                            part = (slice(None), slice(a, z), slice(P * (m % 2), P * (m % 2) + P))
                            dve.wait_ge(pt_hi_made, now(k, CHUNKS, c + 1))
                            nc.vector.tensor_tensor(pt_lo[m // 2 % 2][part],
                                                    pt_ps[c % 2][:, 0:P * (z - a)].rearrange("p (k q) -> p k q", q=P),
                                                    pt_hi[m // 2 % 2][part].bitcast(F32), ALU.subtract).then_inc(pt_split, 1)
                    j = (n - 6) // 2
                    if n % 2 == 0 and runs(j, PAIRS, first, last):
                        part = (slice(None), slice(256 * (j % 2), 256 * (j % 2) + 256))
                        dve.wait_ge(o_hi_made, now(k, PAIRS, j + 1))
                        nc.vector.tensor_tensor(o_lo[j // 2 % 2][part], o_ps[:, 0:256], o_hi[j // 2 % 2][part].bitcast(F32),
                                                ALU.subtract).then_inc(o_split, 1)
                    q = (n - 5) // 4
                    if n % 4 == 1 and runs(q, QUADS, first, last):
                        dve.wait_ge(exped, now(k, STEPS, 4 * q + 4))
                        cols = slice(q % 4 * 4, q % 4 * 4 + 4)
                        nc.vector.reciprocal(row_inv[:, cols], row_sum[:, cols]).then_inc(inv_made, 1)
                    use = fill_at(n - 1)
                    if use and use[0] == "O" and runs(use[1], per("O"), first, last):
                        i = use[1] % per("O")
                        dve.wait_ge(filled["O"], now(k, per("O"), use[1] + 1))
                        dve.wait_ge(inv_made, now(k, QUADS, use[1] // 2 + 1))
                        for t in range(2):
                            tile = 4 * (i // 8 % 2) + 2 * (i % 2) + t
                            col = 4 * (i // 2 % 4) + 2 * (i % 2) + t
                            row = resid[:].rearrange("p i c -> p (i c)")[:, bass.ds(k // (NKV // KV_ROUND) * (BT * H) + tile * H, H)]
                            ins = nc.vector.scalar_tensor_tensor(out=row, in0=proj_ps[:, t * H:(t + 1) * H],
                                                                 scalar=row_inv[:, col:col + 1], in1=row,
                                                                 op0=ALU.mult, op1=ALU.add)
                        ins.then_inc(resid_added, 1)
                    if runs(n, STEPS, first, last):
                        dve.wait_ge(scored, now(k, STEPS, n + 1))
                        nc.vector.tensor_reduce(neg_max[:, n % 4:n % 4 + 1], scores_ps[n % 2][:, 0:key_tiles(n) * P],
                                                AX.X, ALU.max, negate=True).then_inc(max_made, 1)
                    if use and use[0] in "KQ" and runs(use[1], per(use[0]), first, last):
                        r = rope_of(*use)
                        pos = slice(half(*use) * HALF, (half(*use) + 1) * HALF)
                        dve.wait_ge(proj_taken, now(k, len(ROPES), r + 1))
                        dve.wait_ge(turn_made, now(k, len(ROPES), r - 1))
                        nc.vector.tensor_tensor(turn_sin[r % 2][0:64], taken[r % 2][64:128], sin[64:128, pos], ALU.mult)
                        nc.vector.tensor_tensor(turn_sin[r % 2][64:128], taken[r % 2][0:64], sin[0:64, pos],
                                                ALU.mult).then_inc(sin_made, 1)
                    if use and use[0] == "V" and runs(use[1], per("V"), first, last):
                        u, c = kv_of(*use), use[1] % 2
                        dve.wait_ge(v_hi_made, now(k, per("V"), use[1] + 1))
                        nc.vector.tensor_tensor(v_lo[u][:, 4 * c:4 * c + 4, :].rearrange("p t d -> p (t d)"), proj_ps[:],
                                                v_hi[u][:, 4 * c:4 * c + 4, :].rearrange("p t d -> p (t d)").bitcast(F32),
                                                ALU.subtract).then_inc(v_split, 1)
                    if first:
                        lower_parts(dve, nc.vector, k, n, first, last)
                if first:
                    dve.wait_ge(resid_in, 16)

            run_rounds(dve, body)

        @block.tensor
        def _(pe):
            pe.sem_inc(filled["rope"], len(ROPES))
            pe.sem_inc(filled["V"], per("V"))
            pe.sem_inc(filled["O"], per("O"))
            pe.sem_inc(scored, STEPS)
            pe.sem_inc(transposed, CHUNKS)
            pe.sem_inc(o_summed, PAIRS)
            pe.wait_ge(consts_made, 2)

            def products(out, left, right, first, last):
                (lh, ll), (rh, rl) = left, right
                nc.tensor.matmul(out, lh, rh, start=first, stop=False)
                nc.tensor.matmul(out, lh, rl, start=False, stop=False)
                return nc.tensor.matmul(out, ll, rh, start=False, stop=last)

            def body(k, first, last):
                def bank_free(n):
                    for before in range(n - 1, 0, -1):
                        use = fill_at(before)
                        if use and (before < FIRST or runs(use[1], per(use[0]), first, last)):
                            break
                    else:
                        return
                    if use[0] == "O":
                        pe.wait_ge(resid_added, now(k, per("O"), use[1] + 1))
                    elif use[0] == "V":
                        pe.wait_ge(v_split, now(k, per("V"), use[1] + 1))
                    else:
                        pe.wait_ge(proj_taken, now(k, len(ROPES), rope_of(*use) + 1))

                def fill(n, kind, i):
                    bank_free(n)
                    u = kv_of(kind, i)
                    if kind == "O":
                        q, a = i // 2, i % 2
                        u, head = q // 8 % 2, q % GROUP
                        pe.wait_ge(o_split, now(k, PAIRS, i + 1))
                        if q % 8 == 0 and a == 0:
                            pe.wait_ge(wo_split, now(k, SPLITS, q // 8 + 1))
                        for t in range(2):
                            tok = slice((a * 2 + t) * P, (a * 2 + t + 1) * P)
                            mm = products(proj_ps[:, t * H:(t + 1) * H], (o_hi[q % 2][:, tok], o_lo[q % 2][:, tok]),
                                          (wo_hi[u][:, head, :], wo_lo[u][:, head, :]), True, True)
                        mm.then_inc(filled["O"], 1)
                        return
                    if kind == "K":
                        if i % 2 == 0:
                            pe.wait_ge(w_split, now(k, SPLITS, i // 2 + 1))
                        if i % per("K") < 2:
                            pe.wait_ge(x_split, now(k, SPLITS, i // per("K") * SPLITS + i % 2 + 1))
                    if kind == "V":
                        for t in range(4):
                            tok = slice((4 * half(kind, i) + t) * P, (4 * half(kind, i) + t + 1) * P)
                            for c in range(HK):
                                mm = products(proj_ps[:, t * HD:(t + 1) * HD], (x_hi[:, c, tok], x_lo[:, c, tok]),
                                              (w_hi[u][:, c, w_cols(kind, i)], w_lo[u][:, c, w_cols(kind, i)]), c == 0, c == HK - 1)
                        mm.then_inc(filled["V"], 1)
                        return
                    tok = slice(half(kind, i) * HALF, (half(kind, i) + 1) * HALF)
                    for c in range(HK):
                        mm = products(proj_ps[:], (w_hi[u][:, c, w_cols(kind, i)], w_lo[u][:, c, w_cols(kind, i)]),
                                      (x_hi[:, c, tok], x_lo[:, c, tok]), c == 0, c == HK - 1)
                    mm.then_inc(filled["rope"], 1)

                for n in range(FIRST, FIRST + STEPS):
                    if runs(n, STEPS, first, last):
                        if n % 4 == 0:
                            pe.wait_ge(turn_split, now(k, len(ROPES), rope_of("Q", n // 4) + 1))
                        pe.wait_ge(exped, now(k, STEPS, n - 1))
                        u, b = n // 32 % 2, n // 4 % 2
                        qt = (slice(None), slice(P * (n % 4), P * (n % 4) + P))
                        for a, z in chunks(n):
                            keys = slice(a * P, z * P)
                            out = scores_ps[n % 2][:, keys]
                            nc.tensor.matmul(out, q_hi[b][qt], k_hi[u][:, keys], start=True, stop=False)
                            nc.tensor.matmul(out, q_hi[b][qt], k_lo[u][:, keys], start=False, stop=False)
                            if z == key_tiles(n):
                                nc.tensor.matmul(scores_ps[n % 2][:, (z - 1) * P:z * P], ident_bf[:], causal[:],
                                                 start=False, stop=False)
                            mm = nc.tensor.matmul(out, q_lo[b][qt], k_hi[u][:, keys], start=False, stop=True)
                        mm.then_inc(scored, 1)
                    m = n - 2
                    if runs(m, STEPS, first, last):
                        pe.wait_ge(exped, now(k, STEPS, m + 1))
                        for i, (a, z) in enumerate(chunks(m)):
                            c = chunks_before(m) + i
                            pe.wait_ge(pt_split, now(k, CHUNKS, c - 1))
                            for t in range(a, z):
                                mm = nc.tensor.transpose(pt_ps[c % 2][:, (t - a) * P:(t - a + 1) * P],
                                                         probs[:, m % 4, t * P:(t + 1) * P], ident[:])
                            mm.then_inc(transposed, 1)
                    j = (n - 4) // 2
                    if runs(j, PAIRS, first, last):
                        u, count = j // 16 % 2, key_tiles(2 * j + 1)
                        if n % 2 == 0:
                            if j % 8 == 0:
                                pe.wait_ge(v_split, now(k, per("V"), j // 8 + 1))
                            pe.wait_ge(pt_split, now(k, CHUNKS, chunks_before(2 * j + 2)))
                            pe.wait_ge(o_split, now(k, PAIRS, j))
                        for t in (range(count // 2) if n % 2 == 0 else range(count // 2, count)):
                            q0 = P if t == count - 1 else 0
                            qs = slice(q0, 2 * P)
                            mm = products(o_ps[:, qs], (v_hi[u][:, t, :], v_lo[u][:, t, :]),
                                          (pt_hi[j % 2][:, t, qs], pt_lo[j % 2][:, t, qs]), t == 0, t == count - 1)
                        if n % 2 == 1:
                            mm.then_inc(o_summed, 1)
                    use = fill_at(n)
                    if use and runs(use[1], per(use[0]), first, last):
                        fill(n, *use)

            run_rounds(pe, body)


def done(n, back=0):
    return n + 4 - back


def routing(nc, dram, resid, consts):
    with ExitStack() as ctx:
        def sb(name, shape, dt=F32):
            return ctx.enter_context(nc.sbuf_tensor(name, shape, dt))

        def sem(name):
            return ctx.enter_context(nc.semaphore(name))

        ident = consts["ident"]
        stats, moments = sb("stats", [P, TILES, 6]), sb("moments", [P, TILES, 2])
        deviation, inv_dev = sb("deviation", [P, TILES]), sb("inv_dev", [P, TILES])
        xt = sb("xt", [P, HK, T])
        gate = sb("gate", [P, HK, E])
        top, top_at = sb("top", [P, TILES, 8]), sb("top_at", [P, TILES, 8], U32)
        top_id = sb("top_id", [P, TILES, 8])
        shifted, exp_all = sb("shifted", [P, TILES, E]), sb("exp_all", [P, TILES, E])
        exp_top = sb("exp_top", [P, TILES, TOPK])
        sum_all, sum_top = sb("sum_all", [P, TILES]), sb("sum_top", [P, TILES])
        expert_ids = sb("expert_ids", [P, E])
        chosen = sb("chosen", [P, TOPK, TILES, E], BF16)
        mask = sb("mask", [P, 2, TILES, E], BF16)
        before, ones = sb("before", [P, P], BF16), sb("ones", [P, P], BF16)
        counts, counts_int = sb("counts", [P, E]), sb("counts_int", [P, E], I32)
        blocks, blocks_to, first_row = sb("blocks", [P, E]), sb("blocks_to", [P, E]), sb("first_row", [P, E])
        one_row = sb("one_row", [P, E])
        slot_of = sb("slot_of", [P, TILES, E])
        product = sb("product", [P, TILES, E])
        slots, slots_int = sb("slots", [P, TILES, TOPK]), sb("slots_int", [P, TILES, TOPK], I32)
        goes_with = sb("goes_with", [P, TILES, WAYS, 2])
        rows = sb("rows", [P, TILES, WAYS, ROW])
        block_id = sb("block_id", [P, 1])
        started, owner, owner_int = sb("started", [P, E]), sb("owner", [P, 1]), sb("owner_int", [P, 1], I32)
        triples, triples_int = sb("triples", [P, 1]), sb("triples_int", [P, 1], I32)
        up_w, down_w = sb("shared_up", [P, SHARED, HK, GCOLS]), sb("shared_down", [P, SHARED, 2, H])
        silu = [sb(f"shared_silu{i}", [P, 2, BLK]) for i in range(2)]
        hidden = [sb(f"shared_hidden{i}", [P, 2, BLK]) for i in range(4)]

        logits_ps = ctx.enter_context(nc.psum_tensor("logits_ps", [P, TILES * E], F32))
        places_ps = ctx.enter_context(nc.psum_tensor("places_ps", [P, TILES * E], F32))
        xt_ps = [ctx.enter_context(nc.psum_tensor(f"xt_ps{i}", [P, 512], F32)) for i in range(2)]
        counts_ps = ctx.enter_context(nc.psum_tensor("counts_ps", [P, 512], F32))
        gate_up_ps = [logits_ps[:, 512 * i:512 * (i + 1)] for i in range(2)]
        tail_ps = xt_ps
        y_ps = [places_ps[:, 512 * i:512 * (i + 1)] for i in range(2)]

        gate_in, table_out, table_in = sem("gate_in"), sem("table_out"), sem("table_in")
        consts_set, const_step = sem("consts_set"), sem("const_step")
        dve_step = sem("dve_step")
        moments_made, deviation_made, normed = sem("moments_made"), sem("deviation_made"), sem("normed")
        xt_turned, xt_made, logits_made = sem("xt_turned"), sem("xt_made"), sem("logits_made")
        shifted_made, exps_made = sem("shifted_made"), sem("exps_made")
        mask_made, places_made = sem("mask_made"), sem("places_made")
        slots_made, table_made = sem("slots_made"), sem("table_made")
        rows_filled, rows_ready, sent = sem("rows_filled"), sem("rows_ready"), sem("sent")
        shared_in = sem("shared_in")
        gated, silu_made, hidden_made = sem("shared_gated"), sem("shared_silu_made"), sem("shared_hidden_made")
        downed, added = sem("shared_downed"), sem("shared_added")

        block = ctx.enter_context(nc.Block())

        @block.sync
        def _(sp):
            sp.dma_start(gate[:], dram["gate"]).then_inc(gate_in, 16)
            sp.dma_start(up_w[:], dram["shared_up"]).then_inc(shared_in, 16)
            sp.dma_start(down_w[:, :, 0, :], dram["shared_down"]).then_inc(shared_in, 16)
            sp.dma_start(down_w[0:TAIL, :, 1, :], dram["shared_down_tail"]).then_inc(shared_in, 16)
            sp.wait_ge(table_made, 1)
            sp.dma_start(dram["table"][0:P, :], owner_int[:]).then_inc(table_out, 16)
            sp.dma_start(dram["table"][P:P + 1, :], triples_int[0:1, :]).then_inc(table_out, 16)
            sp.wait_ge(table_out, 32)
            sp.dma_start(consts["table"][:], dram["table"].rearrange("r c -> c r")).then_inc(table_in, 16)
            sp.wait_ge(table_in, 16)

        @block.gpsimd
        def _(pool):
            pool.memset(before[:], 1.0).then_inc(const_step, 1)
            pool.memset(ones[:], 1.0).then_inc(const_step, 1)
            pool.memset(one_row[:], 1.0).then_inc(const_step, 1)
            pool.memset(goes_with[:], 1.0).then_inc(const_step, 1)
            pool.iota(expert_ids[:], [[1, E]], base=0, channel_multiplier=0,
                      allow_small_or_imprecise_dtypes=True).then_inc(const_step, 1)
            pool.iota(block_id[:], [[0, 1]], base=0, channel_multiplier=1,
                      allow_small_or_imprecise_dtypes=True).then_inc(const_step, 1)
            pool.wait_ge(const_step, 6)
            pool.affine_select(before[:], before[:], [[1, P]], ALU.is_gt, 0.0, base=0,
                               channel_multiplier=-1).then_inc(const_step, 1)
            pool.iota(goes_with[:, :, :, 0], [[P, TILES], [T, WAYS]], base=0, channel_multiplier=1,
                      allow_small_or_imprecise_dtypes=True).then_inc(const_step, 1)
            pool.wait_ge(const_step, 8)
            pool.sem_inc(consts_set, 1)
            pool.wait_ge(rows_ready, 1)
            for j in range(TOPK):
                pool.wait_ge(slots_made, j + 1)
                for i in range(TILES):
                    pool.indirect_dma_start(
                        out=dram["rows"], out_offset=bass.IndirectOffsetOnAxis(ap=slots_int[:, i, j:j + 1], axis=0),
                        in_=rows[:, i, j, :], in_offset=None, bounds_check=ROWS - 1,
                        oob_is_err=False).then_inc(sent, 16)
            pool.wait_ge(sent, 16 * TOPK * TILES)

        @block.scalar
        def _(act):
            act.wait_ge(moments_made, 1)
            act.activation(deviation[:], deviation[:], ACT.Sqrt).then_inc(deviation_made, 1)
            for i in range(TILES):
                act.wait_ge(xt_turned, i + 1)
                act.activation(xt[:, :, i * P:(i + 1) * P], xt_ps[i % 2][:, 0:H].rearrange("p (k t) -> p k t", k=HK),
                               ACT.Copy).then_inc(xt_made, 1)
            for i in range(TILES):
                act.activation(rows[:, i, :, 0:H], resid[:, i, :].unsqueeze(1).broadcast_to([P, WAYS, H]),
                               ACT.Copy).then_inc(rows_filled, 1)
                if i == TILES - 4:
                    act.wait_ge(shifted_made, 1)
                    act.activation(exp_all[:], shifted[:], ACT.Exp).then_inc(exps_made, 1)
                    act.activation(exp_top[:], exp_top[:], ACT.Exp).then_inc(exps_made, 1)
            act.sem_inc(silu_made, 3)
            with act.Fori(0, UNITS // 4) as q:
                for u in range(4):
                    n = 4 * q + u
                    act.wait_ge(gated, done(n))
                    act.wait_ge(hidden_made, done(n, 2))
                    nc.scalar.activation(silu[u % 2][:, 0, :], gate_up_ps[u % 2][:, 0:BLK], ACT.Silu)
                    nc.scalar.activation(silu[u % 2][0:TAIL, 1, :], tail_ps[u % 2][0:TAIL, 0:BLK], ACT.Silu).then_inc(silu_made, 1)

        @block.vector
        def _(dve):
            steps = [0]

            def then(ins):
                steps[0] += 1
                ins.then_inc(dve_step, 1)
                dve.wait_ge(dve_step, steps[0])

            for i in range(TILES):
                ins = dve.bn_stats(stats[:, i, :], resid[:, i, :])
            then(ins)
            for i in range(TILES):
                ins = dve.bn_aggr(moments[:, i, :], stats[:, i, :])
            then(ins)
            dve.tensor_scalar(deviation[:], moments[:, :, 1], EPS_LN, None, ALU.add).then_inc(moments_made, 1)
            dve.wait_ge(deviation_made, 1)
            then(dve.reciprocal(inv_dev[:], deviation[:]))
            for i in range(TILES):
                dve.tensor_scalar(resid[:, i, :], resid[:, i, :], moments[:, i, 0:1], inv_dev[:, i:i + 1],
                                  ALU.subtract, ALU.mult).then_inc(normed, 1)
            dve.wait_ge(consts_set, 1)
            dve.wait_ge(logits_made, TILES)
            for i in range(TILES):
                ins = dve.max(top[:, i, :], logits_ps[:, i * E:(i + 1) * E])
            then(ins)
            for i in range(TILES):
                ins = dve.max_index(top_at[:, i, :], top[:, i, :], logits_ps[:, i * E:(i + 1) * E])
            then(ins)
            then(dve.tensor_copy(top_id[:], top_at[:]))
            for j in range(TOPK):
                ins = dve.tensor_tensor(chosen[:, j], expert_ids[:].unsqueeze(1).broadcast_to([P, TILES, E]),
                                        top_id[:, :, j:j + 1].broadcast_to([P, TILES, E]), ALU.is_equal)
            then(ins)
            then(dve.tensor_tensor(mask[:, 1], chosen[:, 0], chosen[:, 1], ALU.add))
            for j in range(2, TOPK):
                ins = dve.tensor_tensor(mask[:, j % 2], mask[:, (j - 1) % 2], chosen[:, j], ALU.add)
                then(ins)
            dve.sem_inc(mask_made, 1)
            dve.tensor_tensor(shifted[:], logits_ps[:].rearrange("p (i e) -> p i e", e=E),
                              top[:, :, 0:1].broadcast_to([P, TILES, E]), ALU.subtract)
            dve.tensor_tensor(exp_top[:], top[:, :, 0:TOPK], top[:, :, 0:1].broadcast_to([P, TILES, TOPK]),
                              ALU.subtract).then_inc(shifted_made, 1)
            dve.wait_ge(places_made, 1)
            then(dve.tensor_scalar(counts[:], counts_ps[:, 0:E], float(BLK - 1), None, ALU.add))
            then(dve.tensor_copy(counts_int[:], counts[:]))
            then(dve.tensor_scalar(counts_int[:], counts_int[:], BLK.bit_length() - 1, None, ALU.logical_shift_right))
            then(dve.tensor_copy(blocks[:], counts_int[:]))
            then(dve.tensor_tensor_scan(blocks_to[:], one_row[:], blocks[:], 0.0, ALU.mult, ALU.add))
            then(dve.tensor_tensor(started[:], blocks_to[:], blocks[:], ALU.subtract))
            then(dve.tensor_scalar(first_row[:], started[:], float(BLK), None, ALU.mult))
            dve.wait_ge(places_made, 2)
            then(dve.tensor_tensor(slot_of[:], places_ps[:].rearrange("p (i e) -> p i e", e=E),
                                   first_row[:].unsqueeze(1).broadcast_to([P, TILES, E]), ALU.add))
            dve.wait_ge(exps_made, 2)
            dve.tensor_reduce(sum_all[:], exp_all[:], AX.X, ALU.add)
            then(dve.tensor_reduce(sum_top[:], exp_top[:], AX.X, ALU.add))
            then(dve.scalar_tensor_tensor(out=sum_top[:], in0=sum_all[:], scalar=EPS_TOPK, in1=sum_top[:],
                                          op0=ALU.mult, op1=ALU.add))
            then(dve.reciprocal(sum_top[:], sum_top[:]))
            then(dve.tensor_tensor(goes_with[:, :, 0:TOPK, 1], exp_top[:],
                                   sum_top[:].unsqueeze(2).broadcast_to([P, TILES, TOPK]), ALU.mult))
            dve.wait_ge(rows_filled, TILES)
            dve.tensor_copy(rows[:, :, :, H:ROW], goes_with[:]).then_inc(rows_ready, 1)
            for j in range(TOPK):
                then(dve.tensor_tensor(product[:], chosen[:, j], slot_of[:], ALU.mult))
                then(dve.tensor_reduce(slots[:, :, j], product[:], AX.X, ALU.add))
                dve.tensor_copy(slots_int[:, :, j], slots[:, :, j]).then_inc(slots_made, 1)
            then(dve.tensor_scalar(started[:], started[:], block_id[:], None, ALU.is_le))
            then(dve.tensor_reduce(owner[:], started[:], AX.X, ALU.add))
            then(dve.tensor_scalar(owner[:], owner[:], 1.0, None, ALU.subtract))
            then(dve.tensor_copy(owner_int[:], owner[:]))
            then(dve.tensor_scalar(triples[:], blocks_to[:, E - 1:E], 171.0, 171.0, ALU.mult, ALU.add))
            then(dve.tensor_copy(triples_int[:], triples[:]))
            dve.tensor_scalar(triples_int[:], triples_int[:], 9, None,
                              ALU.logical_shift_right).then_inc(table_made, 1)

            dve.sem_inc(hidden_made, 3)
            dve.sem_inc(added, 3)

            def hide(first, u):
                n, chunk = first + u, first // 2 + u // 2
                dve.wait_ge(silu_made, done(n))
                dve.wait_ge(downed, done(chunk, 2))
                dve.tensor_tensor(hidden[u % 4][:, 0, :], silu[u % 2][:, 0, :], gate_up_ps[u % 2][:, BLK:2 * BLK], ALU.mult)
                dve.tensor_tensor(hidden[u % 4][0:TAIL, 1, :], silu[u % 2][0:TAIL, 1, :],
                                  tail_ps[u % 2][UP_AT:UP_AT + TAIL, 0:BLK], ALU.mult).then_inc(hidden_made, 1)

            def add(first, u):
                chunk = first // 2 + u // 2
                dve.wait_ge(downed, done(chunk))
                tok = resid[:].rearrange("p i c -> p (i c)")[:, bass.ds(chunk * (2 * H), 2 * H)]
                dve.tensor_tensor(tok, y_ps[u // 2 % 2], tok, ALU.add).then_inc(added, 1)

            hide(0, 0)
            hide(0, 1)
            with dve.Fori(0, UNITS // 4 - 1) as q:
                for u in (2, 4):
                    hide(4 * q, u)
                    hide(4 * q, u + 1)
                    add(4 * q, u - 2)
            hide(UNITS - 4, 2)
            hide(UNITS - 4, 3)
            add(UNITS - 4, 0)
            add(UNITS - 4, 2)

        @block.tensor
        def _(pe):
            pe.wait_ge(gate_in, 16)

            pe.sem_inc(gated, 3)
            pe.sem_inc(downed, 3)

            def turn(i):
                pe.wait_ge(normed, i + 1)
                if i >= 2:
                    pe.wait_ge(xt_made, i - 1)
                for k in range(HK):
                    mm = nc.tensor.transpose(xt_ps[i % 2][:, k * P:(k + 1) * P], resid[:, i, k * P:(k + 1) * P], ident[:])
                mm.then_inc(xt_turned, 1)

            turn(0)
            for i in range(TILES):
                if i + 1 < TILES:
                    turn(i + 1)
                pe.wait_ge(xt_made, i + 1)
                for k in range(HK):
                    mm = nc.tensor.matmul(logits_ps[:, i * E:(i + 1) * E], xt[:, k, i * P:(i + 1) * P], gate[:, k, :],
                                          start=(k == 0), stop=(k == HK - 1))
                mm.then_inc(logits_made, 1)
            pe.wait_ge(mask_made, 1)
            pe.wait_ge(consts_set, 1)
            picks = mask[:, (TOPK - 1) % 2]
            for i in range(TILES):
                mm = nc.tensor.matmul(counts_ps[:, 0:E], ones[:], picks[:, i, :], start=(i == 0), stop=(i == TILES - 1))
            mm.then_inc(places_made, 1)
            for i in range(TILES):
                out = places_ps[:, i * E:(i + 1) * E]
                mm = nc.tensor.matmul(out, before[:], picks[:, i, :], start=True, stop=(i == 0))
                for k in range(i):
                    mm = nc.tensor.matmul(out, ones[:], picks[:, k, :], start=False, stop=(k == i - 1))
            mm.then_inc(places_made, 1)

            def gate_up(first, u):
                n = first + u
                pe.wait_ge(hidden_made, done(n, 2))
                for out, c, z in ((gate_up_ps[u % 2][:, 0:BLK], 0, P), (gate_up_ps[u % 2][:, BLK:2 * BLK], P, 2 * P),
                                  (tail_ps[u % 2][0:GCOLS - 2 * P, 0:BLK], 2 * P, GCOLS)):
                    for k in range(HK):
                        mm = nc.tensor.matmul(out, up_w[:, u % 2, k, c:z], xt[:, k, bass.ds((first // 2 + u // 2) * BLK, BLK)],
                                              start=(k == 0), stop=(k == HK - 1))
                mm.then_inc(gated, 1)

            def down(first, u):
                chunk = first // 2 + u // 2
                pe.wait_ge(hidden_made, done(first + u + 1))
                pe.wait_ge(added, done(chunk, 2))
                for t in range(SUB):
                    tok = slice(t * P, (t + 1) * P)
                    out = y_ps[u // 2 % 2][:, t * H:(t + 1) * H]
                    for v in range(SHARED):
                        part = hidden[(u + v) % 4]
                        nc.tensor.matmul(out, part[:, 0, tok], down_w[:, v, 0, :], start=(v == 0), stop=False)
                        mm = nc.tensor.matmul(out, part[0:TAIL, 1, tok], down_w[0:TAIL, v, 1, :],
                                              start=False, stop=(v == SHARED - 1))
                mm.then_inc(downed, 1)

            pe.wait_ge(shared_in, 48)
            gate_up(0, 0)
            gate_up(0, 1)
            pe.wait_ge(slots_made, TOPK)
            with pe.Fori(0, UNITS // 4 - 1) as q:
                for u in (2, 4):
                    gate_up(4 * q, u)
                    gate_up(4 * q, u + 1)
                    down(4 * q, u - 2)
            gate_up(UNITS - 4, 2)
            gate_up(UNITS - 4, 3)
            down(UNITS - 4, 0)
            down(UNITS - 4, 2)


def experts(nc, dram, resid, consts, out):
    with ExitStack() as ctx:
        def sb(name, shape, dt=F32):
            return ctx.enter_context(nc.sbuf_tensor(name, shape, dt))

        def sem(name):
            return ctx.enter_context(nc.semaphore(name))

        def three(name, shape, dt=F32):
            return [sb(f"{name}{i}", shape, dt) for i in range(3)]

        ident, table = consts["ident"], consts["table"]
        up_raw, up_hi, up_lo = three("up_raw", [P, HK, GCOLS]), three("up_hi", [P, HK, GCOLS], F32R), three("up_lo", [P, HK, GCOLS], F32R)
        down_raw, down_hi, down_lo = three("down_raw", [P, 2, H]), three("down_hi", [P, 2, H], F32R), three("down_lo", [P, 2, H], F32R)
        x_in = three("x_in", [P, SUB, ROW])
        x_hi, x_lo = three("xt_hi", [P, HK, BLK], F32R), three("xt_lo", [P, HK, BLK], F32R)
        silu, hidden = three("silu", [P, 2, BLK]), three("hidden", [P, 2, BLK])
        hidden_hi, hidden_lo = three("hidden_hi", [P, 2, BLK], F32R), three("hidden_lo", [P, BLK], F32R)
        y_sb, dest, weight = three("y_sb", [P, SUB, H]), three("dest", [P, SUB], I32), three("weight", [P, SUB])
        goes_with = three("goes_with", [P, SUB, 2])
        RING, GROUP_TILES = 8, 4
        parts = [sb(f"parts{i}", [P, WAYS, H]) for i in range(RING)]
        total = sb("total", [P, 2, H])
        stats, moments = sb("stats2", [P, TILES, 6]), sb("moments2", [P, TILES, 2])
        deviation, inv_dev = sb("deviation2", [P, TILES]), sb("inv_dev2", [P, TILES])
        shift = sb("shift", [P, TILES])

        x_ps = ctx.enter_context(nc.psum_tensor("x_ps", [P, 512], F32))
        gate_up_ps = [ctx.enter_context(nc.psum_tensor(f"gate_up{i}", [P, 512], F32)) for i in range(3)]
        tail_ps = [ctx.enter_context(nc.psum_tensor(f"tail{i}", [P, 512], F32)) for i in range(3)]
        y_ps = ctx.enter_context(nc.psum_tensor("y_ps", [P, 512], F32))

        up_in, down_in, rows_in, y_out = ([sem(f"{name}{i}") for i in range(3)] for name in ("up_in", "down_in", "rows_in", "y_out"))
        x_turned, x_hi_made, x_split, noted = sem("x_turned"), sem("xt_hi_made"), sem("xt_split"), sem("noted")
        up_hi_made, up_split = sem("up_hi_made"), [sem(f"up_split{k}") for k in range(HK)]
        gated, silu_made, hidden_made = sem("gated"), sem("silu_made"), sem("hidden_made")
        hidden_hi_made, hidden_split = sem("hidden_hi_made"), sem("hidden_split")
        down_hi_made, down_split, zeroed, scales_made = sem("down_hi_made"), sem("down_split"), sem("zeroed"), sem("scales_made")
        addressed = sem("addressed")
        downed, y_made, y_sent = sem("downed"), sem("y_made"), sem("y_sent")
        send_begun, all_sent = sem("send_begun"), sem("all_sent")
        parts_in = [sem(f"parts_in{i}") for i in range(RING)]
        parts_used, dve_step = sem("parts_used"), sem("dve_step2")
        variance_made, deviation_made, normed, out_done = sem("variance_made"), sem("deviation_made"), sem("normed2"), sem("out_done")

        block = ctx.enter_context(nc.Block())
        row_blocks = dram["rows"].rearrange("(n p s) c -> n p s c", p=P, s=SUB)
        results = dram["results"].rearrange("(j i p) c -> i p j c", j=WAYS, p=P)
        out_tiles = out.rearrange("b (i p) c -> (b i) p c", p=P)

        def triples_of(eng):
            return eng.value_load(table[0:1, P:P + 1], min_val=T * TOPK // BLK // 3, max_val=(MAX_BLOCKS + 1) // 3)

        def block_of(i, u):
            return 3 * i + u, u % 3, i + u // 3 + 1

        def store(sp, g):
            sp.wait_ge(normed, GROUP_TILES * (g + 1))
            tiles = slice(g * GROUP_TILES, (g + 1) * GROUP_TILES)
            sp.dma_start(out_tiles[tiles].rearrange("i p c -> p i c"), resid[:, tiles, :]).then_inc(out_done, 16)

        @block.sync
        def _(sp):
            def load_rows(i, u):
                n, buf, _ = block_of(i, u)
                sp.wait_ge(x_turned, done(n, 3))
                sp.wait_ge(noted, done(n, 3))
                sp.dma_start(x_in[buf][:], row_blocks[bass.ds(n, 1)].rearrange("o p s c -> (o p) s c")).then_inc(rows_in[buf], 16)

            def load_weights(i, u):
                n, buf, _ = block_of(i, u)
                e = sp.value_load(table[0:1, bass.ds(n, 1)], min_val=0, max_val=E - 1)
                for k in range(HK):
                    sp.wait_ge(up_split[k], done(n, 3))
                sp.dma_start(up_raw[buf][:], dram["up"][bass.ds(e, 1)].rearrange("o p k c -> (o p) k c")).then_inc(up_in[buf], 16)
                sp.wait_ge(down_split, done(n, 3))
                sp.dma_start(down_raw[buf][:, 0, :], dram["down"][bass.ds(e, 1)].rearrange("o p c -> (o p) c")).then_inc(down_in[buf], 16)
                sp.dma_start(down_raw[buf][0:LOW_AT + TAIL, 1, :], dram["down_tail"][bass.ds(e, 1)].rearrange("o p c -> (o p) c")).then_inc(down_in[buf], 16)

            triples = triples_of(sp)
            load_rows(0, 0)
            load_rows(0, 1)
            sp.wait_ge(zeroed, 6)
            for u in range(3):
                load_weights(0, u)
            with sp.Fori(0, triples) as i:
                for u in range(1, 4):
                    load_rows(i, u + 1)
                    load_weights(i, u + 2)
            sp.wait_ge(all_sent, 1)
            for t in range(TILES):
                if t >= RING:
                    sp.wait_ge(parts_used, t - RING + 1)
                sp.dma_start(parts[t % RING][:], results[t]).then_inc(parts_in[t % RING], 16)
                if t >= 2 * GROUP_TILES and t % GROUP_TILES == 0:
                    store(sp, t // GROUP_TILES - 2)
            store(sp, TILES // GROUP_TILES - 2)
            store(sp, TILES // GROUP_TILES - 1)
            sp.wait_ge(out_done, 16 * (TILES // GROUP_TILES))

        @block.gpsimd
        def _(pool):
            pool.sem_inc(up_split[0], 3)
            pool.sem_inc(y_sent, 3)
            last_row = pool.to_reg(WAYS * T - 1)

            def split_up(i, u):
                n, buf, _ = block_of(i, u)
                pool.wait_ge(up_hi_made, done(n))
                pool.tensor_tensor(up_lo[buf][:, 0, :], up_raw[buf][:, 0, :], up_hi[buf][:, 0, :].bitcast(F32),
                                   ALU.subtract).then_inc(up_split[0], 1)

            def send(i, u):
                n, buf, _ = block_of(i, u)
                pool.wait_ge(y_made, done(n))
                pool.sem_inc(send_begun, 1)
                for s in range(SUB):
                    pool.indirect_dma_start(
                        out=dram["results"], out_offset=bass.IndirectOffsetOnAxis(ap=dest[buf][:, s:s + 1], axis=0),
                        in_=y_sb[buf][:, s, :], in_offset=None, bounds_check=last_row,
                        oob_is_err=False).then_inc(y_out[buf], 16)

            def landed(i, u):
                _, buf, count = block_of(i, u)
                pool.wait_ge(y_out[buf], 16 * SUB * count)
                pool.sem_inc(y_sent, 1)

            for buf in range(3):
                pool.memset(hidden[buf][:], 0.0).then_inc(zeroed, 1)
                pool.memset(down_raw[buf][:], 0.0).then_inc(zeroed, 1)
            triples = triples_of(pool)
            for u in range(5):
                split_up(0, u)
            send(0, 0)
            with pool.Fori(1, triples) as i:
                for u in range(-2, 1):
                    split_up(i, u + 4)
                    send(i, u)
                    landed(i, u - 1)
            split_up(triples, 2)
            for u in range(-2, 1):
                send(triples, u)
                landed(triples, u - 1)
            landed(triples, 0)
            pool.sem_inc(all_sent, 1)

        @block.scalar
        def _(act):
            act.sem_inc(x_hi_made, 3)
            act.sem_inc(up_hi_made, 3)
            act.sem_inc(silu_made, 3)
            act.sem_inc(down_hi_made, 3)
            act.sem_inc(hidden_hi_made, 3)
            act.sem_inc(y_made, 3)

            def x_upper(i, u):
                n, buf, _ = block_of(i, u)
                act.wait_ge(x_turned, done(n))
                act.wait_ge(gated, done(n, 3))
                nc.scalar.activation(x_hi[buf][:].rearrange("p k t -> p (k t)"), x_ps[:], ACT.Copy).then_inc(x_hi_made, 1)

            def up_upper(i, u):
                n, buf, count = block_of(i, u)
                act.wait_ge(up_in[buf], 16 * count)
                act.wait_ge(gated, done(n, 3))
                nc.scalar.activation(up_hi[buf][:], up_raw[buf][:], ACT.Copy).then_inc(up_hi_made, 1)

            def gate(i, u):
                n, buf, _ = block_of(i, u)
                act.wait_ge(gated, done(n))
                act.wait_ge(hidden_made, done(n, 3))
                nc.scalar.activation(silu[buf][:, 0, :], gate_up_ps[buf][:, 0:BLK], ACT.Silu)
                nc.scalar.activation(silu[buf][0:TAIL, 1, :], tail_ps[buf][0:TAIL, 0:BLK], ACT.Silu).then_inc(silu_made, 1)

            def down_upper(i, u):
                n, buf, count = block_of(i, u)
                act.wait_ge(down_in[buf], 32 * count)
                act.wait_ge(downed, done(n, 3))
                nc.scalar.activation(down_hi[buf][:], down_raw[buf][:], ACT.Copy).then_inc(down_hi_made, 1)

            def hidden_upper(i, u):
                n, buf, _ = block_of(i, u)
                act.wait_ge(hidden_made, done(n))
                act.wait_ge(downed, done(n, 3))
                nc.scalar.activation(hidden_hi[buf][:], hidden[buf][:], ACT.Copy).then_inc(hidden_hi_made, 1)

            def weigh(i, u):
                n, buf, _ = block_of(i, u)
                act.wait_ge(downed, done(n))
                act.wait_ge(addressed, done(n))
                for s in range(SUB):
                    ins = nc.scalar.activation(y_sb[buf][:, s, :], y_ps[:, s * H:(s + 1) * H], ACT.Copy,
                                               scale=weight[buf][:, s:s + 1])
                ins.then_inc(y_made, 1)

            triples = triples_of(act)
            up_upper(0, 0)
            x_upper(0, 0)
            x_upper(0, 1)
            up_upper(0, 1)
            down_upper(0, 0)
            up_upper(0, 2)
            down_upper(0, 1)
            gate(0, 0)
            with act.Fori(0, triples) as i:
                for u in range(1, 4):
                    hidden_upper(i, u - 1)
                    x_upper(i, u + 1)
                    up_upper(i, u + 2)
                    gate(i, u)
                    down_upper(i, u + 1)
                    weigh(i, u - 1)
            hidden_upper(triples, 0)
            weigh(triples, 0)
            for g in range(TILES // GROUP_TILES):
                act.wait_ge(variance_made, g + 1)
                tiles = slice(g * GROUP_TILES, (g + 1) * GROUP_TILES)
                nc.scalar.activation(deviation[:, tiles], deviation[:, tiles], ACT.Sqrt).then_inc(deviation_made, 1)
                act.wait_ge(scales_made, g + 1)
                for t in range(g * GROUP_TILES, (g + 1) * GROUP_TILES):
                    nc.scalar.activation(resid[:, t, :], resid[:, t, :], ACT.Identity, scale=inv_dev[:, t:t + 1],
                                         bias=shift[:, t:t + 1]).then_inc(normed, 1)

        @block.vector
        def _(dve):
            dve.sem_inc(x_split, 3)
            dve.sem_inc(noted, 3)
            dve.sem_inc(addressed, 3)
            dve.sem_inc(up_split[1], 3)
            dve.sem_inc(hidden_made, 3)
            dve.sem_inc(down_split, 3)
            dve.sem_inc(hidden_split, 3)

            def x_lower(i, u):
                n, buf, _ = block_of(i, u)
                dve.wait_ge(x_hi_made, done(n))
                dve.tensor_tensor(x_lo[buf][:].rearrange("p k t -> p (k t)"), x_ps[:],
                                  x_hi[buf][:].rearrange("p k t -> p (k t)").bitcast(F32), ALU.subtract).then_inc(x_split, 1)

            def note(i, u):
                n, buf, count = block_of(i, u)
                dve.wait_ge(rows_in[buf], 16 * count)
                dve.tensor_copy(goes_with[buf][:], x_in[buf][:, :, H:ROW]).then_inc(noted, 1)

            def address(i, u):
                n, buf, _ = block_of(i, u)
                dve.wait_ge(noted, done(n))
                dve.wait_ge(y_sent, done(n, 3))
                dve.tensor_copy(dest[buf][:], goes_with[buf][:, :, 0])
                dve.tensor_copy(weight[buf][:], goes_with[buf][:, :, 1]).then_inc(addressed, 1)

            def split_up(i, u):
                n, buf, _ = block_of(i, u)
                dve.wait_ge(up_hi_made, done(n))
                dve.tensor_tensor(up_lo[buf][:, 1, :], up_raw[buf][:, 1, :], up_hi[buf][:, 1, :].bitcast(F32),
                                  ALU.subtract).then_inc(up_split[1], 1)

            def hide(i, u):
                n, buf, _ = block_of(i, u)
                dve.wait_ge(silu_made, done(n))
                dve.wait_ge(hidden_split, done(n, 3))
                dve.tensor_tensor(hidden[buf][:, 0, :], silu[buf][:, 0, :], gate_up_ps[buf][:, BLK:2 * BLK], ALU.mult)
                dve.tensor_tensor(hidden[buf][0:TAIL, 1, :], silu[buf][0:TAIL, 1, :], tail_ps[buf][UP_AT:UP_AT + TAIL, 0:BLK],
                                  ALU.mult).then_inc(hidden_made, 1)

            def split_down(i, u):
                n, buf, _ = block_of(i, u)
                dve.wait_ge(down_hi_made, done(n))
                dve.tensor_tensor(down_lo[buf][:], down_raw[buf][:], down_hi[buf][:].bitcast(F32), ALU.subtract).then_inc(down_split, 1)

            def hidden_lower(i, u):
                n, buf, _ = block_of(i, u)
                dve.wait_ge(hidden_hi_made, done(n))
                dve.tensor_tensor(hidden_lo[buf][:], hidden[buf][:, 0, :], hidden_hi[buf][:, 0, :].bitcast(F32), ALU.subtract)
                dve.tensor_tensor(hidden_hi[buf][LOW_AT:LOW_AT + TAIL, 1, :], hidden[buf][0:TAIL, 1, :],
                                  hidden_hi[buf][0:TAIL, 1, :].bitcast(F32), ALU.subtract).then_inc(hidden_split, 1)

            triples = triples_of(dve)
            split_up(0, 0)
            x_lower(0, 0)
            note(0, 0)
            x_lower(0, 1)
            note(0, 1)
            split_up(0, 1)
            split_down(0, 0)
            split_up(0, 2)
            split_down(0, 1)
            dve.wait_ge(zeroed, 6)
            hide(0, 0)
            address(0, 0)
            with dve.Fori(0, triples) as i:
                for u in range(1, 4):
                    hidden_lower(i, u - 1)
                    x_lower(i, u + 1)
                    note(i, u + 1)
                    split_up(i, u + 2)
                    hide(i, u)
                    split_down(i, u + 1)
                    address(i, u)
            hidden_lower(triples, 0)

            steps = [0]

            def then(ins):
                steps[0] += 1
                ins.then_inc(dve_step, 1)
                dve.wait_ge(dve_step, steps[0])

            def scales(g):
                tiles = slice(g * GROUP_TILES, (g + 1) * GROUP_TILES)
                dve.wait_ge(deviation_made, g + 1)
                then(dve.reciprocal(inv_dev[:, tiles], deviation[:, tiles]))
                dve.scalar_tensor_tensor(out=shift[:, tiles], in0=moments[:, tiles, 0], scalar=-1.0, in1=inv_dev[:, tiles],
                                         op0=ALU.mult, op1=ALU.mult).then_inc(scales_made, 1)

            for t in range(TILES):
                dve.wait_ge(parts_in[t % RING], 16 * (t // RING + 1))
                dve.tensor_reduce(total[:, t % 2, :], parts[t % RING][:].rearrange("p j c -> p c j"), AX.X,
                                  ALU.add).then_inc(parts_used, 1)
                dve.wait_ge(parts_used, t + 1)
                then(dve.tensor_tensor(resid[:, t, :], resid[:, t, :], total[:, t % 2, :], ALU.add))
                then(dve.bn_stats(stats[:, t, :], resid[:, t, :]))
                then(dve.bn_aggr(moments[:, t, :], stats[:, t, :]))
                g = t // GROUP_TILES
                if t % GROUP_TILES == GROUP_TILES - 1:
                    tiles = slice(g * GROUP_TILES, (g + 1) * GROUP_TILES)
                    dve.tensor_scalar(deviation[:, tiles], moments[:, tiles, 1], EPS_LN, None, ALU.add).then_inc(variance_made, 1)
                if t % GROUP_TILES == 0 and g > 0:
                    scales(g - 1)
            scales(TILES // GROUP_TILES - 1)

        @block.tensor
        def _(pe):
            pe.sem_inc(x_turned, 3)
            pe.sem_inc(gated, 3)
            pe.sem_inc(downed, 3)

            def turn(i, u):
                n, buf, count = block_of(i, u)
                pe.wait_ge(rows_in[buf], 16 * count)
                pe.wait_ge(x_split, done(n, 1))
                for k in range(HK):
                    for s in range(SUB):
                        mm = nc.tensor.transpose(x_ps[:, k * BLK + s * P:k * BLK + (s + 1) * P],
                                                 x_in[buf][:, s, k * P:(k + 1) * P], ident[:])
                mm.then_inc(x_turned, 1)

            def gate_up(i, u):
                n, buf, _ = block_of(i, u)
                pe.wait_ge(x_split, done(n))
                for k in range(HK):
                    pe.wait_ge(up_split[k], done(n))
                pe.wait_ge(hidden_made, done(n, 3))
                for out, c, z in ((gate_up_ps[buf][:, 0:BLK], 0, P), (gate_up_ps[buf][:, BLK:2 * BLK], P, 2 * P),
                                  (tail_ps[buf][0:GCOLS - 2 * P, 0:BLK], 2 * P, GCOLS)):
                    for k in range(HK):
                        nc.tensor.matmul(out, up_hi[buf][:, k, c:z], x_hi[buf][:, k, :], start=(k == 0), stop=False)
                        nc.tensor.matmul(out, up_hi[buf][:, k, c:z], x_lo[buf][:, k, :], start=False, stop=False)
                        mm = nc.tensor.matmul(out, up_lo[buf][:, k, c:z], x_hi[buf][:, k, :], start=False, stop=(k == HK - 1))
                mm.then_inc(gated, 1)

            def down(i, u):
                n, buf, _ = block_of(i, u)
                pe.wait_ge(down_split, done(n))
                pe.wait_ge(hidden_split, done(n))
                pe.wait_ge(y_made, done(n, 1))
                for s in range(SUB):
                    tok, y = slice(s * P, (s + 1) * P), y_ps[:, s * H:(s + 1) * H]
                    nc.tensor.matmul(y, hidden_hi[buf][:, 0, tok], down_hi[buf][:, 0, :], start=True, stop=False)
                    nc.tensor.matmul(y, hidden_hi[buf][:, 0, tok], down_lo[buf][:, 0, :], start=False, stop=False)
                    nc.tensor.matmul(y, hidden_lo[buf][:, tok], down_hi[buf][:, 0, :], start=False, stop=False)
                    nc.tensor.matmul(y, hidden_hi[buf][0:LOW_AT + TAIL, 1, tok], down_hi[buf][0:LOW_AT + TAIL, 1, :],
                                     start=False, stop=False)
                    mm = nc.tensor.matmul(y, hidden_hi[buf][0:TAIL, 1, tok], down_lo[buf][0:TAIL, 1, :], start=False, stop=True)
                mm.then_inc(downed, 1)

            triples = triples_of(pe)
            turn(0, 0)
            turn(0, 1)
            gate_up(0, 0)
            with pe.Fori(0, triples) as i:
                for u in range(1, 4):
                    turn(i, u + 1)
                    gate_up(i, u)
                    down(i, u - 1)
            down(triples, 0)


def rope_tables():
    inv = (1.0 / 10000.0 ** (np.arange(0, HD, 2, dtype=np.float64) / HD)).astype(np.float32)
    angle = (np.arange(S, dtype=np.float32)[:, None] * inv[None, :]).astype(np.float64)
    angle = np.concatenate([angle, angle], axis=-1).T
    sin = np.sin(angle) * HD ** -0.25
    sin[HD // 2:] *= -1
    return (np.cos(angle) * HD ** -0.25).astype(np.float32), sin.astype(np.float32)


def build(nc, dram, out):
    with ExitStack() as ctx:
        resid = ctx.enter_context(nc.sbuf_tensor("resid", [P, TILES, H], F32))
        consts = {"ident": ctx.enter_context(nc.sbuf_tensor("ident", [P, P], F32)),
                  "table": ctx.enter_context(nc.sbuf_tensor("table", [1, P + 1], I32))}
        attention(nc, dram, resid, consts)
        routing(nc, dram, resid, consts)
        experts(nc, dram, resid, consts, out)


def kernel(**inputs):
    import concourse.bacc as bacc
    from concourse.bass_utils import run_bass_kernel_spmd

    def given(name):
        return np.asarray(inputs[f"L0_{name}"])

    x = given("attn_hidden_states").reshape(T, H)
    cos, sin = rope_tables()
    qkv = np.concatenate([given("attn_Wq").reshape(NKV, GROUP * HD, H), given("attn_Wk").reshape(NKV, HD, H),
                          given("attn_Wv").reshape(NKV, HD, H)], axis=1)
    shared_up = given("ffn_ws_gate_up").reshape(2, SHARED, FFN, H).transpose(1, 0, 2, 3).reshape(SHARED, 2 * FFN, H)
    up = np.concatenate([shared_up, given("ffn_w_gate_up")], axis=0)
    gap = np.zeros((E + SHARED, UP_AT - TAIL, H), up.dtype)
    up = np.concatenate([up[:, 0:P], up[:, FFN:FFN + P], up[:, P:FFN], gap, up[:, FFN + P:]], axis=1)
    up = up.reshape(E + SHARED, GCOLS, HK, P).transpose(0, 3, 2, 1)
    shared_down = given("ffn_ws_down").reshape(H, SHARED, FFN).transpose(2, 1, 0)
    down = given("ffn_w_down").transpose(0, 2, 1)
    arrays = {
        "x": x,
        "xT": x.reshape(B, 2, HALF, HK, P).transpose(0, 1, 4, 3, 2),
        "cos": cos, "sin": sin,
        "w": qkv.reshape(NKV, WCOLS, HK, P).transpose(0, 3, 2, 1),
        "wo": given("attn_Wo").reshape(H, NKV, GROUP, HD).transpose(1, 3, 2, 0),
        "gate": given("ffn_gate_w").reshape(E, HK, P).transpose(2, 1, 0),
        "shared_up": up[0:SHARED].transpose(1, 0, 2, 3), "up": up[SHARED:],
        "shared_down": shared_down[0:P], "shared_down_tail": shared_down[P:],
        "down": down[:, 0:P],
        "down_tail": np.concatenate([down[:, P:], np.zeros((E, LOW_AT - TAIL, H), down.dtype), down[:, P:]], axis=1),
    }
    arrays = {f"in_{k}": np.ascontiguousarray(v) for k, v in arrays.items()}
    nc = bacc.Bacc("TRN2", target_bir_lowering=False, num_devices=1)
    dram = {k[3:]: nc.dram_tensor(k, v.shape, F32, kind="ExternalInput").ap() for k, v in arrays.items()}
    dram["rows"] = nc.dram_tensor("rows_dram", (ROWS, ROW), F32, kind="Internal").ap()
    dram["results"] = nc.dram_tensor("results_dram", (WAYS * T, H), F32, kind="Internal").ap()
    dram["table"] = nc.dram_tensor("table_dram", (P + 1, 1), I32, kind="Internal").ap()
    dram["empty"] = dram["rows"].rearrange("(n p r) c -> n p r c", p=LIST_BLOCKS, r=EMPTY_ROWS)
    out = nc.dram_tensor("out", (B, S, H), F32, kind="ExternalOutput").ap()
    build(nc, dram, out)
    got = run_bass_kernel_spmd(nc, [arrays], core_ids=[0])
    return got.results[0]["out"]
```
